# Optimizing a Trainium2 kernel written in Bass

```python
import numpy as np
import jax
import jax.numpy as jnp

def _softmax(x, axis=-1):
    return jax.nn.softmax(x, axis=axis)

def _gelu(x):
    return jax.nn.gelu(x, approximate=True)

def _silu(x):
    return jax.nn.silu(x)

def _sigmoid(x):
    return jax.nn.sigmoid(x)

def _layernorm(x, axis=-1, eps=1e-05):
    m = jnp.mean(x, axis=axis, keepdims=True)
    v = jnp.var(x, axis=axis, keepdims=True)
    return (x - m) / jnp.sqrt(v + eps)

def _scatter_add(tgt, idx, src, axis=0):
    return tgt.at[idx].add(src)

def _segment_sum(src, seg, n):
    return jax.ops.segment_sum(src, seg, n)
kernel_name = 'mk_adaln_attn_ffn_d1_seqx_r8_210b6a'

def setup_inputs(seed: int=0):
    np.random.seed(seed)
    _w = jnp.asarray

    def _rec_inputs():
        import jax
        import jax.numpy as jnp
        _rk = jax.random.key(seed)
        x = -0.000125 + 0.9999 * jax.random.normal(jax.random.fold_in(_rk, 1), (128, 32, 512), jnp.float32)
        _lenS = 32 - jax.random.randint(jax.random.fold_in(_rk, 7), (128,), 0, max(1, 32 // 4) + 1, jnp.int32)
        _lenS2 = 32 - jax.random.randint(jax.random.fold_in(_rk, 8), (128,), 0, max(1, 32 // 4) + 1, jnp.int32)
        condB_codebook = -0.0625 + 0.715345 * jax.random.normal(jax.random.fold_in(_rk, 11), (128,), jnp.float32)
        itok_B_0_7 = jax.random.randint(jax.random.fold_in(_rk, 12), (128,), 0, 8, jnp.int32)
        return (x, condB_codebook, itok_B_0_7)
    x, condB_codebook, itok_B_0_7 = _rec_inputs()

    def _L0_cond_setup():
        import jax, jax.numpy as jnp
        import numpy as np
        GROUP = 128
        LORA_ALPHA = 32.0
        LORA_RANK = 64
        key = jax.random.key(seed)
        k1, k2, k3, k4 = jax.random.split(key, 4)
        O, I = (512, 512)
        x = jax.random.normal(k1, (4, 256, I), dtype=jnp.float32)
        weight = jax.random.normal(k2, (O, I), dtype=jnp.float32) * 0.02
        wg = weight.reshape(O, I // GROUP, GROUP)
        scale_log = jnp.log(jnp.clip(jnp.max(jnp.abs(wg), axis=2, keepdims=True), 1e-05))
        codebook = jnp.array([-1.0, -0.25, 0.0, 1.0], dtype=jnp.float32)
        lora_A = jax.random.normal(k3, (LORA_RANK, I), dtype=jnp.float32) * 0.02
        lora_B = jax.random.normal(k4, (O, LORA_RANK), dtype=jnp.float32) * 0.02
        return {'x': x, 'weight': weight, 'scale_log': scale_log, 'codebook': codebook, 'lora_A': lora_A, 'lora_B': lora_B}
    _L0_cond_all = _L0_cond_setup()
    _L0_cond_in = {k: v for k, v in _L0_cond_all.items() if k in ('weight', 'scale_log', 'lora_A', 'lora_B')}
    del _L0_cond_all

    def _L0_attn_setup():
        import jax, jax.numpy as jnp
        import numpy as np
        HIDDEN = 512
        NUM_HEADS = 32
        NUM_KV_HEADS = 8
        HEAD_DIM = HIDDEN // NUM_HEADS
        N_REP = NUM_HEADS // NUM_KV_HEADS
        B, S = (1, 256)
        ACT_BITS = 8
        QB = 2 ** (ACT_BITS - 1) - 1
        ROPE_BASE = 10000.0
        LN_EPS = 1e-05

        def _act_quant(x):
            scale = QB / jnp.clip(jnp.max(jnp.abs(x), axis=-1, keepdims=True), 1e-05, None)
            q = jnp.clip(jnp.round(x * scale), -QB - 1, QB) / scale
            return x + jax.lax.stop_gradient(q - x)

        def _weight_quant(w):
            scale = 1.0 / jnp.clip(jnp.mean(jnp.abs(w)), 1e-05, None)
            q = jnp.clip(jnp.round(w * scale), -1.0, 1.0) / scale
            return w + jax.lax.stop_gradient(q - w)

        def _bitlinear(x, w):
            return jnp.einsum('...i,oi->...o', _act_quant(x), _weight_quant(w))

        def _layernorm(x, g, b):
            mu = jnp.mean(x, axis=-1, keepdims=True)
            var = jnp.mean(jnp.square(x - mu), axis=-1, keepdims=True)
            return (x - mu) * jax.lax.rsqrt(var + LN_EPS) * g + b

        def _rope(x):
            s, d = (x.shape[2], x.shape[3])
            inv_freq = 1.0 / ROPE_BASE ** (jnp.arange(0, d, 2, dtype=jnp.float32) / d)
            freqs = jnp.arange(s, dtype=jnp.float32)[:, None] * inv_freq[None, :]
            emb = jnp.concatenate([freqs, freqs], axis=-1)
            cos, sin = (jnp.cos(emb), jnp.sin(emb))
            x1, x2 = jnp.split(x, 2, axis=-1)
            rot = jnp.concatenate([-x2, x1], axis=-1)
            return x * cos + rot * sin
        key = jax.random.key(seed)
        ks = jax.random.split(key, 5)
        hidden_states = jax.random.normal(ks[0], (B, S, HIDDEN), dtype=jnp.float32)
        std = 0.02
        Wq = jax.random.normal(ks[1], (HIDDEN, HIDDEN), dtype=jnp.float32) * std
        Wk = jax.random.normal(ks[2], (NUM_KV_HEADS * HEAD_DIM, HIDDEN), dtype=jnp.float32) * std
        Wv = jax.random.normal(ks[3], (NUM_KV_HEADS * HEAD_DIM, HIDDEN), dtype=jnp.float32) * std
        Wo = jax.random.normal(ks[4], (HIDDEN, HIDDEN), dtype=jnp.float32) * std
        ln_w = jnp.ones((HIDDEN,), dtype=jnp.float32)
        ln_b = jnp.zeros((HIDDEN,), dtype=jnp.float32)
        return {'hidden_states': hidden_states, 'ln_w': ln_w, 'ln_b': ln_b, 'Wq': Wq, 'Wk': Wk, 'Wv': Wv, 'Wo': Wo}
    _L0_attn_all = _L0_attn_setup()
    _L0_attn_in = {k: v for k, v in _L0_attn_all.items() if k in ('ln_w', 'ln_b', 'Wq', 'Wk', 'Wv', 'Wo')}
    del _L0_attn_all

    def _L0_cond2_setup():
        import jax, jax.numpy as jnp
        import numpy as np
        TOP_K = 2
        LANG_BIAS = 5.0
        SCALING = 32.0 / 16.0
        LANGUAGE_PAD_ID = -1
        key = jax.random.key(seed)
        ks = jax.random.split(key, 6)
        B, T, D, O, E, R = (4, 256, 512, 512, 8, 16)
        x = jax.random.normal(ks[0], (B, T, D), dtype=jnp.float32)
        language_ids = jax.random.randint(ks[1], (B,), 0, E).astype(jnp.int64)
        W = jax.random.normal(ks[2], (O, D), dtype=jnp.float32) * (1.0 / np.sqrt(D))
        Wr = jax.random.normal(ks[3], (E, D), dtype=jnp.float32) * (1.0 / np.sqrt(D))
        A = jax.random.normal(ks[4], (E, R, D), dtype=jnp.float32) * (1.0 / np.sqrt(D))
        Bm = jax.random.normal(ks[5], (O, R), dtype=jnp.float32) * 0.0
        Bm = jnp.broadcast_to(Bm, (E, O, R)) + jax.random.normal(ks[5], (E, O, R), dtype=jnp.float32) * 0.02
        return {'x': x, 'language_ids': language_ids, 'W': W, 'Wr': Wr, 'A': A, 'B': Bm}
    _L0_cond2_all = _L0_cond2_setup()
    _L0_cond2_in = {k: v for k, v in _L0_cond2_all.items() if k in ('W', 'Wr', 'A', 'B')}
    del _L0_cond2_all

    def _L0_ffn_setup():
        import jax, jax.numpy as jnp
        import numpy as np
        EPS = 1e-06
        QMAX = 127.0

        def _quant_act(x):
            s = jnp.max(jnp.abs(x), axis=-1, keepdims=True) / QMAX
            s = jnp.maximum(s, 1e-08)
            q = jnp.clip(jnp.round(x / s), -QMAX, QMAX)
            return (q, s)

        def _quant_w(W):
            ws = jnp.max(jnp.abs(W), axis=1, keepdims=True) / QMAX
            ws = jnp.maximum(ws, 1e-08)
            Wq = jnp.clip(jnp.round(W / ws), -QMAX, QMAX)
            return (Wq, ws)
        key = jax.random.key(seed)
        k1, k2, k3, k4, k5 = jax.random.split(key, 5)
        B, S, D, I = (4, 256, 512, 1376)
        return {'hidden_states': jax.random.normal(k1, (B, S, D), dtype=jnp.float32), 'rmsnorm_weight': jax.random.uniform(k2, (D,), dtype=jnp.float32), 'Wg': jax.random.normal(k3, (I, D), dtype=jnp.float32) * 0.02, 'Wu': jax.random.normal(k4, (I, D), dtype=jnp.float32) * 0.02, 'Wd': jax.random.normal(k5, (D, I), dtype=jnp.float32) * 0.02}
    _L0_ffn_all = _L0_ffn_setup()
    _L0_ffn_in = {k: v for k, v in _L0_ffn_all.items() if k in ('rmsnorm_weight', 'Wg', 'Wu', 'Wd')}
    del _L0_ffn_all
    return {'x': x, 'condB_codebook': condB_codebook, 'itok_B_0_7': itok_B_0_7, 'L0_cond_weight': _L0_cond_in['weight'], 'L0_cond_scale_log': _L0_cond_in['scale_log'], 'L0_cond_lora_A': _L0_cond_in['lora_A'], 'L0_cond_lora_B': _L0_cond_in['lora_B'], 'L0_attn_ln_w': _L0_attn_in['ln_w'], 'L0_attn_ln_b': _L0_attn_in['ln_b'], 'L0_attn_Wq': _L0_attn_in['Wq'], 'L0_attn_Wk': _L0_attn_in['Wk'], 'L0_attn_Wv': _L0_attn_in['Wv'], 'L0_attn_Wo': _L0_attn_in['Wo'], 'L0_cond2_W': _L0_cond2_in['W'], 'L0_cond2_Wr': _L0_cond2_in['Wr'], 'L0_cond2_A': _L0_cond2_in['A'], 'L0_cond2_B': _L0_cond2_in['B'], 'L0_ffn_rmsnorm_weight': _L0_ffn_in['rmsnorm_weight'], 'L0_ffn_Wg': _L0_ffn_in['Wg'], 'L0_ffn_Wu': _L0_ffn_in['Wu'], 'L0_ffn_Wd': _L0_ffn_in['Wd']}

def reference(x, condB_codebook, itok_B_0_7, L0_cond_weight, L0_cond_scale_log, L0_cond_lora_A, L0_cond_lora_B, L0_attn_ln_w, L0_attn_ln_b, L0_attn_Wq, L0_attn_Wk, L0_attn_Wv, L0_attn_Wo, L0_cond2_W, L0_cond2_Wr, L0_cond2_A, L0_cond2_B, L0_ffn_rmsnorm_weight, L0_ffn_Wg, L0_ffn_Wu, L0_ffn_Wd):
    import jax
    import jax.numpy as jnp

    def _L0_cond_ref(x, weight, scale_log, codebook, lora_A, lora_B):
        import jax, jax.numpy as jnp
        import numpy as np
        GROUP = 128
        LORA_ALPHA = 32.0
        LORA_RANK = 64
        O, I = weight.shape
        lora_delta = lora_B @ lora_A * (LORA_ALPHA / LORA_RANK)
        cb = codebook / jnp.clip(jnp.max(jnp.abs(codebook)), 1e-08)
        scale = jnp.exp(scale_log)
        wg = (weight + lora_delta).reshape(O, I // GROUP, GROUP)
        normalized = wg / scale
        thresholds = (cb[:-1] + cb[1:]) * 0.5
        idx = jnp.searchsorted(thresholds, normalized, side='left')
        quantized = cb[idx]
        w = jax.lax.stop_gradient(quantized - normalized) + normalized
        w_q = (w * scale).reshape(O, I)
        w_eff = w_q + lora_delta
        return x @ w_eff.T

    def _L0_attn_ref(hidden_states, ln_w, ln_b, Wq, Wk, Wv, Wo):
        import jax, jax.numpy as jnp
        import numpy as np
        HIDDEN = 512
        NUM_HEADS = 32
        NUM_KV_HEADS = 8
        HEAD_DIM = HIDDEN // NUM_HEADS
        N_REP = NUM_HEADS // NUM_KV_HEADS
        B, S = (1, 256)
        ACT_BITS = 8
        QB = 2 ** (ACT_BITS - 1) - 1
        ROPE_BASE = 10000.0
        LN_EPS = 1e-05

        def _act_quant(x):
            scale = QB / jnp.clip(jnp.max(jnp.abs(x), axis=-1, keepdims=True), 1e-05, None)
            q = jnp.clip(jnp.round(x * scale), -QB - 1, QB) / scale
            return x + jax.lax.stop_gradient(q - x)

        def _weight_quant(w):
            scale = 1.0 / jnp.clip(jnp.mean(jnp.abs(w)), 1e-05, None)
            q = jnp.clip(jnp.round(w * scale), -1.0, 1.0) / scale
            return w + jax.lax.stop_gradient(q - w)

        def _bitlinear(x, w):
            return jnp.einsum('...i,oi->...o', _act_quant(x), _weight_quant(w))

        def _layernorm(x, g, b):
            mu = jnp.mean(x, axis=-1, keepdims=True)
            var = jnp.mean(jnp.square(x - mu), axis=-1, keepdims=True)
            return (x - mu) * jax.lax.rsqrt(var + LN_EPS) * g + b

        def _rope(x):
            s, d = (x.shape[2], x.shape[3])
            inv_freq = 1.0 / ROPE_BASE ** (jnp.arange(0, d, 2, dtype=jnp.float32) / d)
            freqs = jnp.arange(s, dtype=jnp.float32)[:, None] * inv_freq[None, :]
            emb = jnp.concatenate([freqs, freqs], axis=-1)
            cos, sin = (jnp.cos(emb), jnp.sin(emb))
            x1, x2 = jnp.split(x, 2, axis=-1)
            rot = jnp.concatenate([-x2, x1], axis=-1)
            return x * cos + rot * sin
        b, s, _ = hidden_states.shape
        normed = _layernorm(hidden_states, ln_w, ln_b)
        q = _bitlinear(normed, Wq).reshape(b, s, NUM_HEADS, HEAD_DIM).transpose(0, 2, 1, 3)
        k = _bitlinear(normed, Wk).reshape(b, s, NUM_KV_HEADS, HEAD_DIM).transpose(0, 2, 1, 3)
        v = _bitlinear(normed, Wv).reshape(b, s, NUM_KV_HEADS, HEAD_DIM).transpose(0, 2, 1, 3)
        q = _rope(q)
        k = _rope(k)
        scale = 1.0 / np.sqrt(HEAD_DIM)
        qg = q.reshape(b, NUM_KV_HEADS, N_REP, s, HEAD_DIM)
        scores = jnp.einsum('bgrqd,bgkd->bgrqk', qg, k) * scale
        attn = jax.nn.softmax(scores, axis=-1)
        out = jnp.einsum('bgrqk,bgkd->bgrqd', attn, v)
        out = out.reshape(b, NUM_HEADS, s, HEAD_DIM).transpose(0, 2, 1, 3).reshape(b, s, HIDDEN)
        return _bitlinear(out, Wo)

    def _L0_cond2_ref(x, language_ids, W, Wr, A, B):
        import jax, jax.numpy as jnp
        import numpy as np
        TOP_K = 2
        LANG_BIAS = 5.0
        SCALING = 32.0 / 16.0
        LANGUAGE_PAD_ID = -1
        base = jnp.einsum('btd,od->bto', x, W)
        E = Wr.shape[0]
        logits = jnp.einsum('btd,ed->bte', x.astype(jnp.float32), Wr.astype(jnp.float32))
        expert_targets = language_ids
        valid = expert_targets >= 0
        tgt = jnp.where(valid, expert_targets, 0)
        bias = jax.nn.one_hot(tgt, E, dtype=logits.dtype) * LANG_BIAS
        bias = jnp.where(valid[:, None], bias, 0.0)
        logits = logits + bias[:, None, :]
        topw, topi = jax.lax.top_k(logits, TOP_K)
        weights = jax.nn.softmax(topw, axis=-1)
        gates = jnp.sum(jax.nn.one_hot(topi, E, dtype=weights.dtype) * weights[..., None], axis=-2)
        gates = gates.astype(x.dtype)
        h = jnp.einsum('btd,erd->bter', x, A)
        lora_out = jnp.einsum('bter,bte,eor->bto', h, gates, B)
        return base + SCALING * lora_out

    def _L0_ffn_ref(hidden_states, rmsnorm_weight, Wg, Wu, Wd):
        import jax, jax.numpy as jnp
        import numpy as np
        EPS = 1e-06
        QMAX = 127.0

        def _quant_act(x):
            s = jnp.max(jnp.abs(x), axis=-1, keepdims=True) / QMAX
            s = jnp.maximum(s, 1e-08)
            q = jnp.clip(jnp.round(x / s), -QMAX, QMAX)
            return (q, s)

        def _quant_w(W):
            ws = jnp.max(jnp.abs(W), axis=1, keepdims=True) / QMAX
            ws = jnp.maximum(ws, 1e-08)
            Wq = jnp.clip(jnp.round(W / ws), -QMAX, QMAX)
            return (Wq, ws)
        B, S, D = hidden_states.shape
        x = hidden_states.reshape(B * S, D)
        x = x * jax.lax.rsqrt(jnp.mean(x * x, axis=-1, keepdims=True) + EPS)
        x = x * rmsnorm_weight
        q, s = _quant_act(x)
        Wgq, wsg = _quant_w(Wg)
        Wuq, wsu = _quant_w(Wu)
        gate = jnp.einsum('td,id->ti', q, Wgq) * s * wsg.T
        up = jnp.einsum('td,id->ti', q, Wuq) * s * wsu.T
        h = jax.nn.silu(gate) * up
        q2, s2 = _quant_act(h)
        Wdq, wsd = _quant_w(Wd)
        out = jnp.einsum('ti,di->td', q2, Wdq) * s2 * wsd.T
        return out.reshape(B, S, D)
    x = x + _L0_attn_ref(_L0_cond_ref(x, L0_cond_weight, L0_cond_scale_log, condB_codebook, L0_cond_lora_A, L0_cond_lora_B), L0_attn_ln_w, L0_attn_ln_b, L0_attn_Wq, L0_attn_Wk, L0_attn_Wv, L0_attn_Wo)
    x = x + _L0_ffn_ref(_L0_cond2_ref(x, itok_B_0_7, L0_cond2_W, L0_cond2_Wr, L0_cond2_A, L0_cond2_B), L0_ffn_rmsnorm_weight, L0_ffn_Wg, L0_ffn_Wu, L0_ffn_Wd)
    return x

_drawn_inputs = setup_inputs


def setup_inputs(seed=0):
    import zlib

    import numpy as np

    out = dict(_drawn_inputs(seed))
    spreads = {'L0_attn_ln_w': (1.0, 0.6), 'L0_attn_ln_b': (0.0, 0.8)}
    factors = {'L0_cond_weight': 3.375,
     'L0_cond_scale_log': 8.0,
     'L0_cond_lora_A': 8.0,
     'L0_cond_lora_B': 8.0,
     'L0_attn_Wq': 8.0,
     'L0_attn_Wk': 8.0,
     'L0_attn_Wv': 2.937,
     'L0_attn_Wo': 2.99,
     'L0_cond2_Wr': 8.0,
     'L0_cond2_A': 8.0,
     'L0_cond2_B': 8.0,
     'L0_ffn_rmsnorm_weight': 3.342}
    for name, (base, spread) in spreads.items():
        noise = np.random.default_rng([zlib.crc32(name.encode()), seed]).standard_normal(out[name].shape)
        drawn = base * np.exp(spread * noise) if base else spread * noise
        out[name] = jnp.asarray(drawn.astype(out[name].dtype))
    for name, factor in factors.items():
        out[name] = (out[name] * factor).astype(out[name].dtype)
    return out
```

```python
import concourse.bass as bass
from concourse import mybir
from contextlib import ExitStack


def adaln_attn_ffn_kernel(nc, d):
    f32, bf16, i32, u8 = mybir.dt.float32, mybir.dt.bfloat16, mybir.dt.int32, mybir.dt.uint8
    ALU, ACT, AX = mybir.AluOpType, mybir.ActivationFunctionType, mybir.AxisListType

    NT, P, D = d["x_tok"].shape
    KC = D // P
    SLOTS = 2
    ITERS = NT // SLOTS
    SEQ, HD, G, R = 32, 16, 8, 4
    NB = P // SEQ
    H = G * R
    KV = G * HD
    QK = D + KV
    HALF = G // 2
    RANK = d["lora_A"].shape[0]
    E, LR = d["c2_wr"].shape[2], d["c2_b"].shape[0] // d["c2_wr"].shape[2]
    ER = E * LR
    W2N = D + ER + E
    F = d["ffn_wd"].shape[2]
    FC = -(-F // P)
    FL = F - (FC - 1) * P
    NCB = d["codebook"].shape[1]
    E_HI = 2.7182817459106445
    E_REST = 3.0367860004432146e-08
    MAGIC = 12582912.0
    FCH = [(n, min(n + 512, F)) for n in range(0, F, 512)]
    SEGS = 18
    LAG = 9

    ctx = ExitStack()
    with ctx:
        def sb(name, shape, dt=f32):
            return ctx.enter_context(nc.sbuf_tensor(name, shape, dt))

        def sem(name):
            return ctx.enter_context(nc.semaphore(name))

        def sems(name):
            return [sem(f"{name}{s}") for s in range(SLOTS)]

        consts = sb("consts", [P, d["consts"].shape[1]])
        at = [0]

        def const(n):
            at[0] += n
            return consts[:, at[0] - n:at[0]]

        ident, cos_t, sin_t = const(P), const(QK), const(QK)
        mask_k, mask_v = const(G), const(HALF)
        rep = const(NB * P)
        expert_no, ones = const(E), const(P)
        ident_bf = sb("ident_bf", [P, P], bf16)
        neg_half = sb("neg_half", [P, 1])
        euler = sb("euler", [P, KC * KC])

        w_eff = sb("w_eff", [P, KC, D])
        w_qkv = sb("w_qkv", [P, KC, D + 2 * KV], bf16)
        w_o = sb("w_o", [P, KC, D], bf16)
        w_c2 = sb("w_c2", [P, KC, W2N])
        b_c2 = sb("b_c2", [ER, D])
        w_gate = sb("w_gate", [P, KC, F], bf16)
        w_up = sb("w_up", [P, KC, F], bf16)
        w_down = sb("w_down", [P, FC, D], bf16)
        ln_g, ln_b, rms_g = sb("ln_g", [P, D]), sb("ln_b", [P, D]), sb("rms_g", [P, D])
        gate_s, up_s, down_s = sb("gate_s", [P, F]), sb("up_s", [P, F]), sb("down_s", [P, D])
        wmean = sb("wmean", [P, 4])
        wrecip = sb("wrecip", [P, 4])
        wabs = sb("wabs", [P, 4])
        lang = sb("lang", [P, NT, E])
        col_s = sb("col_s", [P, 2 * FC + KC])

        A_WORDS = 6656
        area = [sb(f"area{s}", [P, A_WORDS]) for s in range(SLOTS)]
        xT = [sb(f"xT{s}", [P, KC, P]) for s in range(SLOTS)]
        xt = [sb(f"xt{s}", [P, D]) for s in range(SLOTS)]
        work = [sb(f"work{s}", [P, D]) for s in range(SLOTS)]
        work_bf = [sb(f"work_bf{s}", [P, KC, P], bf16) for s in range(SLOTS)]
        x1 = [sb(f"x1_{s}", [P, D]) for s in range(SLOTS)]
        x1T = [sb(f"x1T{s}", [P, KC, P]) for s in range(SLOTS)]
        small = [sb(f"small{s}", [P, 192]) for s in range(SLOTS)]
        hid_bf = [sb(f"hid_bf{s}", [P, FC, P], bf16) for s in range(SLOTS)]

        def carve(t, sizes):
            out, o = [], 0
            for n in sizes:
                out.append(t[:, o:o + n])
                o += n
            return out

        att_sizes = [QK, QK, KV, D, NB * G * SEQ, NB * 2 * 64, H * SEQ]
        rope_c, rope_s, v_row, q_T, k_bd, v_bd, prob = zip(*[carve(a, att_sizes) for a in area])
        prob_T = [sb(f"prob_T{s}", [P, H * SEQ]) for s in range(SLOTS)]
        att_T = [v[:, 0:D] for v in rope_c]
        hid_g, hid_u, hid_t = zip(*[carve(a, [F, F, F]) for a in area])
        (st, mv, rstd, q_scale, deq, v_scale, smax, rsum, logit, top8, keep, ew, sq,
         steps) = zip(*[carve(t, [6, 2, 2, 4, 2, 1, H, H, E, 8, E, E, 4, 16]) for t in small])
        topi = [sb(f"topi{s}", [P, 8], mybir.dt.uint32) for s in range(SLOTS)]
        hg = [sb(f"hg{s}", [P, ER]) for s in range(SLOTS)]
        hg_T = [sb(f"hg_T{s}", [P, P]) for s in range(SLOTS)]

        bank = [[ctx.enter_context(nc.psum_tensor(f"bank{s}_{b}", [P, 512], f32)) for b in range(4)]
                for s in range(SLOTS)]

        ld = {n: sem("ld_" + n) for n in ("consts", "lora", "w", "sl", "qkv", "o", "c2", "vec")}
        ld_g, ld_u, ld_d = sem("ld_g"), sem("ld_u"), sem("ld_d")
        delta_mm, scale_exp, diag_ok = sem("delta_mm"), sem("scale_exp"), sem("diag_ok")
        bc_mm = sem("bc_mm")
        prep = sem("prep")
        near_col, near_row = sem("near_col"), sem("near_row")
        w_eff_ready = sem("w_eff_ready")
        abs_sum, abs_tot = sem("abs_sum"), sem("abs_tot")
        cast_ready = sem("cast_ready")
        gu_q, gu_T, gu_ev = sem("gu_q"), sem("gu_T"), sem("gu_ev")
        d_q, d_T, d_ev = sem("d_q"), sem("d_T"), sem("d_ev")
        row_step, row_mm, row_ev = sem("row_step"), sem("row_mm"), sem("row_ev")
        search = sem("search")
        c_ready = sem("c_ready")

        xT_in, x_in = sems("xT_in"), sems("x_in")
        y_mm, y_step, y_rstd = sems("y_mm"), sems("y_step"), sems("y_rstd")
        yq, yqT_mm, yqT = sems("yq"), sems("yqT_mm"), sems("yqT")
        qkv_mm, rope_step, qk, v_ev = sems("qkv_mm"), sems("rope_step"), sems("qk"), sems("v_ev")
        qkT_mm, v_mm = sems("qkT_mm"), sems("v_mm")
        qT, kbd, vbd = sems("qT"), sems("kbd"), sems("vbd")
        s_mm, s_step, s_exp, s_sum = sems("s_mm"), sems("s_step"), sems("s_exp"), sems("s_sum")
        pT_mm, pT, pv_mm, attT, att_mm = sems("pT_mm"), sems("pT"), sems("pv_mm"), sems("attT"), sems("att_mm")
        a_step, aq, aqT_mm, aqT = sems("a_step"), sems("aq"), sems("aqT_mm"), sems("aqT")
        o_mm, x1_ok, x1T_mm, x1T_ok = sems("o_mm"), sems("x1_ok"), sems("x1T_mm"), sems("x1T_ok")
        hl_mm, l_step, l_exp, hg_ok, hgT_mm, hgT = (
            sems("hl_mm"), sems("l_step"), sems("l_exp"), sems("hg_ok"), sems("hgT_mm"), sems("hgT"))
        c2_mm, z_sq, z_step, z_rstd, zq, zT_mm, zT = (
            sems("c2_mm"), sems("z_sq"), sems("z_step"), sems("z_rstd"), sems("zq"), sems("zT_mm"), sems("zT"))
        gu_mm, gu_sc, gu_tanh, gu_h, h_step, hq, hT_mm, hT = (
            sems("gu_mm"), sems("gu_sc"), sems("gu_tanh"), sems("gu_h"), sems("h_step"), sems("hq"),
            sems("hT_mm"), sems("hT"))
        d_mm, out_ok, out_st = sems("d_mm"), sems("out_ok"), sems("out_st")

        block = ctx.enter_context(nc.Block())

        def rounds(e, segment):
            for k in range(LAG):
                segment(0, k, 0)
            for k in range(SEGS):
                segment(0, (k + LAG) % SEGS, (k + LAG) // SEGS)
                segment(1, k, 0)
            with e.Fori(1, ITERS - 1) as i:
                for k in range(SEGS):
                    segment(0, (k + LAG) % SEGS, i + (k + LAG) // SEGS)
                    segment(1, k, i)
            for k in range(SEGS):
                if k + LAG < SEGS:
                    segment(0, k + LAG, ITERS - 1)
                segment(1, k, ITERS - 1)

        def cols(ap, n):
            return ap.unsqueeze(2).to_broadcast([ap.shape[0], ap.shape[1], n])

        def rows(ap, n):
            return ap.unsqueeze(1).to_broadcast([ap.shape[0], n, ap.shape[1]])

        a0, a1 = area
        delta, wg = a0[:, 0:KC * D], a0[:, KC * D:2 * KC * D]
        norm, quant = a1[:, 0:KC * D], a1[:, KC * D:2 * KC * D]
        diag = a0[:, 2 * KC * D:3 * KC * D]
        loraA = xT[0][0:RANK].rearrange("p a b -> p (a b)")
        loraB = xT[1][0:RANK].rearrange("p a b -> p (a b)")
        sl = sb("sl", [P, 2 * KC * KC])
        cbk = sb("cbk", [P, NCB])
        thr = sb("thr", [P, NCB + 1])
        cbx = sb("cbx", [P, 8])
        cell = sb("cell", [P, 8])
        flag = sb("flag", [1, 1], i32)
        picked = w_gate[:, 0, :]
        qkv_f = a1[:, 2 * KC * D:2 * KC * D + 512]
        idf = sb("idf", [P, NT])
        ids = sb("ids", [P, NT], i32)

        @block.sync
        def _(sp):
            sp.dma_start(loraA, d["lora_A"]).then_inc(ld["lora"], 16)
            sp.dma_start(loraB, d["lora_B"]).then_inc(ld["lora"], 16)
            sp.dma_start(consts[:, :], d["consts"]).then_inc(ld["consts"], 16)
            sp.dma_start(wg, d["w_cond"].rearrange("p g o -> p (g o)")).then_inc(ld["w"], 16)
            sp.dma_start(w_c2[:, :, 0:D], d["c2_w"]).then_inc(ld["c2"], 16)
            sp.dma_start(w_c2[:, :, D:D + ER], d["c2_a"]).then_inc(ld["c2"], 16)
            with nc.allow_non_contiguous_dma(reason="router columns, once"):
                sp.dma_start(w_c2[:, :, D + ER:W2N], d["c2_wr"]).then_inc(ld["c2"], 16)
            sp.dma_start(b_c2[:, :], d["c2_b"]).then_inc(ld["c2"], 16)

            sp.wait_ge(w_eff_ready, 1)
            sp.dma_start(a0[:, 0:KC * (D + 2 * KV)], d["w_qkv"].rearrange("p c o -> p (c o)")).then_inc(ld["qkv"], 16)
            sp.dma_start(a0[:, KC * (D + 2 * KV):KC * (2 * D + 2 * KV)],
                         d["w_o"].rearrange("p c o -> p (c o)")).then_inc(ld["o"], 16)
            def load_rows(c, n):
                sp.wait_ge(gu_q, 2 * c)
                sp.dma_start(a1[0:n, 0:D], d["ffn_wg"][bass.ds(c, 1), 0:n, :].rearrange("a p n -> (a p) n")).then_inc(ld_g, 16)
                sp.dma_start(a1[0:n, D:2 * D], d["ffn_wu"][bass.ds(c, 1), 0:n, :].rearrange("a p n -> (a p) n")).then_inc(ld_u, 16)

            load_rows(0, P)
            with sp.Fori(1, FC - 1) as c:
                load_rows(c, P)
            load_rows(FC - 1, FL)

            def load_down(c):
                sp.wait_ge(d_q, c)
                sp.dma_start(a1[:, 2 * D:2 * D + F],
                             d["ffn_wd"][bass.ds(c, 1), :, :].rearrange("a p n -> (a p) n")).then_inc(ld_d, 16)

            load_down(0)
            with sp.Fori(1, KC) as c:
                load_down(c)

            def segment(s, k, it):
                t = it * SLOTS + s
                if k == 0:
                    sp.wait_ge(y_mm[s], it)
                    sp.dma_start(xT[s][:, :, :], d["x_T"][bass.ds(t, 1)].rearrange("a p c n -> (a p) c n")).then_inc(xT_in[s], 16)
                    sp.wait_ge(x1_ok[s], it)
                    sp.dma_start(xt[s][:, :], d["x_tok"][bass.ds(t, 1)].rearrange("a p n -> (a p) n")).then_inc(x_in[s], 16)
                if k == SEGS - 1:
                    sp.wait_ge(out_ok[s], it + 1)
                    sp.dma_start(d["out"][bass.ds(t, 1)].rearrange("a p n -> (a p) n"), work[s][:, :]).then_inc(out_st[s], 16)

            sp.wait_ge(delta_mm, 1)
            rounds(sp, segment)
            for s in range(SLOTS):
                sp.wait_ge(out_st[s], 16 * ITERS)

        @block.gpsimd
        def _(pool):
            pool.dma_start(sl[:, 0:KC * KC], d["scale_log"]).then_inc(ld["sl"], 16)
            pool.dma_start(cbk[:, :], d["codebook"].to_broadcast([P, NCB])).then_inc(ld["vec"], 16)
            for v, n in ((ln_g, "ln_g"), (ln_b, "ln_b"), (rms_g, "rms_g")):
                pool.dma_start(v[:, :], d[n].to_broadcast([P, D])).then_inc(ld["vec"], 16)
            pool.dma_start(ids[:, :], d["ids"]).then_inc(ld["vec"], 16)
            nc.gpsimd.memset(neg_half[:, :], -0.5)
            nc.gpsimd.memset(euler[:, :], E_HI).then_inc(c_ready, 1)
            pool.wait_ge(c_ready, 1)
            pool.wait_ge(ld["sl"], 16)
            nc.gpsimd.tensor_tensor(sl[:, KC * KC:2 * KC * KC], euler[:, :], sl[:, 0:KC * KC], ALU.pow).then_inc(scale_exp, 1)

            def segment(s, k, it):
                if k == 0:
                    pool.wait_ge(y_step[s], 8 * it + 3)
                    nc.gpsimd.tensor_tensor(rstd[s][:, 0:1], steps[s][:, 0:1], neg_half[:, :], ALU.pow).then_inc(y_rstd[s], 1)
                if k == 13:
                    pool.wait_ge(z_step[s], 8 * it + 1)
                    nc.gpsimd.tensor_tensor(rstd[s][:, 1:2], steps[s][:, 8:9], neg_half[:, :], ALU.pow).then_inc(z_rstd[s], 1)
                if k == 17:
                    pool.wait_ge(h_step[s], 7 * it + 7)
                    nc.gpsimd.tensor_tensor(work[s][:, :], work[s][:, :], x1[s][:, :], ALU.add).then_inc(out_ok[s], 1)

            rounds(pool, segment)

        @block.scalar
        def _(act):
            A = nc.scalar.activation
            act.wait_ge(ld["qkv"], 16)
            wq3 = a0[:, 0:KC * (D + 2 * KV)].rearrange("p (c o) -> p c o", c=KC)
            spare = w_up.rearrange("p c o -> p (c o)").bitcast(f32)[:, 0:KC * D]
            junk = spare[:, 0:KC * KV].rearrange("p (c o) -> p c o", c=KC)
            A(spare.rearrange("p (c o) -> p c o", c=KC), wq3[:, :, 0:D], ACT.Abs, accum_out=wabs[:, 0:1]).then_inc(abs_sum, 1)
            act.wait_ge(abs_sum, 1)
            A(junk, wq3[:, :, D:D + KV], ACT.Abs, accum_out=wabs[:, 1:2]).then_inc(abs_sum, 1)
            act.wait_ge(abs_sum, 2)
            A(junk, wq3[:, :, D + KV:D + 2 * KV], ACT.Abs, accum_out=wabs[:, 2:3]).then_inc(abs_sum, 1)
            act.wait_ge(ld["o"], 16)
            act.wait_ge(abs_sum, 3)
            A(spare, a0[:, KC * (D + 2 * KV):KC * (2 * D + 2 * KV)], ACT.Abs, accum_out=wabs[:, 3:4]).then_inc(abs_sum, 1)

            def out_rows(c, n):
                for j, w in enumerate((w_gate, w_up)):
                    act.wait_ge(gu_T, 2 * c + j + 1)
                    src = bank[0][j][:, 0:256].bitcast(bf16).rearrange("p (k n) -> p k n", k=KC)[:, :, 0:n]
                    A(w[:, :, bass.ds(c * P, n)], src, ACT.Copy).then_inc(gu_ev, 1)

            out_rows(0, P)
            with act.Fori(1, FC - 1) as c:
                out_rows(c, P)
            out_rows(FC - 1, FL)
            with act.Fori(0, KC) as c:
                act.wait_ge(d_T, c + 1)
                for b in range(3):
                    m = min(4, FC - 4 * b)
                    full = m - 1 if 4 * b + m == FC else m
                    src = bank[1][b][:, 0:256].bitcast(bf16).rearrange("p (k n) -> p k n", k=4)
                    A(w_down[:, 4 * b:4 * b + full, bass.ds(c * P, P)], src[:, 0:full, :], ACT.Copy)
                    if full < m:
                        A(w_down[0:FL, FC - 1, bass.ds(c * P, P)], src[0:FL, full, :], ACT.Copy).then_inc(d_ev, 1)

            def segment(s, k, it):
                B, w = bank[s], work[s]
                wb = work_bf[s].rearrange("p c n -> p (c n)")
                if k == 0:
                    act.wait_ge(y_step[s], 8 * it + 8)
                    A(w[:, :], w[:, :], ACT.Copy, scale=q_scale[s][:, 0:1], bias=MAGIC).then_inc(yq[s], 1)
                if k == 1:
                    act.wait_ge(yqT_mm[s], it + 1)
                    A(wb, B[1][:, :], ACT.Copy, bias=-MAGIC).then_inc(yqT[s], 1)
                if k == 2:
                    act.wait_ge(rope_step[s], 2 * it + 2)
                    A(v_row[s], B[3][:, KV:2 * KV], ACT.Copy, scale=v_scale[s]).then_inc(v_ev[s], 1)
                if k == 3:
                    act.wait_ge(qkT_mm[s], 2 * it + 1)
                    A(q_T[s], B[0][:, :], ACT.Copy).then_inc(qT[s], 1)
                if k == 4:
                    for j in range(2):
                        act.wait_ge(s_step[s], 4 * it + 2 * j + 2)
                        p = prob[s][:, 512 * j:512 * (j + 1)]
                        A(p, p, ACT.Exp, scale=HD ** -0.5).then_inc(s_exp[s], 1)
                if k == 5:
                    for j in range(2):
                        act.wait_ge(pT_mm[s], 2 * it + j + 1)
                        A(prob_T[s][:, 512 * j:512 * (j + 1)], B[1 + j][:, :], ACT.Copy).then_inc(pT[s], 1)
                if k == 6:
                    act.wait_ge(pv_mm[s], it + 1)
                    A(att_T[s].rearrange("p (r b q) -> p b r q", r=R, b=NB),
                      B[3].rearrange("p (b r q) -> p b r q", b=NB, r=R), ACT.Copy).then_inc(attT[s], 1)
                if k == 7:
                    act.wait_ge(a_step[s], 5 * it + 5)
                    A(w[:, :], w[:, :], ACT.Copy, scale=q_scale[s][:, 1:2], bias=MAGIC).then_inc(aq[s], 1)
                if k == 8:
                    act.wait_ge(aqT_mm[s], it + 1)
                    A(wb, B[1][:, :], ACT.Copy, bias=-MAGIC).then_inc(aqT[s], 1)
                if k == 10:
                    act.wait_ge(x1T_mm[s], it + 1)
                    A(x1T[s].rearrange("p c n -> p (c n)"), B[3][:, :], ACT.Copy).then_inc(x1T_ok[s], 1)
                if k == 11:
                    act.wait_ge(l_step[s], 10 * it + 3)
                    A(ew[s], logit[s], ACT.Exp, bias=steps[s][:, 4:5]).then_inc(l_exp[s], 1)
                if k == 12:
                    act.wait_ge(hgT_mm[s], it + 1)
                    A(hg_T[s][:, :], B[2][:, 0:P], ACT.Copy).then_inc(hgT[s], 1)
                if k == 13:
                    act.wait_ge(c2_mm[s], it + 1)
                    A(prob_T[s][:, 0:D], B[0][:, :], ACT.Square, accum_out=sq[s][:, 0:1]).then_inc(z_sq[s], 1)
                    act.wait_ge(z_step[s], 8 * it + 8)
                    A(w[:, :], w[:, :], ACT.Copy, scale=q_scale[s][:, 2:3], bias=MAGIC).then_inc(zq[s], 1)
                if k == 14:
                    act.wait_ge(zT_mm[s], it + 1)
                    A(wb, B[3][:, :], ACT.Copy, bias=-MAGIC).then_inc(zT[s], 1)
                if k == 15:
                    for n, (lo, hi) in enumerate(FCH):
                        act.wait_ge(gu_sc[s], 6 * it + 2 * n + 1)
                        A(hid_t[s][:, lo:hi], hid_g[s][:, lo:hi], ACT.Tanh, scale=deq[s][:, 1:2]).then_inc(gu_tanh[s], 1)
                    act.wait_ge(h_step[s], 7 * it + 6)
                    A(hid_g[s], hid_u[s], ACT.Copy, scale=q_scale[s][:, 3:4], bias=MAGIC).then_inc(hq[s], 1)
                if k == 16:
                    for b in range(3):
                        m = min(4, FC - 4 * b)
                        full = m - 1 if 4 * b + m == FC else m
                        act.wait_ge(hT_mm[s], 3 * it + b + 1)
                        src = B[b].rearrange("p (k n) -> p k n", k=4)
                        ev = A(hid_bf[s][:, 4 * b:4 * b + full, :], src[:, 0:full, :], ACT.Copy, bias=-MAGIC)
                        if full < m:
                            ev = A(hid_bf[s][0:FL, FC - 1, :], src[0:FL, full, :], ACT.Copy, bias=-MAGIC)
                        ev.then_inc(hT[s], 1)

            rounds(act, segment)

        @block.vector
        def _(dve):
            V = nc.vector
            n_prep = [0]

            def step(ins):
                n_prep[0] += 1
                ins.then_inc(prep, 1)
                dve.wait_ge(prep, n_prep[0])

            dve.wait_ge(ld["consts"], 16)
            step(V.tensor_copy(ident_bf[:, :], ident))
            dve.wait_ge(ld["vec"], 80)
            step(V.tensor_copy(idf[:, :], ids[:, :]))
            step(V.tensor_tensor(lang[:, :, :], cols(idf[:, :], E), rows(expert_no, NT), ALU.is_equal))
            step(V.tensor_scalar(lang[:, :, :], lang[:, :, :], 5.0, None, ALU.mult))
            dve.wait_ge(scale_exp, 1)
            step(V.tensor_scalar(sl[:, 0:KC * KC], sl[:, 0:KC * KC], E_REST, 1.0, ALU.mult, ALU.add))
            step(V.tensor_tensor(sl[:, 0:KC * KC], sl[:, 0:KC * KC], sl[:, KC * KC:2 * KC * KC], ALU.mult))
            step(V.reciprocal(sl[:, KC * KC:2 * KC * KC], sl[:, 0:KC * KC]))
            diag3 = diag.rearrange("p (j n) -> p j n", n=P)
            V.tensor_tensor(diag3, rows(ident, KC * KC), cols(sl[:, KC * KC:2 * KC * KC], P), ALU.mult).then_inc(diag_ok, 1)
            step(V.tensor_reduce(cbx[:, 0:1], cbk[:, :], AX.X, ALU.max, apply_absolute_value=True))
            step(V.tensor_scalar(cbx[:, 1:2], cbx[:, 0:1], 1e-8, None, ALU.max))
            step(V.reciprocal(cbx[:, 2:3], cbx[:, 1:2]))
            step(V.tensor_scalar(cbk[:, :], cbk[:, :], cbx[:, 2:3], None, ALU.mult))
            dve.wait_ge(delta_mm, 1)
            for c in range(KC):
                last = V.tensor_scalar(delta[:, c * D:(c + 1) * D], bank[0][c][:, :], 0.5, None, ALU.mult)
            step(last)
            dve.wait_ge(ld["w"], 16)
            step(V.tensor_tensor(wg, wg, delta, ALU.add))
            dve.wait_ge(bc_mm, 1)
            for c in range(KC):
                last = V.tensor_tensor(norm[:, c * D:(c + 1) * D], wg[:, c * D:(c + 1) * D], bank[1][c][:, :], ALU.mult)
            step(last)
            V.tensor_tensor(diag3, rows(ident, KC * KC), cols(sl[:, 0:KC * KC], P), ALU.mult).then_inc(diag_ok, 1)
            step(V.tensor_reduce(cell[:, 0:1], norm, AX.X, ALU.min, apply_absolute_value=True))
            step(V.tensor_scalar(quant, norm, 0.0, cbk[:, NCB - 1:NCB], ALU.is_gt, ALU.mult))
            step(V.tensor_scalar(wg, norm, 0.0, cbk[:, 0:1], ALU.is_le, ALU.mult))
            step(V.tensor_tensor(quant, quant, wg, ALU.add))
            nc.vector.tensor_copy(cell[:, 1:2], cell[:, 0:1]).then_inc(near_col, 1)
            dve.wait_ge(near_row, 1)
            step(V.tensor_reduce(cell[0:1, 2:3], bank[0][0][0:1, 0:P], AX.X, ALU.min))
            step(V.tensor_scalar(flag[:, :], cell[0:1, 2:3], 1.001, None, ALU.is_le))
            near = dve.value_load(flag[0:1, 0:1], min_val=0, max_val=1)
            with dve.If(near == 1):
                m = [0]

                def found(ins):
                    m[0] += 1
                    ins.then_inc(search, 1)
                    dve.wait_ge(search, m[0])

                found(V.memset(thr[:, :], 3e38))
                found(V.memset(thr[:, 0:1], -3e38))
                found(V.tensor_tensor(thr[:, 1:NCB], cbk[:, 0:NCB - 1], cbk[:, 1:NCB], ALU.add))
                found(V.tensor_scalar(thr[:, 1:NCB], thr[:, 1:NCB], 0.5, None, ALU.mult))
                h = NCB // 2
                while h:
                    node = thr[:, h:NCB:2 * h]
                    found(V.tensor_tensor(node, node, thr[:, 0:NCB:2 * h], ALU.max))
                    found(V.tensor_tensor(node, node, thr[:, 2 * h:NCB + 1:2 * h], ALU.min))
                    h //= 2
                found(V.tensor_copy(quant, cbk[:, 0:1].to_broadcast([P, KC * D])))
                base, per = m[0], 4
                mask = picked.bitcast(u8)[:, 0:KC * D]
                with dve.Fori(0, NCB - 1) as j:
                    V.tensor_copy(cbx[:, 4:5], thr[:, bass.ds(j + 1, 1)]).then_inc(search, 1)
                    V.tensor_copy(cbx[:, 5:6], cbk[:, bass.ds(j + 1, 1)]).then_inc(search, 1)
                    dve.wait_ge(search, j * per + (base + 2))
                    V.tensor_scalar(mask, norm, cbx[:, 4:5], None, ALU.is_gt).then_inc(search, 1)
                    dve.wait_ge(search, j * per + (base + 3))
                    V.memset(cell[:, 3:4], 0.0)
                    V.copy_predicated(quant, mask, cbx[:, 5:6].to_broadcast([P, KC * D])).then_inc(search, 1)
                    dve.wait_ge(search, j * per + (base + 4))
            step(V.tensor_tensor(quant, quant, norm, ALU.subtract))
            step(V.tensor_tensor(quant, quant, norm, ALU.add))
            dve.wait_ge(bc_mm, 2)
            for c in range(KC):
                last = V.tensor_tensor(quant[:, c * D:(c + 1) * D], quant[:, c * D:(c + 1) * D], bank[1][c][:, :], ALU.mult)
            step(last)
            V.tensor_tensor(w_eff.rearrange("p c o -> p (c o)"), quant, delta, ALU.add).then_inc(w_eff_ready, 1)

            dve.wait_ge(abs_tot, 1)
            for j, n in enumerate((D * D, D * KV, D * KV, D * D)):
                last = V.tensor_scalar(wmean[:, j:j + 1], bank[0][3][:, j:j + 1], 1.0 / n, 1e-5, ALU.mult, ALU.max)
            step(last)
            step(V.reciprocal(wrecip[:, :], wmean[:, :]))
            qkv_src = a0[:, 0:KC * (D + 2 * KV)].rearrange("p (c o) -> p c o", c=KC)
            o_src = a0[:, KC * (D + 2 * KV):KC * (2 * D + 2 * KV)].rearrange("p (c o) -> p c o", c=KC)
            dve.wait_ge(abs_sum, 4)
            parts = ((qkv_src[:, :, 0:D], w_qkv[:, :, 0:D], 0), (qkv_src[:, :, D:D + KV], w_qkv[:, :, D:D + KV], 1),
                     (qkv_src[:, :, D + KV:D + 2 * KV], w_qkv[:, :, D + KV:D + 2 * KV], 2), (o_src, w_o[:, :, :], 3))
            for src, _, j in parts:
                last = V.tensor_scalar(src, src, wrecip[:, j:j + 1], MAGIC, ALU.mult, ALU.add)
            step(last)
            for src, _, j in parts:
                last = V.tensor_scalar(src, src, MAGIC + 1.0, MAGIC - 1.0, ALU.min, ALU.max)
            step(last)
            for src, dst, j in parts:
                last = V.tensor_scalar(dst, src, -MAGIC, None, ALU.add)
            last.then_inc(cast_ready, 1)
            for tab in (cos_t, sin_t):
                V.tensor_scalar(tab[:, 0:D], tab[:, 0:D], wmean[:, 0:1], None, ALU.mult)
                last = V.tensor_scalar(tab[:, D:QK], tab[:, D:QK], wmean[:, 1:2], None, ALU.mult)
            step(last)
            g_bf = a1[:, 4096:4096 + D // 2].bitcast(bf16)
            u_bf = a1[:, 4608:4608 + D // 2].bitcast(bf16)
            d_bf = a1[:, 5120:5120 + F // 2].bitcast(bf16)

            def quant_rows(src, dst, scol, rcol, before, rounded):
                dve.wait_ge(row_step, before)
                V.tensor_reduce(scol, src, AX.X, ALU.max, apply_absolute_value=True).then_inc(row_step, 1)
                dve.wait_ge(row_step, before + 1)
                V.tensor_scalar(scol, scol, 1.0 / 127.0, 1e-8, ALU.mult, ALU.max).then_inc(row_step, 1)
                dve.wait_ge(row_step, before + 2)
                V.reciprocal(rcol, scol).then_inc(row_step, 1)
                dve.wait_ge(row_step, before + 3)
                V.tensor_scalar(src, src, rcol, MAGIC, ALU.mult, ALU.add).then_inc(row_step, 1)
                dve.wait_ge(row_step, before + 4)
                V.tensor_scalar(dst, src, -MAGIC, None, ALU.add).then_inc(rounded, 1)

            def quant_gu(c, n):
                for j, (buf, ldsem) in enumerate(((g_bf, ld_g), (u_bf, ld_u))):
                    dve.wait_ge(ldsem, 16 * c + 16)
                    dve.wait_ge(gu_T, 2 * c)
                    scol = cell[0:n, 4 + j:5 + j]
                    quant_rows(a1[0:n, j * D:(j + 1) * D], buf[0:n, :], scol, cell[0:n, 6 + j:7 + j],
                               10 * c + 5 * j, gu_q)
                    V.tensor_copy(col_s[0:n, bass.ds(2 * c + j, 1)], scol).then_inc(row_step, 1)

            step(V.memset(col_s[:, :], 0.0))
            quant_gu(0, P)
            with dve.Fori(1, FC - 1) as c:
                quant_gu(c, P)
            quant_gu(FC - 1, FL)
            base = 10 * FC

            def quant_down(c):
                dve.wait_ge(ld_d, 16 * c + 16)
                dve.wait_ge(d_T, c)
                quant_rows(a1[:, 2 * D:2 * D + F], d_bf, cell[:, 4:5], cell[:, 6:7], 5 * c + base, d_q)
                V.tensor_copy(col_s[:, bass.ds(2 * FC + c, 1)], cell[:, 4:5]).then_inc(row_step, 1)

            quant_down(0)
            with dve.Fori(1, KC) as c:
                quant_down(c)
            dve.wait_ge(row_step, 10 * FC + 5 * KC)
            NCH = 2 * FC + KC
            dg = a0[:, 0:NCH * P].rearrange("p (j n) -> p j n", n=P)
            V.tensor_tensor(dg, rows(ident, NCH), cols(col_s[:, 0:NCH], P), ALU.mult).then_inc(diag_ok, 1)
            for b in range(-(-NCH // 4)):
                dve.wait_ge(row_mm, b + 1)
                for j in range(4 * b, min(4 * b + 4, NCH)):
                    src = bank[b // 4 % 2][b % 4][:, (j % 4) * P:(j % 4 + 1) * P]
                    if j < 2 * FC:
                        c = j // 2
                        n = P if c < FC - 1 else FL
                        last = V.tensor_copy((gate_s, up_s)[j % 2][:, c * P:c * P + n], src[:, 0:n])
                    else:
                        c = j - 2 * FC
                        last = V.tensor_copy(down_s[:, c * P:(c + 1) * P], src)
                last.then_inc(row_ev, 1)
            dve.wait_ge(row_ev, -(-NCH // 4))

            def segment(s, k, it):
                B, w, sm = bank[s], work[s], steps[s]
                if k == 0:
                    y8 = 8 * it
                    dve.wait_ge(y_mm[s], it + 1)
                    V.bn_stats(st[s], B[0][:, :]).then_inc(y_step[s], 1)
                    dve.wait_ge(y_step[s], y8 + 1)
                    V.memset(sm[:, 15:16], 0.0)
                    V.bn_aggr(mv[s], st[s]).then_inc(y_step[s], 1)
                    dve.wait_ge(y_step[s], y8 + 2)
                    V.tensor_scalar(sm[:, 0:1], mv[s][:, 1:2], 1e-5, None, ALU.add).then_inc(y_step[s], 1)
                    dve.wait_ge(out_st[s], 16 * it)
                    V.scalar_tensor_tensor(w[:, :], B[0][:, :], mv[s][:, 0:1], ln_g[:, :], ALU.subtract, ALU.mult).then_inc(y_step[s], 1)
                    dve.wait_ge(y_rstd[s], it + 1)
                    dve.wait_ge(y_step[s], y8 + 4)
                    V.scalar_tensor_tensor(w[:, :], w[:, :], rstd[s][:, 0:1], ln_b[:, :], ALU.mult, ALU.add).then_inc(y_step[s], 1)
                    dve.wait_ge(y_step[s], y8 + 5)
                    V.tensor_reduce(sm[:, 1:2], w[:, :], AX.X, ALU.max, apply_absolute_value=True).then_inc(y_step[s], 1)
                    dve.wait_ge(y_step[s], y8 + 6)
                    V.tensor_scalar(deq[s][:, 0:1], sm[:, 1:2], 1e-5, 1.0 / 127.0, ALU.max, ALU.mult).then_inc(y_step[s], 1)
                    dve.wait_ge(y_step[s], y8 + 7)
                    V.reciprocal(q_scale[s][:, 0:1], deq[s][:, 0:1]).then_inc(y_step[s], 1)
                if k == 2:
                    r4 = 2 * it
                    V.tensor_scalar(v_scale[s], deq[s][:, 0:1], wmean[:, 2:3], None, ALU.mult).then_inc(rope_step[s], 1)
                    dve.wait_ge(qkv_mm[s], it + 1)
                    sc = deq[s][:, 0:1]
                    for o, n, src in ((0, D, B[2][:, :]), (D, KV, B[3][:, 0:KV])):
                        V.scalar_tensor_tensor(rope_c[s][:, o:o + n], src, sc, cos_t[:, o:o + n], ALU.mult, ALU.mult)
                        x3 = src.rearrange("p (h j) -> p h j", j=HD)
                        s3 = sin_t[:, o:o + n].rearrange("p (h j) -> p h j", j=HD)
                        o3 = rope_s[s][:, o:o + n].rearrange("p (h j) -> p h j", j=HD)
                        hh = HD // 2
                        V.scalar_tensor_tensor(o3[:, :, 0:hh], x3[:, :, hh:HD], sc, s3[:, :, 0:hh], ALU.mult, ALU.mult)
                        last = V.scalar_tensor_tensor(o3[:, :, hh:HD], x3[:, :, 0:hh], sc, s3[:, :, hh:HD], ALU.mult, ALU.mult)
                    last.then_inc(rope_step[s], 1)
                    dve.wait_ge(rope_step[s], r4 + 2)
                    V.tensor_tensor(rope_c[s], rope_c[s], rope_s[s], ALU.add).then_inc(qk[s], 1)
                if k == 3:
                    dve.wait_ge(qkT_mm[s], 2 * it + 2)
                    kT = B[1][:, 0:P].rearrange("p (b q) -> p b q", b=NB)
                    kb = k_bd[s].rearrange("p (b g q) -> p b g q", b=NB, g=G)
                    V.tensor_tensor(kb, kT.unsqueeze(2).to_broadcast([P, NB, G, SEQ]),
                                    mask_k.unsqueeze(1).unsqueeze(3).to_broadcast([P, NB, G, SEQ]), ALU.mult).then_inc(kbd[s], 1)
                    dve.wait_ge(v_mm[s], it + 1)
                    vr = B[2].rearrange("p (e g j) -> p e g j", e=NB * 2, g=HALF)
                    vb = v_bd[s].rearrange("p (e g j) -> p e g j", e=NB * 2, g=HALF)
                    mk = mask_v.unsqueeze(1).unsqueeze(3).to_broadcast([P, NB * 2, HALF, HD])
                    V.tensor_tensor(vb, vr, mk, ALU.mult).then_inc(vbd[s], 1)
                if k == 4:
                    for j in range(2):
                        dve.wait_ge(s_mm[s], 2 * it + j + 1)
                        sc = B[(3, 0)[j]].rearrange("p (h q) -> p h q", q=SEQ)
                        m = smax[s][:, 16 * j:16 * (j + 1)]
                        V.tensor_reduce(m, sc, AX.X, ALU.max).then_inc(s_step[s], 1)
                        dve.wait_ge(s_step[s], 4 * it + 2 * j + 1)
                        p = prob[s][:, 512 * j:512 * (j + 1)].rearrange("p (h q) -> p h q", q=SEQ)
                        V.tensor_tensor(p, sc, cols(m, SEQ), ALU.subtract).then_inc(s_step[s], 1)
                    dve.wait_ge(s_exp[s], 2 * it + 2)
                    V.tensor_reduce(rsum[s], prob[s].rearrange("p (h q) -> p h q", q=SEQ), AX.X, ALU.add).then_inc(s_sum[s], 1)
                    dve.wait_ge(s_sum[s], 2 * it + 1)
                    V.reciprocal(rsum[s], rsum[s]).then_inc(s_sum[s], 1)
                if k == 7:
                    dve.wait_ge(att_mm[s], it + 1)
                    dve.wait_ge(s_sum[s], 2 * it + 2)
                    w3 = w.rearrange("p (h j) -> p h j", j=HD)
                    V.tensor_tensor(w3, B[0].rearrange("p (h j) -> p h j", j=HD), cols(rsum[s], HD), ALU.mult).then_inc(a_step[s], 1)
                    dve.wait_ge(a_step[s], 5 * it + 1)
                    V.tensor_reduce(sm[:, 2:3], w[:, :], AX.X, ALU.max, apply_absolute_value=True).then_inc(a_step[s], 1)
                    dve.wait_ge(a_step[s], 5 * it + 2)
                    V.tensor_scalar(sm[:, 3:4], sm[:, 2:3], 1e-5, 1.0 / 127.0, ALU.max, ALU.mult).then_inc(a_step[s], 1)
                    dve.wait_ge(a_step[s], 5 * it + 3)
                    V.tensor_scalar(deq[s][:, 0:1], sm[:, 3:4], wmean[:, 3:4], None, ALU.mult).then_inc(a_step[s], 1)
                    V.reciprocal(q_scale[s][:, 1:2], sm[:, 3:4]).then_inc(a_step[s], 1)
                if k == 9:
                    dve.wait_ge(o_mm[s], it + 1)
                    dve.wait_ge(x_in[s], 16 * it + 16)
                    dve.wait_ge(a_step[s], 5 * it + 4)
                    V.scalar_tensor_tensor(x1[s][:, :], B[2][:, :], deq[s][:, 0:1], xt[s][:, :], ALU.mult, ALU.add).then_inc(x1_ok[s], 1)
                if k == 11:
                    l10 = 10 * it
                    t = it * SLOTS + s
                    dve.wait_ge(hl_mm[s], it + 1)
                    V.tensor_tensor(logit[s], B[1][:, ER:ER + E], lang[:, bass.ds(t, 1), :].rearrange("p a e -> p (a e)"),
                                    ALU.add).then_inc(l_step[s], 1)
                    dve.wait_ge(l_step[s], l10 + 1)
                    V.memset(sm[:, 15:16], 0.0)
                    V.max(top8[s], logit[s]).then_inc(l_step[s], 1)
                    dve.wait_ge(l_step[s], l10 + 2)
                    V.tensor_scalar(sm[:, 4:5], top8[s][:, 0:1], -1.0, None, ALU.mult).then_inc(l_step[s], 1)
                    V.max_index(topi[s][:, :], top8[s], logit[s]).then_inc(l_step[s], 1)
                    dve.wait_ge(l_step[s], l10 + 4)
                    V.tensor_scalar(keep[s], expert_no, topi[s][:, 0:1], None, ALU.is_equal).then_inc(l_step[s], 1)
                    dve.wait_ge(l_step[s], l10 + 5)
                    V.scalar_tensor_tensor(keep[s], expert_no, topi[s][:, 1:2], keep[s], ALU.is_equal, ALU.add).then_inc(l_step[s], 1)
                    dve.wait_ge(l_step[s], l10 + 6)
                    dve.wait_ge(l_exp[s], it + 1)
                    V.tensor_tensor(ew[s], ew[s], keep[s], ALU.mult).then_inc(l_step[s], 1)
                    dve.wait_ge(l_step[s], l10 + 7)
                    V.tensor_reduce(sm[:, 5:6], ew[s], AX.X, ALU.add).then_inc(l_step[s], 1)
                    dve.wait_ge(l_step[s], l10 + 8)
                    V.reciprocal(sm[:, 6:7], sm[:, 5:6]).then_inc(l_step[s], 1)
                    dve.wait_ge(l_step[s], l10 + 9)
                    V.tensor_scalar(ew[s], ew[s], sm[:, 6:7], 2.0, ALU.mult, ALU.mult).then_inc(l_step[s], 1)
                    dve.wait_ge(l_step[s], l10 + 10)
                    V.tensor_tensor(hg[s].rearrange("p (e r) -> p e r", e=E), B[1][:, 0:ER].rearrange("p (e r) -> p e r", e=E),
                                    cols(ew[s], LR), ALU.mult).then_inc(hg_ok[s], 1)
                if k == 13:
                    z8 = 8 * it
                    dve.wait_ge(z_sq[s], it + 1)
                    V.tensor_scalar(sm[:, 8:9], sq[s][:, 0:1], 1.0 / D, 1e-6, ALU.mult, ALU.add).then_inc(z_step[s], 1)
                    V.tensor_tensor(w[:, :], B[0][:, :], rms_g[:, :], ALU.mult).then_inc(z_step[s], 1)
                    dve.wait_ge(z_step[s], z8 + 2)
                    V.tensor_reduce(sm[:, 9:10], w[:, :], AX.X, ALU.max, apply_absolute_value=True).then_inc(z_step[s], 1)
                    dve.wait_ge(z_step[s], z8 + 3)
                    dve.wait_ge(z_rstd[s], it + 1)
                    V.tensor_scalar(sm[:, 10:11], sm[:, 9:10], rstd[s][:, 1:2], None, ALU.mult).then_inc(z_step[s], 1)
                    dve.wait_ge(z_step[s], z8 + 4)
                    V.tensor_scalar(sm[:, 11:12], sm[:, 10:11], 1.0 / 127.0, 1e-8, ALU.mult, ALU.max).then_inc(z_step[s], 1)
                    dve.wait_ge(z_step[s], z8 + 5)
                    V.tensor_scalar(deq[s][:, 1:2], sm[:, 11:12], 0.5, None, ALU.mult).then_inc(z_step[s], 1)
                    V.reciprocal(sm[:, 12:13], sm[:, 11:12]).then_inc(z_step[s], 1)
                    dve.wait_ge(z_step[s], z8 + 7)
                    V.tensor_scalar(q_scale[s][:, 2:3], sm[:, 12:13], rstd[s][:, 1:2], None, ALU.mult).then_inc(z_step[s], 1)
                if k == 15:
                    for n, (lo, hi) in enumerate(FCH):
                        dve.wait_ge(gu_mm[s], 6 * it + 2 * n + 1)
                        V.tensor_tensor(hid_g[s][:, lo:hi], B[(n % 2) * 2][:, 0:hi - lo], gate_s[:, lo:hi], ALU.mult).then_inc(gu_sc[s], 1)
                        dve.wait_ge(gu_mm[s], 6 * it + 2 * n + 2)
                        V.tensor_tensor(hid_u[s][:, lo:hi], B[(n % 2) * 2 + 1][:, 0:hi - lo], up_s[:, lo:hi], ALU.mult).then_inc(gu_sc[s], 1)
                    for n, (lo, hi) in enumerate(FCH):
                        dve.wait_ge(gu_tanh[s], 3 * it + n + 1)
                        V.scalar_tensor_tensor(hid_t[s][:, lo:hi], hid_t[s][:, lo:hi], 1.0, hid_g[s][:, lo:hi],
                                               ALU.add, ALU.mult).then_inc(gu_h[s], 1)
                        dve.wait_ge(gu_h[s], 6 * it + 2 * n + 1)
                        V.tensor_tensor(hid_u[s][:, lo:hi], hid_u[s][:, lo:hi], hid_t[s][:, lo:hi], ALU.mult).then_inc(gu_h[s], 1)
                    h7 = 7 * it
                    dve.wait_ge(gu_h[s], 6 * it + 6)
                    V.tensor_reduce(sm[:, 13:14], hid_u[s], AX.X, ALU.max, apply_absolute_value=True).then_inc(h_step[s], 1)
                    V.tensor_scalar(sm[:, 14:15], deq[s][:, 1:2], sm[:, 11:12], None, ALU.mult).then_inc(h_step[s], 1)
                    dve.wait_ge(h_step[s], h7 + 2)
                    V.tensor_scalar(sm[:, 13:14], sm[:, 13:14], sm[:, 14:15], 1.0 / 127.0, ALU.mult, ALU.mult).then_inc(h_step[s], 1)
                    dve.wait_ge(h_step[s], h7 + 3)
                    V.tensor_scalar(sq[s][:, 1:2], sm[:, 13:14], 1e-8, None, ALU.max).then_inc(h_step[s], 1)
                    dve.wait_ge(h_step[s], h7 + 4)
                    V.reciprocal(sq[s][:, 2:3], sq[s][:, 1:2]).then_inc(h_step[s], 1)
                    dve.wait_ge(h_step[s], h7 + 5)
                    V.tensor_scalar(q_scale[s][:, 3:4], sq[s][:, 2:3], sm[:, 14:15], None, ALU.mult).then_inc(h_step[s], 1)
                if k == 17:
                    dve.wait_ge(d_mm[s], it + 1)
                    V.scalar_tensor_tensor(w[:, :], B[3][:, :], sq[s][:, 1:2], down_s[:, :], ALU.mult, ALU.mult).then_inc(h_step[s], 1)

            rounds(dve, segment)

        @block.tensor
        def _(pe):
            MM, TR = nc.tensor.matmul, nc.tensor.transpose
            pe.wait_ge(ld["lora"], 32)
            for c in range(KC):
                last = MM(bank[0][c][:, :], loraA[:, c * P:(c + 1) * P], loraB, start=True, stop=True)
            last.then_inc(delta_mm, 1)
            dg = diag
            for n in range(2):
                pe.wait_ge(diag_ok, n + 1)
                if n:
                    pe.wait_ge(near_col, 1)
                    TR(bank[0][0][0:1, 0:P], cell[:, 1:2], ident).then_inc(near_row, 1)
                for g in range(KC):
                    last = MM(bank[1][g][:, :], ones, dg[:, g * D:(g + 1) * D], start=True, stop=True)
                last.then_inc(bc_mm, 1)
            pe.wait_ge(abs_sum, 4)
            MM(bank[0][3][:, 0:4], ones, wabs[:, :], start=True, stop=True).then_inc(abs_tot, 1)
            g_bf = a1[:, 4096:4096 + D // 2].bitcast(bf16)
            u_bf = a1[:, 4608:4608 + D // 2].bitcast(bf16)
            d_bf = a1[:, 5120:5120 + F // 2].bitcast(bf16)

            def turn_rows(c, n):
                for j, buf in enumerate((g_bf, u_bf)):
                    pe.wait_ge(gu_q, 2 * c + j + 1)
                    pe.wait_ge(gu_ev, 2 * c)
                    dst = bank[0][j][:, 0:256].bitcast(bf16)
                    for i in range(KC):
                        last = TR(dst[:, i * P:i * P + n], buf[0:n, i * P:(i + 1) * P], ident_bf[0:n, 0:n])
                    last.then_inc(gu_T, 1)

            turn_rows(0, P)
            with pe.Fori(1, FC - 1) as c:
                turn_rows(c, P)
            turn_rows(FC - 1, FL)

            def turn_down(c):
                pe.wait_ge(d_q, c + 1)
                pe.wait_ge(d_ev, c)
                for f in range(FC):
                    n = P if f < FC - 1 else FL
                    dst = bank[1][f // 4][:, 0:256].bitcast(bf16)
                    last = TR(dst[0:n, (f % 4) * P:(f % 4 + 1) * P], d_bf[:, f * P:f * P + n], ident_bf[:, :])
                last.then_inc(d_T, 1)

            turn_down(0)
            with pe.Fori(1, KC) as c:
                turn_down(c)
            pe.wait_ge(diag_ok, 3)
            pe.wait_ge(gu_ev, 2 * FC)
            pe.wait_ge(d_ev, KC)
            NCH = 2 * FC + KC
            for b in range(-(-NCH // 4)):
                n = min(4, NCH - 4 * b) * P
                MM(bank[b // 4 % 2][b % 4][:, 0:n], ones, a0[:, b * 512:b * 512 + n], start=True, stop=True).then_inc(row_mm, 1)
            pe.wait_ge(row_ev, -(-NCH // 4))
            pe.wait_ge(w_eff_ready, 1)
            pe.wait_ge(cast_ready, 1)
            pe.wait_ge(ld["c2"], 64)

            def turn(dst, src, idn):
                for i in range(KC):
                    last = TR(dst[:, i * P:(i + 1) * P], src[:, i * P:(i + 1) * P], idn)
                return last

            def segment(s, k, it):
                B, w = bank[s], work[s]
                if k == 0:
                    pe.wait_ge(xT_in[s], 16 * it + 16)
                    pe.wait_ge(hT[s], 3 * it)
                    for c in range(KC):
                        last = MM(B[0][:, :], xT[s][:, c, :], w_eff[:, c, :], start=c == 0, stop=c == KC - 1)
                    last.then_inc(y_mm[s], 1)
                if k == 1:
                    pe.wait_ge(yq[s], it + 1)
                    turn(B[1], w, ident).then_inc(yqT_mm[s], 1)
                if k == 2:
                    pe.wait_ge(yqT[s], it + 1)
                    pe.wait_ge(h_step[s], 7 * it)
                    for c in range(KC):
                        MM(B[2][:, :], work_bf[s][:, c, :], w_qkv[:, c, 0:D], start=c == 0, stop=c == KC - 1)
                    for c in range(KC):
                        last = MM(B[3][:, 0:2 * KV], work_bf[s][:, c, :], w_qkv[:, c, D:], start=c == 0, stop=c == KC - 1)
                    last.then_inc(qkv_mm[s], 1)
                if k == 3:
                    pe.wait_ge(qk[s], it + 1)
                    turn(B[0], rope_c[s], ident).then_inc(qkT_mm[s], 1)
                    TR(B[1][:, 0:P], rope_c[s][:, D:QK], ident).then_inc(qkT_mm[s], 1)
                    pe.wait_ge(v_ev[s], it + 1)
                    for b in range(NB):
                        last = MM(B[2][:, b * P:(b + 1) * P], rep[:, b * P:(b + 1) * P], v_row[s], start=True, stop=True)
                    last.then_inc(v_mm[s], 1)
                if k == 4:
                    pe.wait_ge(qT[s], it + 1)
                    pe.wait_ge(kbd[s], it + 1)
                    for r in range(R):
                        dst = B[(3, 0)[r // 2]][:, (r % 2) * 256:(r % 2 + 1) * 256]
                        for b in range(NB):
                            q0 = r * P + b * SEQ
                            last = MM(dst[b * SEQ:(b + 1) * SEQ, :], q_T[s][:, q0:q0 + SEQ],
                                      k_bd[s][:, b * 256:(b + 1) * 256], start=True, stop=True, tile_position=(0, b * SEQ))
                        if r % 2:
                            last.then_inc(s_mm[s], 1)
                if k == 5:
                    for j in range(2):
                        pe.wait_ge(s_exp[s], 2 * it + j + 1)
                        if j:
                            pe.wait_ge(vbd[s], it + 1)
                        turn(B[1 + j], prob[s][:, 512 * j:512 * (j + 1)], ident).then_inc(pT_mm[s], 1)
                if k == 6:
                    pe.wait_ge(pT[s], 2 * it + 2)
                    pe.wait_ge(vbd[s], it + 1)
                    pt = prob_T[s].rearrange("p (r e b q) -> p r e b q", r=R, e=2, b=NB)
                    for b in range(NB):
                        for e in range(2):
                            last = MM(B[3][64 * e:64 * (e + 1), b * P:(b + 1) * P],
                                      v_bd[s][:, (b * 2 + e) * 64:(b * 2 + e + 1) * 64], pt[:, :, e, b, :],
                                      start=True, stop=True, tile_position=(0, 64 * e))
                    last.then_inc(pv_mm[s], 1)
                if k == 7:
                    pe.wait_ge(attT[s], it + 1)
                    turn(B[0], att_T[s], ident).then_inc(att_mm[s], 1)
                if k == 8:
                    pe.wait_ge(aq[s], it + 1)
                    turn(B[1], w, ident).then_inc(aqT_mm[s], 1)
                if k == 9:
                    pe.wait_ge(aqT[s], it + 1)
                    for c in range(KC):
                        last = MM(B[2][:, :], work_bf[s][:, c, :], w_o[:, c, :], start=c == 0, stop=c == KC - 1)
                    last.then_inc(o_mm[s], 1)
                if k == 10:
                    pe.wait_ge(x1_ok[s], it + 1)
                    turn(B[3], x1[s], ident).then_inc(x1T_mm[s], 1)
                if k == 11:
                    pe.wait_ge(x1T_ok[s], it + 1)
                    for c in range(KC):
                        last = MM(B[1][:, 0:ER + E], x1T[s][:, c, :], w_c2[:, c, D:W2N], start=c == 0, stop=c == KC - 1)
                    last.then_inc(hl_mm[s], 1)
                    for c in range(KC):
                        MM(B[0][:, :], x1T[s][:, c, :], w_c2[:, c, 0:D], start=c == 0, stop=False)
                if k == 12:
                    pe.wait_ge(hg_ok[s], it + 1)
                    TR(B[2][:, 0:P], hg[s][:, :], ident).then_inc(hgT_mm[s], 1)
                if k == 13:
                    pe.wait_ge(hgT[s], it + 1)
                    MM(B[0][:, :], hg_T[s][:, :], b_c2[:, :], start=False, stop=True).then_inc(c2_mm[s], 1)
                if k == 14:
                    pe.wait_ge(zq[s], it + 1)
                    turn(B[3], w, ident).then_inc(zT_mm[s], 1)
                if k == 15:
                    pe.wait_ge(zT[s], it + 1)
                    for n, (lo, hi) in enumerate(FCH):
                        if n == 2:
                            pe.wait_ge(gu_sc[s], 6 * it + 2)
                        for j, wt in enumerate((w_gate, w_up)):
                            for c in range(KC):
                                last = MM(B[(n % 2) * 2 + j][:, 0:hi - lo], work_bf[s][:, c, :], wt[:, c, lo:hi],
                                          start=c == 0, stop=c == KC - 1)
                            last.then_inc(gu_mm[s], 1)
                if k == 16:
                    pe.wait_ge(hq[s], it + 1)
                    for f in range(FC):
                        n = P if f < FC - 1 else FL
                        last = TR(B[f // 4][0:n, (f % 4) * P:(f % 4 + 1) * P], hid_g[s][:, f * P:f * P + n], ident)
                        if f % 4 == 3 or f == FC - 1:
                            last.then_inc(hT_mm[s], 1)
                if k == 17:
                    for f in range(FC):
                        n = P if f < FC - 1 else FL
                        if f % 4 == 0:
                            pe.wait_ge(hT[s], 3 * it + f // 4 + 1)
                        last = MM(B[3][:, :], hid_bf[s][0:n, f, :], w_down[0:n, f, :], start=f == 0, stop=f == FC - 1)
                    last.then_inc(d_mm[s], 1)

            rounds(pe, segment)


_OUT = "out"


def _constants():
    import numpy as np
    P, SEQ, HD, G, R, NB, E = 128, 32, 16, 8, 4, 4, 8
    p = np.arange(P)
    ident = np.eye(P, dtype=np.float32)
    inv = (1.0 / np.float32(10000.0) ** (np.arange(0, HD, 2, dtype=np.float32) / HD)).astype(np.float32)
    ang = (np.arange(SEQ, dtype=np.float32)[:, None] * inv[None, :]).astype(np.float32).astype(np.float64)
    cos, sin = np.cos(ang), np.sin(ang)
    heads = G * R + G
    cos_t = np.tile(np.tile(np.concatenate([cos, cos], 1), (NB, 1)), (1, heads)).astype(np.float32)
    sin_t = np.tile(np.tile(np.concatenate([-sin, sin], 1), (NB, 1)), (1, heads)).astype(np.float32)
    mask_k = (p[:, None] // HD == np.arange(G)[None, :]).astype(np.float32)
    mask_v = (p[:, None] // SEQ == np.arange(G // 2)[None, :]).astype(np.float32)
    rep = np.concatenate([(p[:, None] == b * SEQ + p[None, :] % SEQ).astype(np.float32) for b in range(NB)], 1)
    expert = np.tile(np.arange(E, dtype=np.float32), (P, 1))
    ones = np.ones((P, P), np.float32)
    return np.ascontiguousarray(np.concatenate([ident, cos_t, sin_t, mask_k, mask_v, rep, expert, ones], 1))


def kernel(**inputs):
    import numpy as np
    import concourse.bacc as bacc
    from concourse import mybir
    from concourse.bass_utils import run_bass_kernel_spmd

    a = {k: np.asarray(v) for k, v in inputs.items()}
    P, D, G, R, HD = 128, 512, 8, 4, 16
    KC, NT = D // P, a["x"].shape[0] * a["x"].shape[1] // P
    F = a["L0_ffn_Wg"].shape[0]
    FC = -(-F // P)

    def by_chunk(w):
        return w.T.reshape(w.shape[1] // P, P, w.shape[0]).transpose(1, 0, 2)

    def padded_rows(w):
        return np.concatenate([w, w[:FC * P - F]]).reshape(FC, P, D)

    wq = a["L0_attn_Wq"].reshape(G, R, HD, D).transpose(1, 0, 2, 3).reshape(D, D)
    wo = a["L0_attn_Wo"].reshape(D, G, R, HD).transpose(0, 2, 1, 3).reshape(D, D)
    c2a, c2b = a["L0_cond2_A"], a["L0_cond2_B"]
    arrays = {
        "x_tok": a["x"].reshape(NT, P, D),
        "x_T": a["x"].reshape(NT, P, KC, P).transpose(0, 3, 2, 1),
        "ids": np.repeat(a["itok_B_0_7"], a["x"].shape[1]).reshape(NT, P).T,
        "codebook": a["condB_codebook"].reshape(1, -1),
        "w_cond": by_chunk(a["L0_cond_weight"]),
        "scale_log": a["L0_cond_scale_log"].reshape(D // P, P, KC).transpose(1, 2, 0).reshape(P, -1),
        "lora_A": a["L0_cond_lora_A"],
        "lora_B": a["L0_cond_lora_B"].T,
        "ln_g": a["L0_attn_ln_w"].reshape(1, D), "ln_b": a["L0_attn_ln_b"].reshape(1, D),
        "w_qkv": by_chunk(np.concatenate([wq, a["L0_attn_Wk"], a["L0_attn_Wv"]], 0)),
        "w_o": by_chunk(wo),
        "c2_w": by_chunk(a["L0_cond2_W"]),
        "c2_a": by_chunk(c2a.reshape(-1, D)),
        "c2_wr": by_chunk(a["L0_cond2_Wr"]),
        "c2_b": c2b.transpose(0, 2, 1).reshape(-1, D),
        "rms_g": a["L0_ffn_rmsnorm_weight"].reshape(1, D),
        "ffn_wg": padded_rows(a["L0_ffn_Wg"]), "ffn_wu": padded_rows(a["L0_ffn_Wu"]),
        "ffn_wd": a["L0_ffn_Wd"].reshape(KC, P, F),
        "consts": _constants(),
    }
    arrays = {k: np.ascontiguousarray(v) for k, v in arrays.items()}
    nc = bacc.Bacc("TRN2", target_bir_lowering=False, num_devices=1)
    d = {k: nc.dram_tensor("in_" + k, v.shape, mybir.dt.from_np(v.dtype), kind="ExternalInput").ap() for k, v in arrays.items()}
    d["out"] = nc.dram_tensor("out", (NT, P, D), mybir.dt.float32, kind="ExternalOutput").ap()
    adaln_attn_ffn_kernel(nc, d)
    r = run_bass_kernel_spmd(nc, [{"in_" + k: v for k, v in arrays.items()}], core_ids=[0])
    return r.results[0]["out"].reshape(a["x"].shape)
```

```python
import concourse.bass as bass
from concourse import mybir
from contextlib import ExitStack


def adaln_attn_ffn_kernel(nc, d):
    f32, bf16, i32, u8 = mybir.dt.float32, mybir.dt.bfloat16, mybir.dt.int32, mybir.dt.uint8
    ALU, ACT, AX = mybir.AluOpType, mybir.ActivationFunctionType, mybir.AxisListType

    NT, P, D = d["x_tok"].shape
    KC = D // P
    SLOTS = 4
    ITERS = NT // SLOTS
    SEQ, HD, G, R = 32, 16, 8, 4
    NB = P // SEQ
    H = G * R
    KV = G * HD
    QK = D + KV
    HALF = G // 2
    RANK = d["lora_A"].shape[0]
    E, LR = d["c2_wr"].shape[2], d["c2_b"].shape[0] // d["c2_wr"].shape[2]
    ER = E * LR
    W2N = D + ER + E
    F = d["ffn_wd"].shape[2]
    FC = -(-F // P)
    FL = F - (FC - 1) * P
    NCB = d["codebook"].shape[1]
    E_HI = 2.7182817459106445
    E_REST = 3.0367860004432146e-08
    MAGIC = 12582912.0
    FCH = [(n, min(n + 512, F)) for n in range(0, F, 512)]
    STAGES = ("cond", "norm", "norm_round", "y_T", "qkv", "rope", "qk_T", "scores", "softmax", "softmax_sum",
              "p_T", "pv", "att", "att_T", "o", "x1_T", "router", "gates", "hg_T", "lora", "rms", "z_T",
              "gate_up0", "gate_up1", "gate_up2", "hidden0", "hidden1", "hidden2", "h_round", "h_T", "down", "out")

    ctx = ExitStack()
    with ctx:
        def sb(name, shape, dt=f32):
            return ctx.enter_context(nc.sbuf_tensor(name, shape, dt))

        def sem(name):
            return ctx.enter_context(nc.semaphore(name))

        def sems(name):
            return [sem(f"{name}{s}") for s in range(SLOTS)]

        consts = sb("consts", [P, d["consts"].shape[1]])
        at = [0]

        def const(n):
            at[0] += n
            return consts[:, at[0] - n:at[0]]

        ident, cos_t, sin_t = const(P), const(QK), const(QK)
        mask_k, mask_v = const(G), const(HALF)
        rep = const(NB * P)
        expert_no, ones = const(E), const(P)
        ident_bf = sb("ident_bf", [P, P], bf16)
        neg_half = sb("neg_half", [P, 1])
        euler = sb("euler", [P, KC * KC])

        w_eff = sb("w_eff", [P, KC, D])
        w_qkv = sb("w_qkv", [P, KC, D + 2 * KV], bf16)
        w_o = sb("w_o", [P, KC, D], bf16)
        w_c2 = sb("w_c2", [P, KC, W2N])
        b_c2 = sb("b_c2", [ER, D])
        w_gate = sb("w_gate", [P, KC, F], bf16)
        w_up = sb("w_up", [P, KC, F], bf16)
        w_down = sb("w_down", [P, FC, D], bf16)
        ln_g, ln_b, rms_g = sb("ln_g", [P, D]), sb("ln_b", [P, D]), sb("rms_g", [P, D])
        gate_s, up_s, down_s = sb("gate_s", [P, F]), sb("up_s", [P, F]), sb("down_s", [P, D])
        wmean = sb("wmean", [P, 4])
        wrecip = sb("wrecip", [P, 4])
        wabs = sb("wabs", [P, 4])
        lang = sb("lang", [P, NT, E])
        col_s = sb("col_s", [P, 2 * FC + KC])

        A_WORDS = 4480
        area_all = sb("area", [P, SLOTS * A_WORDS])
        area = [area_all[:, s * A_WORDS:(s + 1) * A_WORDS] for s in range(SLOTS)]
        xT = [sb(f"xT{s}", [P, KC, P]) for s in range(SLOTS)]
        xt = [sb(f"xt{s}", [P, D]) for s in range(SLOTS)]
        work = [sb(f"work{s}", [P, D]) for s in range(SLOTS)]
        work_bf = [sb(f"work_bf{s}", [P, KC, P], bf16) for s in range(SLOTS)]
        x1 = [sb(f"x1_{s}", [P, D]) for s in range(SLOTS)]
        small = [sb(f"small{s}", [P, 192]) for s in range(SLOTS)]

        def carve(t, sizes):
            out, o = [], 0
            for n in sizes:
                out.append(t[:, o:o + n])
                o += n
            return out

        att_sizes = [QK, QK, KV, D, NB * G * SEQ, NB * 2 * 64, H * SEQ]
        rope_c, rope_s, v_row, q_T, k_bd, v_bd, prob = zip(*[carve(a, att_sizes) for a in area])
        prob_T = [a[:, QK:QK + H * SEQ] for a in area]
        att_T = [v[:, 0:D] for v in rope_c]
        x1T = [v[:, 0:D].rearrange("p (c n) -> p c n", c=KC) for v in prob]
        hg, hg_T, squares = zip(*[carve(a, [ER, P, D]) for a in area])
        hid_g, hid_u, hid_t = zip(*[carve(a, [F, F, F]) for a in area])
        hid_bf = [a[:, 2 * F + F % 2:2 * F + F % 2 + FC * P // 2].bitcast(bf16).rearrange("p (f n) -> p f n", f=FC) for a in area]
        (st, mv, rstd, q_scale, deq, v_scale, smax, rsum, logit, top8, keep, ew, sq,
         steps) = zip(*[carve(t, [6, 2, 2, 4, 2, 1, H, H, E, 8, E, E, 4, 20]) for t in small])
        topi = [sb(f"topi{s}", [P, 8], mybir.dt.uint32) for s in range(SLOTS)]

        psum = [ctx.enter_context(nc.psum_tensor(f"bank{b}", [P, 512], f32)) for b in range(2 * SLOTS)]
        bank = [psum[2 * s:2 * s + 2] for s in range(SLOTS)]

        ld = {n: sem("ld_" + n) for n in ("consts", "lora", "w", "sl", "qkv", "o", "c2", "vec")}
        ld_g, ld_u, ld_d = sem("ld_g"), sem("ld_u"), sem("ld_d")
        delta_mm, scale_exp, diag_ok = sem("delta_mm"), sem("scale_exp"), sem("diag_ok")
        bc_mm = sem("bc_mm")
        prep = sem("prep")
        near_col, near_row = sem("near_col"), sem("near_row")
        w_eff_ready = sem("w_eff_ready")
        abs_sum, abs_tot = sem("abs_sum"), sem("abs_tot")
        cast_ready = sem("cast_ready")
        gu_q, gu_T, gu_ev = sem("gu_q"), sem("gu_T"), sem("gu_ev")
        d_q, d_T, d_ev = sem("d_q"), sem("d_T"), sem("d_ev")
        row_step, row_mm, row_ev = sem("row_step"), sem("row_mm"), sem("row_ev")
        search = sem("search")
        c_ready = sem("c_ready")

        TICKS = 16

        class Step:
            def __init__(self, sem, before, n):
                self.sem, self.before, self.n = sem, before, n
                self.full = TICKS - before - n + 1

            def done(self, it, j=None):
                j = self.before + (self.n if j is None else j)
                return it * TICKS + j

            def phase_done(self, it):
                return it * TICKS + TICKS

            def last(self, it):
                return it * TICKS

        def phase(name, *ns):
            group, out, before = sems(name), [], 0
            for n in ns:
                out.append(Step(group, before, n))
                before += n
            return out if len(out) > 1 else out[0]

        xT_in, x_in, out_st = phase("xT_in", 16), phase("x_in", 16), phase("out_st", 16)
        y_mm, yqT_mm, qkv_mm = phase("cond_pe", 1, 1, 1)
        qkT_mm, s_mm, v_mm, pT_mm, pv_mm, att_mm = phase("att_pe", 2, 2, 1, 2, 1, 1)
        aqT_mm, o_mm, x1T_mm = phase("oproj_pe", 1, 1, 1)
        hl_mm, hgT_mm, c2_mm, zT_mm = phase("lora_pe", 1, 1, 1, 1)
        gu_mm = phase("gate_up_pe", 6)
        hT_mm, d_mm = phase("down_pe", 3, 1)
        yq, yqT, v_ev = phase("cond_act", 1, 1, 1)
        qT, s_exp, pT, attT = phase("att_act", 1, 2, 2, 1)
        aq, aqT, x1T_ok = phase("oproj_act", 1, 1, 1)
        l_exp, hgT, z_sq, zq, zT = phase("lora_act", 1, 1, 1, 1, 1)
        gu_tanh, hq, hT = phase("ffn_act", 3, 1, 3)
        y_step = phase("y_step", 8)
        rope_step = phase("rope_step", 2)
        kbd = phase("kbd", 1)
        s_step, vbd, s_sum = phase("softmax_dve", 4, 1, 2)
        a_step, x1_ok = phase("oproj_dve", 5, 1)
        l_step, hg_ok = phase("router_dve", 10, 1)
        z_step = phase("z_step", 8)
        gu_sc, gu_h = phase("gate_up_dve", 6, 3)
        h_step = phase("h_step", 10)
        y_rstd, z_rstd = phase("rstd_pool", 1, 1)
        qk = phase("qk_pool", 1)
        hid_ok, out_ok = phase("ffn_pool", 3, 1)

        block = ctx.enter_context(nc.Block())

        TURNS = ("3301031222130213021002120133210121323230031203102301113201331023"
                 "0120202102131032032120311302102200311330230213201103203232310132")
        ENTER = (0, 11, 16, 25)
        ORDER, nxt = [], list(ENTER)
        for turn_of in map(int, TURNS):
            ORDER.append((turn_of, STAGES[nxt[turn_of] % len(STAGES)], nxt[turn_of] // len(STAGES)))
            nxt[turn_of] += 1

        def rounds(e, stage):
            for i in (-1, 0):
                for s, k, ahead in ORDER:
                    if i + ahead >= 0:
                        stage(s, k, i + ahead)
            with e.Fori(1, ITERS - 1) as i:
                for s, k, ahead in ORDER:
                    stage(s, k, i + ahead)
            for s, k, ahead in ORDER:
                if not ahead:
                    stage(s, k, ITERS - 1)

        def cols(ap, n):
            return ap.unsqueeze(2).to_broadcast([ap.shape[0], ap.shape[1], n])

        def rows(ap, n):
            return ap.unsqueeze(1).to_broadcast([ap.shape[0], n, ap.shape[1]])

        a0, a1 = area_all[:, 0:3 * KC * D + 512], area_all[:, 3 * KC * D + 512:2 * (3 * KC * D + 512)]
        delta, wg = a0[:, 0:KC * D], a0[:, KC * D:2 * KC * D]
        norm, quant = a1[:, 0:KC * D], a1[:, KC * D:2 * KC * D]
        diag = a0[:, 2 * KC * D:3 * KC * D]
        loraA = xT[0][0:RANK].rearrange("p a b -> p (a b)")
        loraB = xT[1][0:RANK].rearrange("p a b -> p (a b)")
        sl = sb("sl", [P, 2 * KC * KC])
        cbk = sb("cbk", [P, NCB])
        thr = sb("thr", [P, NCB + 1])
        cbx = sb("cbx", [P, 8])
        cell = sb("cell", [P, 8])
        flag = sb("flag", [1, 1], i32)
        picked = w_gate[:, 0, :]
        qkv_f = a1[:, 2 * KC * D:2 * KC * D + 512]
        idf = sb("idf", [P, NT])
        ids = sb("ids", [P, NT], i32)

        @block.sync
        def _(sp):
            sp.dma_start(loraA, d["lora_A"]).then_inc(ld["lora"], 16)
            sp.dma_start(loraB, d["lora_B"]).then_inc(ld["lora"], 16)
            sp.dma_start(consts[:, :], d["consts"]).then_inc(ld["consts"], 16)
            sp.dma_start(wg, d["w_cond"].rearrange("p g o -> p (g o)")).then_inc(ld["w"], 16)
            sp.dma_start(w_c2[:, :, 0:D], d["c2_w"]).then_inc(ld["c2"], 16)
            sp.dma_start(w_c2[:, :, D:D + ER], d["c2_a"]).then_inc(ld["c2"], 16)
            with nc.allow_non_contiguous_dma(reason="router columns, once"):
                sp.dma_start(w_c2[:, :, D + ER:W2N], d["c2_wr"]).then_inc(ld["c2"], 16)
            sp.dma_start(b_c2[:, :], d["c2_b"]).then_inc(ld["c2"], 16)

            sp.wait_ge(w_eff_ready, 1)
            sp.dma_start(a0[:, 0:KC * (D + 2 * KV)], d["w_qkv"].rearrange("p c o -> p (c o)")).then_inc(ld["qkv"], 16)
            sp.dma_start(a0[:, KC * (D + 2 * KV):KC * (2 * D + 2 * KV)],
                         d["w_o"].rearrange("p c o -> p (c o)")).then_inc(ld["o"], 16)
            def load_rows(c, n):
                sp.wait_ge(gu_q, 2 * c)
                sp.dma_start(a1[0:n, 0:D], d["ffn_wg"][bass.ds(c, 1), 0:n, :].rearrange("a p n -> (a p) n")).then_inc(ld_g, 16)
                sp.dma_start(a1[0:n, D:2 * D], d["ffn_wu"][bass.ds(c, 1), 0:n, :].rearrange("a p n -> (a p) n")).then_inc(ld_u, 16)

            load_rows(0, P)
            with sp.Fori(1, FC - 1) as c:
                load_rows(c, P)
            load_rows(FC - 1, FL)

            def load_down(c):
                sp.wait_ge(d_q, c)
                sp.dma_start(a1[:, 2 * D:2 * D + F],
                             d["ffn_wd"][bass.ds(c, 1), :, :].rearrange("a p n -> (a p) n")).then_inc(ld_d, 16)

            load_down(0)
            with sp.Fori(1, KC) as c:
                load_down(c)

            def stage(s, k, it):
                t = it * SLOTS + s
                if k == "cond":
                    sp.wait_ge(y_mm.sem[s], y_mm.last(it))
                    sp.dma_start(xT[s][:, :, :], d["x_T"][bass.ds(t, 1)].rearrange("a p c n -> (a p) c n")).then_inc(xT_in.sem[s], 16)
                    sp.wait_ge(x1_ok.sem[s], x1_ok.last(it))
                    sp.dma_start(xt[s][:, :], d["x_tok"][bass.ds(t, 1)].rearrange("a p n -> (a p) n")).then_inc(x_in.sem[s], 16)
                if k == "out":
                    sp.wait_ge(out_ok.sem[s], out_ok.phase_done(it))
                    sp.dma_start(d["out"][bass.ds(t, 1)].rearrange("a p n -> (a p) n"), work[s][:, :]).then_inc(out_st.sem[s], 16)

            sp.wait_ge(delta_mm, 1)
            rounds(sp, stage)
            for s in range(SLOTS):
                sp.wait_ge(out_st.sem[s], out_st.phase_done(ITERS - 1))

        @block.gpsimd
        def _(pool):
            pool.dma_start(sl[:, 0:KC * KC], d["scale_log"]).then_inc(ld["sl"], 16)
            pool.dma_start(cbk[:, :], d["codebook"].to_broadcast([P, NCB])).then_inc(ld["vec"], 16)
            for v, n in ((ln_g, "ln_g"), (ln_b, "ln_b"), (rms_g, "rms_g")):
                pool.dma_start(v[:, :], d[n].to_broadcast([P, D])).then_inc(ld["vec"], 16)
            pool.dma_start(ids[:, :], d["ids"]).then_inc(ld["vec"], 16)
            nc.gpsimd.memset(neg_half[:, :], -0.5)
            nc.gpsimd.memset(euler[:, :], E_HI).then_inc(c_ready, 1)
            pool.wait_ge(c_ready, 1)
            pool.wait_ge(ld["sl"], 16)
            nc.gpsimd.tensor_tensor(sl[:, KC * KC:2 * KC * KC], euler[:, :], sl[:, 0:KC * KC], ALU.pow).then_inc(scale_exp, 1)

            def stage(s, k, it):
                if k == "norm":
                    pool.wait_ge(y_step.sem[s], y_step.done(it, 3))
                    nc.gpsimd.tensor_tensor(rstd[s][:, 0:1], steps[s][:, 0:1], neg_half[:, :], ALU.pow).then_inc(y_rstd.sem[s], 1)
                if k == "rope":
                    pool.wait_ge(rope_step.sem[s], rope_step.phase_done(it))
                    nc.gpsimd.tensor_tensor(rope_c[s], rope_c[s], rope_s[s], ALU.add).then_inc(qk.sem[s], qk.full)
                if k == "lora":
                    pool.wait_ge(z_step.sem[s], z_step.done(it, 1))
                    nc.gpsimd.tensor_tensor(rstd[s][:, 1:2], steps[s][:, 8:9], neg_half[:, :], ALU.pow).then_inc(z_rstd.sem[s], z_rstd.full)
                for n, (lo, hi) in enumerate(FCH):
                    if k == f"hidden{n}":
                        pool.wait_ge(gu_h.sem[s], gu_h.done(it, n + 1) if n < 2 else gu_h.phase_done(it))
                        nc.gpsimd.tensor_tensor(hid_u[s][:, lo:hi], hid_u[s][:, lo:hi], hid_t[s][:, lo:hi], ALU.mult).then_inc(hid_ok.sem[s], 1)
                if k == "out":
                    pool.wait_ge(h_step.sem[s], h_step.phase_done(it))
                    nc.gpsimd.tensor_tensor(work[s][:, :], work[s][:, :], x1[s][:, :], ALU.add).then_inc(out_ok.sem[s], out_ok.full)

            rounds(pool, stage)

        @block.scalar
        def _(act):
            A = nc.scalar.activation
            act.wait_ge(ld["qkv"], 16)
            wq3 = a0[:, 0:KC * (D + 2 * KV)].rearrange("p (c o) -> p c o", c=KC)
            spare = w_up.rearrange("p c o -> p (c o)").bitcast(f32)[:, 0:KC * D]
            junk = spare[:, 0:KC * KV].rearrange("p (c o) -> p c o", c=KC)
            A(spare.rearrange("p (c o) -> p c o", c=KC), wq3[:, :, 0:D], ACT.Abs, accum_out=wabs[:, 0:1]).then_inc(abs_sum, 1)
            act.wait_ge(abs_sum, 1)
            A(junk, wq3[:, :, D:D + KV], ACT.Abs, accum_out=wabs[:, 1:2]).then_inc(abs_sum, 1)
            act.wait_ge(abs_sum, 2)
            A(junk, wq3[:, :, D + KV:D + 2 * KV], ACT.Abs, accum_out=wabs[:, 2:3]).then_inc(abs_sum, 1)
            act.wait_ge(ld["o"], 16)
            act.wait_ge(abs_sum, 3)
            A(spare, a0[:, KC * (D + 2 * KV):KC * (2 * D + 2 * KV)], ACT.Abs, accum_out=wabs[:, 3:4]).then_inc(abs_sum, 1)

            def out_rows(c, n):
                for j, w in enumerate((w_gate, w_up)):
                    act.wait_ge(gu_T, 2 * c + j + 1)
                    src = psum[j][:, 0:256].bitcast(bf16).rearrange("p (k n) -> p k n", k=KC)[:, :, 0:n]
                    A(w[:, :, bass.ds(c * P, n)], src, ACT.Copy).then_inc(gu_ev, 1)

            out_rows(0, P)
            with act.Fori(1, FC - 1) as c:
                out_rows(c, P)
            out_rows(FC - 1, FL)
            with act.Fori(0, KC) as c:
                act.wait_ge(d_T, c + 1)
                for b in range(3):
                    m = min(4, FC - 4 * b)
                    full = m - 1 if 4 * b + m == FC else m
                    src = psum[4 + b][:, 0:256].bitcast(bf16).rearrange("p (k n) -> p k n", k=4)
                    A(w_down[:, 4 * b:4 * b + full, bass.ds(c * P, P)], src[:, 0:full, :], ACT.Copy)
                    if full < m:
                        A(w_down[0:FL, FC - 1, bass.ds(c * P, P)], src[0:FL, full, :], ACT.Copy).then_inc(d_ev, 1)

            def stage(s, k, it):
                B, w = bank[s], work[s]
                wb = work_bf[s].rearrange("p c n -> p (c n)")
                if k == "norm_round":
                    act.wait_ge(y_step.sem[s], y_step.phase_done(it))
                    A(w[:, :], w[:, :], ACT.Copy, scale=q_scale[s][:, 0:1], bias=MAGIC).then_inc(yq.sem[s], 1)
                if k == "y_T":
                    act.wait_ge(yqT_mm.sem[s], yqT_mm.done(it))
                    A(wb, B[1][:, :], ACT.Copy, bias=-MAGIC).then_inc(yqT.sem[s], 1)
                if k == "rope":
                    act.wait_ge(rope_step.sem[s], rope_step.phase_done(it))
                    A(v_row[s], B[1][:, KV:2 * KV], ACT.Copy, scale=v_scale[s]).then_inc(v_ev.sem[s], v_ev.full)
                if k == "qk_T":
                    act.wait_ge(qkT_mm.sem[s], qkT_mm.done(it))
                    A(q_T[s], B[0][:, :], ACT.Copy).then_inc(qT.sem[s], 1)
                if k == "softmax":
                    for j in range(2):
                        act.wait_ge(s_step.sem[s], s_step.done(it, 2 * j + 2))
                        p = prob[s][:, 512 * j:512 * (j + 1)]
                        A(p, p, ACT.Exp, scale=HD ** -0.5).then_inc(s_exp.sem[s], 1)
                if k == "p_T":
                    for j in range(2):
                        act.wait_ge(pT_mm.sem[s], pT_mm.done(it, j + 1))
                        A(prob_T[s][:, 512 * j:512 * (j + 1)], B[j][:, :], ACT.Copy).then_inc(pT.sem[s], 1)
                if k == "pv":
                    act.wait_ge(pv_mm.sem[s], pv_mm.done(it))
                    A(att_T[s].rearrange("p (r b q) -> p b r q", r=R, b=NB),
                      B[0].rearrange("p (b r q) -> p b r q", b=NB, r=R), ACT.Copy).then_inc(attT.sem[s], attT.full)
                if k == "att":
                    act.wait_ge(a_step.sem[s], a_step.done(it))
                    A(w[:, :], w[:, :], ACT.Copy, scale=q_scale[s][:, 1:2], bias=MAGIC).then_inc(aq.sem[s], 1)
                if k == "att_T":
                    act.wait_ge(aqT_mm.sem[s], aqT_mm.done(it))
                    A(wb, B[0][:, :], ACT.Copy, bias=-MAGIC).then_inc(aqT.sem[s], 1)
                if k == "x1_T":
                    act.wait_ge(x1T_mm.sem[s], x1T_mm.phase_done(it))
                    A(prob[s][:, 0:D], B[0][:, :], ACT.Copy).then_inc(x1T_ok.sem[s], x1T_ok.full)
                if k == "router":
                    act.wait_ge(l_step.sem[s], l_step.done(it, 3))
                    A(ew[s], logit[s], ACT.Exp, bias=steps[s][:, 4:5]).then_inc(l_exp.sem[s], 1)
                if k == "hg_T":
                    act.wait_ge(hgT_mm.sem[s], hgT_mm.done(it))
                    A(hg_T[s], B[1][:, 2 * P:3 * P], ACT.Copy).then_inc(hgT.sem[s], 1)
                if k == "lora":
                    act.wait_ge(c2_mm.sem[s], c2_mm.done(it))
                    A(squares[s], B[0][:, :], ACT.Square, accum_out=sq[s][:, 0:1]).then_inc(z_sq.sem[s], 1)
                if k == "rms":
                    act.wait_ge(z_step.sem[s], z_step.phase_done(it))
                    A(w[:, :], w[:, :], ACT.Copy, scale=q_scale[s][:, 2:3], bias=MAGIC).then_inc(zq.sem[s], 1)
                if k == "z_T":
                    act.wait_ge(zT_mm.sem[s], zT_mm.phase_done(it))
                    A(wb, B[1][:, :], ACT.Copy, bias=-MAGIC).then_inc(zT.sem[s], zT.full)
                for n, (lo, hi) in enumerate(FCH):
                    if k == f"gate_up{n}":
                        act.wait_ge(gu_sc.sem[s], gu_sc.done(it, 2 * n + 1))
                        A(hid_t[s][:, lo:hi], hid_g[s][:, lo:hi], ACT.Tanh, scale=deq[s][:, 1:2]).then_inc(gu_tanh.sem[s], 1)
                if k == "h_round":
                    act.wait_ge(h_step.sem[s], h_step.done(it, 9))
                    A(hid_g[s], hid_u[s], ACT.Copy, scale=q_scale[s][:, 3:4], bias=MAGIC).then_inc(hq.sem[s], 1)
                if k == "h_T":
                    for b in range(3):
                        m = min(4, FC - 4 * b)
                        full = m - 1 if 4 * b + m == FC else m
                        act.wait_ge(hT_mm.sem[s], hT_mm.done(it, b + 1))
                        src = B[b % 2].rearrange("p (k n) -> p k n", k=4)
                        ev = A(hid_bf[s][:, 4 * b:4 * b + full, :], src[:, 0:full, :], ACT.Copy, bias=-MAGIC)
                        if full < m:
                            ev = A(hid_bf[s][0:FL, FC - 1, :], src[0:FL, full, :], ACT.Copy, bias=-MAGIC)
                        ev.then_inc(hT.sem[s], hT.full if b == 2 else 1)

            rounds(act, stage)

        @block.vector
        def _(dve):
            V = nc.vector
            n_prep = [0]

            def step(ins):
                n_prep[0] += 1
                ins.then_inc(prep, 1)
                dve.wait_ge(prep, n_prep[0])

            dve.wait_ge(ld["consts"], 16)
            step(V.tensor_copy(ident_bf[:, :], ident))
            dve.wait_ge(ld["vec"], 80)
            step(V.tensor_copy(idf[:, :], ids[:, :]))
            step(V.tensor_tensor(lang[:, :, :], cols(idf[:, :], E), rows(expert_no, NT), ALU.is_equal))
            step(V.tensor_scalar(lang[:, :, :], lang[:, :, :], 5.0, None, ALU.mult))
            dve.wait_ge(scale_exp, 1)
            step(V.tensor_scalar(sl[:, 0:KC * KC], sl[:, 0:KC * KC], E_REST, 1.0, ALU.mult, ALU.add))
            step(V.tensor_tensor(sl[:, 0:KC * KC], sl[:, 0:KC * KC], sl[:, KC * KC:2 * KC * KC], ALU.mult))
            step(V.reciprocal(sl[:, KC * KC:2 * KC * KC], sl[:, 0:KC * KC]))
            diag3 = diag.rearrange("p (j n) -> p j n", n=P)
            V.tensor_tensor(diag3, rows(ident, KC * KC), cols(sl[:, KC * KC:2 * KC * KC], P), ALU.mult).then_inc(diag_ok, 1)
            step(V.tensor_reduce(cbx[:, 0:1], cbk[:, :], AX.X, ALU.max, apply_absolute_value=True))
            step(V.tensor_scalar(cbx[:, 1:2], cbx[:, 0:1], 1e-8, None, ALU.max))
            step(V.reciprocal(cbx[:, 2:3], cbx[:, 1:2]))
            step(V.tensor_scalar(cbk[:, :], cbk[:, :], cbx[:, 2:3], None, ALU.mult))
            dve.wait_ge(delta_mm, 1)
            for c in range(KC):
                last = V.tensor_scalar(delta[:, c * D:(c + 1) * D], psum[c][:, :], 0.5, None, ALU.mult)
            step(last)
            dve.wait_ge(ld["w"], 16)
            step(V.tensor_tensor(wg, wg, delta, ALU.add))
            dve.wait_ge(bc_mm, 1)
            for c in range(KC):
                last = V.tensor_tensor(norm[:, c * D:(c + 1) * D], wg[:, c * D:(c + 1) * D], psum[4 + c][:, :], ALU.mult)
            step(last)
            V.tensor_tensor(diag3, rows(ident, KC * KC), cols(sl[:, 0:KC * KC], P), ALU.mult).then_inc(diag_ok, 1)
            step(V.tensor_reduce(cell[:, 0:1], norm, AX.X, ALU.min, apply_absolute_value=True))
            step(V.tensor_scalar(quant, norm, 0.0, cbk[:, NCB - 1:NCB], ALU.is_gt, ALU.mult))
            step(V.tensor_scalar(wg, norm, 0.0, cbk[:, 0:1], ALU.is_le, ALU.mult))
            step(V.tensor_tensor(quant, quant, wg, ALU.add))
            nc.vector.tensor_copy(cell[:, 1:2], cell[:, 0:1]).then_inc(near_col, 1)
            dve.wait_ge(near_row, 1)
            step(V.tensor_reduce(cell[0:1, 2:3], psum[0][0:1, 0:P], AX.X, ALU.min))
            step(V.tensor_scalar(flag[:, :], cell[0:1, 2:3], 1.001, None, ALU.is_le))
            near = dve.value_load(flag[0:1, 0:1], min_val=0, max_val=1)
            with dve.If(near == 1):
                m = [0]

                def found(ins):
                    m[0] += 1
                    ins.then_inc(search, 1)
                    dve.wait_ge(search, m[0])

                found(V.memset(thr[:, :], 3e38))
                found(V.memset(thr[:, 0:1], -3e38))
                found(V.tensor_tensor(thr[:, 1:NCB], cbk[:, 0:NCB - 1], cbk[:, 1:NCB], ALU.add))
                found(V.tensor_scalar(thr[:, 1:NCB], thr[:, 1:NCB], 0.5, None, ALU.mult))
                h = NCB // 2
                while h:
                    node = thr[:, h:NCB:2 * h]
                    found(V.tensor_tensor(node, node, thr[:, 0:NCB:2 * h], ALU.max))
                    found(V.tensor_tensor(node, node, thr[:, 2 * h:NCB + 1:2 * h], ALU.min))
                    h //= 2
                found(V.tensor_copy(quant, cbk[:, 0:1].to_broadcast([P, KC * D])))
                base, per = m[0], 4
                mask = picked.bitcast(u8)[:, 0:KC * D]
                with dve.Fori(0, NCB - 1) as j:
                    V.tensor_copy(cbx[:, 4:5], thr[:, bass.ds(j + 1, 1)]).then_inc(search, 1)
                    V.tensor_copy(cbx[:, 5:6], cbk[:, bass.ds(j + 1, 1)]).then_inc(search, 1)
                    dve.wait_ge(search, j * per + (base + 2))
                    V.tensor_scalar(mask, norm, cbx[:, 4:5], None, ALU.is_gt).then_inc(search, 1)
                    dve.wait_ge(search, j * per + (base + 3))
                    V.memset(cell[:, 3:4], 0.0)
                    V.copy_predicated(quant, mask, cbx[:, 5:6].to_broadcast([P, KC * D])).then_inc(search, 1)
                    dve.wait_ge(search, j * per + (base + 4))
            step(V.tensor_tensor(quant, quant, norm, ALU.subtract))
            step(V.tensor_tensor(quant, quant, norm, ALU.add))
            dve.wait_ge(bc_mm, 2)
            for c in range(KC):
                last = V.tensor_tensor(quant[:, c * D:(c + 1) * D], quant[:, c * D:(c + 1) * D], psum[4 + c][:, :], ALU.mult)
            step(last)
            V.tensor_tensor(w_eff.rearrange("p c o -> p (c o)"), quant, delta, ALU.add).then_inc(w_eff_ready, 1)

            dve.wait_ge(abs_tot, 1)
            for j, n in enumerate((D * D, D * KV, D * KV, D * D)):
                last = V.tensor_scalar(wmean[:, j:j + 1], psum[3][:, j:j + 1], 1.0 / n, 1e-5, ALU.mult, ALU.max)
            step(last)
            step(V.reciprocal(wrecip[:, :], wmean[:, :]))
            qkv_src = a0[:, 0:KC * (D + 2 * KV)].rearrange("p (c o) -> p c o", c=KC)
            o_src = a0[:, KC * (D + 2 * KV):KC * (2 * D + 2 * KV)].rearrange("p (c o) -> p c o", c=KC)
            dve.wait_ge(abs_sum, 4)
            parts = ((qkv_src[:, :, 0:D], w_qkv[:, :, 0:D], 0), (qkv_src[:, :, D:D + KV], w_qkv[:, :, D:D + KV], 1),
                     (qkv_src[:, :, D + KV:D + 2 * KV], w_qkv[:, :, D + KV:D + 2 * KV], 2), (o_src, w_o[:, :, :], 3))
            for src, _, j in parts:
                last = V.tensor_scalar(src, src, wrecip[:, j:j + 1], MAGIC, ALU.mult, ALU.add)
            step(last)
            for src, _, j in parts:
                last = V.tensor_scalar(src, src, MAGIC + 1.0, MAGIC - 1.0, ALU.min, ALU.max)
            step(last)
            for src, dst, j in parts:
                last = V.tensor_scalar(dst, src, -MAGIC, None, ALU.add)
            last.then_inc(cast_ready, 1)
            for tab in (cos_t, sin_t):
                V.tensor_scalar(tab[:, 0:D], tab[:, 0:D], wmean[:, 0:1], None, ALU.mult)
                last = V.tensor_scalar(tab[:, D:QK], tab[:, D:QK], wmean[:, 1:2], None, ALU.mult)
            step(last)
            g_bf = a1[:, 4096:4096 + D // 2].bitcast(bf16)
            u_bf = a1[:, 4608:4608 + D // 2].bitcast(bf16)
            d_bf = a1[:, 5120:5120 + F // 2].bitcast(bf16)

            def quant_rows(src, dst, scol, rcol, before, rounded):
                dve.wait_ge(row_step, before)
                V.tensor_reduce(scol, src, AX.X, ALU.max, apply_absolute_value=True).then_inc(row_step, 1)
                dve.wait_ge(row_step, before + 1)
                V.tensor_scalar(scol, scol, 1.0 / 127.0, 1e-8, ALU.mult, ALU.max).then_inc(row_step, 1)
                dve.wait_ge(row_step, before + 2)
                V.reciprocal(rcol, scol).then_inc(row_step, 1)
                dve.wait_ge(row_step, before + 3)
                V.tensor_scalar(src, src, rcol, MAGIC, ALU.mult, ALU.add).then_inc(row_step, 1)
                dve.wait_ge(row_step, before + 4)
                V.tensor_scalar(dst, src, -MAGIC, None, ALU.add).then_inc(rounded, 1)

            def quant_gu(c, n):
                for j, (buf, ldsem) in enumerate(((g_bf, ld_g), (u_bf, ld_u))):
                    dve.wait_ge(ldsem, 16 * c + 16)
                    dve.wait_ge(gu_T, 2 * c)
                    scol = cell[0:n, 4 + j:5 + j]
                    quant_rows(a1[0:n, j * D:(j + 1) * D], buf[0:n, :], scol, cell[0:n, 6 + j:7 + j],
                               10 * c + 5 * j, gu_q)
                    V.tensor_copy(col_s[0:n, bass.ds(2 * c + j, 1)], scol).then_inc(row_step, 1)

            step(V.memset(col_s[:, :], 0.0))
            quant_gu(0, P)
            with dve.Fori(1, FC - 1) as c:
                quant_gu(c, P)
            quant_gu(FC - 1, FL)
            base = 10 * FC

            def quant_down(c):
                dve.wait_ge(ld_d, 16 * c + 16)
                dve.wait_ge(d_T, c)
                quant_rows(a1[:, 2 * D:2 * D + F], d_bf, cell[:, 4:5], cell[:, 6:7], 5 * c + base, d_q)
                V.tensor_copy(col_s[:, bass.ds(2 * FC + c, 1)], cell[:, 4:5]).then_inc(row_step, 1)

            quant_down(0)
            with dve.Fori(1, KC) as c:
                quant_down(c)
            dve.wait_ge(row_step, 10 * FC + 5 * KC)
            NCH = 2 * FC + KC
            dg = a0[:, 0:NCH * P].rearrange("p (j n) -> p j n", n=P)
            V.tensor_tensor(dg, rows(ident, NCH), cols(col_s[:, 0:NCH], P), ALU.mult).then_inc(diag_ok, 1)
            for b in range(-(-NCH // 4)):
                dve.wait_ge(row_mm, b + 1)
                for j in range(4 * b, min(4 * b + 4, NCH)):
                    src = psum[b % 8][:, (j % 4) * P:(j % 4 + 1) * P]
                    if j < 2 * FC:
                        c = j // 2
                        n = P if c < FC - 1 else FL
                        last = V.tensor_copy((gate_s, up_s)[j % 2][:, c * P:c * P + n], src[:, 0:n])
                    else:
                        c = j - 2 * FC
                        last = V.tensor_copy(down_s[:, c * P:(c + 1) * P], src)
                last.then_inc(row_ev, 1)
            dve.wait_ge(row_ev, -(-NCH // 4))

            def stage(s, k, it):
                B, w, sm = bank[s], work[s], steps[s]
                if k == "norm":
                    dve.wait_ge(y_mm.sem[s], y_mm.done(it))
                    V.bn_stats(st[s], B[0][:, :]).then_inc(y_step.sem[s], 1)
                    dve.wait_ge(y_step.sem[s], y_step.done(it, 1))
                    V.memset(sm[:, 15:16], 0.0)
                    V.bn_aggr(mv[s], st[s]).then_inc(y_step.sem[s], 1)
                    dve.wait_ge(y_step.sem[s], y_step.done(it, 2))
                    V.tensor_scalar(sm[:, 0:1], mv[s][:, 1:2], 1e-5, None, ALU.add).then_inc(y_step.sem[s], 1)
                    dve.wait_ge(out_st.sem[s], out_st.last(it))
                    V.scalar_tensor_tensor(w[:, :], B[0][:, :], mv[s][:, 0:1], ln_g[:, :], ALU.subtract, ALU.mult).then_inc(y_step.sem[s], 1)
                if k == "norm_round":
                    dve.wait_ge(y_rstd.sem[s], y_rstd.done(it))
                    dve.wait_ge(y_step.sem[s], y_step.done(it, 4))
                    V.scalar_tensor_tensor(w[:, :], w[:, :], rstd[s][:, 0:1], ln_b[:, :], ALU.mult, ALU.add).then_inc(y_step.sem[s], 1)
                    dve.wait_ge(y_step.sem[s], y_step.done(it, 5))
                    V.tensor_reduce(sm[:, 1:2], w[:, :], AX.X, ALU.max, apply_absolute_value=True).then_inc(y_step.sem[s], 1)
                    dve.wait_ge(y_step.sem[s], y_step.done(it, 6))
                    V.tensor_scalar(deq[s][:, 0:1], sm[:, 1:2], 1e-5, 1.0 / 127.0, ALU.max, ALU.mult).then_inc(y_step.sem[s], 1)
                    dve.wait_ge(y_step.sem[s], y_step.done(it, 7))
                    V.reciprocal(q_scale[s][:, 0:1], deq[s][:, 0:1]).then_inc(y_step.sem[s], y_step.full)
                if k == "qkv":
                    V.tensor_scalar(v_scale[s], deq[s][:, 0:1], wmean[:, 2:3], None, ALU.mult).then_inc(rope_step.sem[s], 1)
                    dve.wait_ge(qkv_mm.sem[s], qkv_mm.phase_done(it))
                    sc = deq[s][:, 0:1]
                    for o, n, src in ((0, D, B[0][:, :]), (D, KV, B[1][:, 0:KV])):
                        V.scalar_tensor_tensor(rope_c[s][:, o:o + n], src, sc, cos_t[:, o:o + n], ALU.mult, ALU.mult)
                        x3 = src.rearrange("p (h j) -> p h j", j=HD)
                        s3 = sin_t[:, o:o + n].rearrange("p (h j) -> p h j", j=HD)
                        o3 = rope_s[s][:, o:o + n].rearrange("p (h j) -> p h j", j=HD)
                        hh = HD // 2
                        V.scalar_tensor_tensor(o3[:, :, 0:hh], x3[:, :, hh:HD], sc, s3[:, :, 0:hh], ALU.mult, ALU.mult)
                        last = V.scalar_tensor_tensor(o3[:, :, hh:HD], x3[:, :, 0:hh], sc, s3[:, :, hh:HD], ALU.mult, ALU.mult)
                    last.then_inc(rope_step.sem[s], rope_step.full)
                if k == "qk_T":
                    dve.wait_ge(qkT_mm.sem[s], qkT_mm.done(it, 1))
                    kT = B[1][:, 0:P].rearrange("p (b q) -> p b q", b=NB)
                    kb = k_bd[s].rearrange("p (b g q) -> p b g q", b=NB, g=G)
                    V.tensor_tensor(kb, kT.unsqueeze(2).to_broadcast([P, NB, G, SEQ]),
                                    mask_k.unsqueeze(1).unsqueeze(3).to_broadcast([P, NB, G, SEQ]), ALU.mult).then_inc(kbd.sem[s], kbd.full)
                def row_max(j):
                    dve.wait_ge(s_mm.sem[s], s_mm.done(it, j + 1))
                    sc = B[j].rearrange("p (h q) -> p h q", q=SEQ)
                    V.tensor_reduce(smax[s][:, 16 * j:16 * (j + 1)], sc, AX.X, ALU.max).then_inc(s_step.sem[s], 1)

                def less_max(j):
                    dve.wait_ge(s_step.sem[s], s_step.done(it, 2 * j + 1))
                    sc = B[j].rearrange("p (h q) -> p h q", q=SEQ)
                    p = prob[s][:, 512 * j:512 * (j + 1)].rearrange("p (h q) -> p h q", q=SEQ)
                    V.tensor_tensor(p, sc, cols(smax[s][:, 16 * j:16 * (j + 1)], SEQ), ALU.subtract).then_inc(s_step.sem[s], 1)

                if k == "scores":
                    row_max(0)
                if k == "softmax":
                    less_max(0)
                    row_max(1)
                    less_max(1)
                    dve.wait_ge(v_mm.sem[s], v_mm.done(it))
                    vr = B[0].rearrange("p (e g j) -> p e g j", e=NB * 2, g=HALF)
                    vb = v_bd[s].rearrange("p (e g j) -> p e g j", e=NB * 2, g=HALF)
                    mk = mask_v.unsqueeze(1).unsqueeze(3).to_broadcast([P, NB * 2, HALF, HD])
                    V.tensor_tensor(vb, vr, mk, ALU.mult).then_inc(vbd.sem[s], 1)
                if k == "softmax_sum":
                    dve.wait_ge(s_exp.sem[s], s_exp.done(it))
                    V.tensor_reduce(rsum[s], prob[s].rearrange("p (h q) -> p h q", q=SEQ), AX.X, ALU.add).then_inc(s_sum.sem[s], 1)
                    dve.wait_ge(s_sum.sem[s], s_sum.done(it, 1))
                    V.reciprocal(rsum[s], rsum[s]).then_inc(s_sum.sem[s], s_sum.full)
                if k == "att":
                    dve.wait_ge(att_mm.sem[s], att_mm.phase_done(it))
                    dve.wait_ge(s_sum.sem[s], s_sum.phase_done(it))
                    w3 = w.rearrange("p (h j) -> p h j", j=HD)
                    V.tensor_tensor(w3, B[1].rearrange("p (h j) -> p h j", j=HD), cols(rsum[s], HD), ALU.mult).then_inc(a_step.sem[s], 1)
                    dve.wait_ge(a_step.sem[s], a_step.done(it, 1))
                    V.tensor_reduce(sm[:, 2:3], w[:, :], AX.X, ALU.max, apply_absolute_value=True).then_inc(a_step.sem[s], 1)
                    dve.wait_ge(a_step.sem[s], a_step.done(it, 2))
                    V.tensor_scalar(sm[:, 3:4], sm[:, 2:3], 1e-5, 1.0 / 127.0, ALU.max, ALU.mult).then_inc(a_step.sem[s], 1)
                    dve.wait_ge(a_step.sem[s], a_step.done(it, 3))
                    V.tensor_scalar(deq[s][:, 0:1], sm[:, 3:4], wmean[:, 3:4], None, ALU.mult).then_inc(a_step.sem[s], 1)
                    V.reciprocal(q_scale[s][:, 1:2], sm[:, 3:4]).then_inc(a_step.sem[s], 1)
                if k == "o":
                    dve.wait_ge(o_mm.sem[s], o_mm.done(it))
                    dve.wait_ge(x_in.sem[s], x_in.phase_done(it))
                    dve.wait_ge(a_step.sem[s], a_step.done(it, 4))
                    V.scalar_tensor_tensor(x1[s][:, :], B[1][:, :], deq[s][:, 0:1], xt[s][:, :], ALU.mult, ALU.add).then_inc(x1_ok.sem[s], x1_ok.full)
                if k == "router":
                    t = it * SLOTS + s
                    dve.wait_ge(hl_mm.sem[s], hl_mm.done(it))
                    V.tensor_tensor(logit[s], B[1][:, ER:ER + E], lang[:, bass.ds(t, 1), :].rearrange("p a e -> p (a e)"),
                                    ALU.add).then_inc(l_step.sem[s], 1)
                    dve.wait_ge(l_step.sem[s], l_step.done(it, 1))
                    V.memset(sm[:, 15:16], 0.0)
                    V.max(top8[s], logit[s]).then_inc(l_step.sem[s], 1)
                    dve.wait_ge(l_step.sem[s], l_step.done(it, 2))
                    V.tensor_scalar(sm[:, 4:5], top8[s][:, 0:1], -1.0, None, ALU.mult).then_inc(l_step.sem[s], 1)
                    V.max_index(topi[s][:, :], top8[s], logit[s]).then_inc(l_step.sem[s], 1)
                    dve.wait_ge(l_step.sem[s], l_step.done(it, 4))
                    V.tensor_scalar(keep[s], expert_no, topi[s][:, 0:1], None, ALU.is_equal).then_inc(l_step.sem[s], 1)
                if k == "gates":
                    dve.wait_ge(l_step.sem[s], l_step.done(it, 5))
                    V.scalar_tensor_tensor(keep[s], expert_no, topi[s][:, 1:2], keep[s], ALU.is_equal, ALU.add).then_inc(l_step.sem[s], 1)
                    dve.wait_ge(l_step.sem[s], l_step.done(it, 6))
                    dve.wait_ge(l_exp.sem[s], l_exp.done(it))
                    V.tensor_tensor(ew[s], ew[s], keep[s], ALU.mult).then_inc(l_step.sem[s], 1)
                    dve.wait_ge(l_step.sem[s], l_step.done(it, 7))
                    V.tensor_reduce(sm[:, 5:6], ew[s], AX.X, ALU.add).then_inc(l_step.sem[s], 1)
                    dve.wait_ge(l_step.sem[s], l_step.done(it, 8))
                    V.reciprocal(sm[:, 6:7], sm[:, 5:6]).then_inc(l_step.sem[s], 1)
                    dve.wait_ge(l_step.sem[s], l_step.done(it, 9))
                    V.tensor_scalar(ew[s], ew[s], sm[:, 6:7], 2.0, ALU.mult, ALU.mult).then_inc(l_step.sem[s], 1)
                    dve.wait_ge(l_step.sem[s], l_step.done(it))
                    V.tensor_tensor(hg[s].rearrange("p (e r) -> p e r", e=E), B[1][:, 0:ER].rearrange("p (e r) -> p e r", e=E),
                                    cols(ew[s], LR), ALU.mult).then_inc(hg_ok.sem[s], hg_ok.full)
                if k == "lora":
                    dve.wait_ge(z_sq.sem[s], z_sq.done(it))
                    V.tensor_scalar(sm[:, 8:9], sq[s][:, 0:1], 1.0 / D, 1e-6, ALU.mult, ALU.add).then_inc(z_step.sem[s], 1)
                    V.tensor_tensor(w[:, :], B[0][:, :], rms_g[:, :], ALU.mult).then_inc(z_step.sem[s], 1)
                if k == "rms":
                    dve.wait_ge(z_step.sem[s], z_step.done(it, 2))
                    V.tensor_reduce(sm[:, 9:10], w[:, :], AX.X, ALU.max, apply_absolute_value=True).then_inc(z_step.sem[s], 1)
                    dve.wait_ge(z_step.sem[s], z_step.done(it, 3))
                    dve.wait_ge(z_rstd.sem[s], z_rstd.phase_done(it))
                    V.tensor_scalar(sm[:, 10:11], sm[:, 9:10], rstd[s][:, 1:2], None, ALU.mult).then_inc(z_step.sem[s], 1)
                    dve.wait_ge(z_step.sem[s], z_step.done(it, 4))
                    V.tensor_scalar(sm[:, 11:12], sm[:, 10:11], 1.0 / 127.0, 1e-8, ALU.mult, ALU.max).then_inc(z_step.sem[s], 1)
                    dve.wait_ge(z_step.sem[s], z_step.done(it, 5))
                    V.tensor_scalar(deq[s][:, 1:2], sm[:, 11:12], 0.5, None, ALU.mult).then_inc(z_step.sem[s], 1)
                    V.reciprocal(sm[:, 12:13], sm[:, 11:12]).then_inc(z_step.sem[s], 1)
                    dve.wait_ge(z_step.sem[s], z_step.done(it, 7))
                    V.tensor_scalar(q_scale[s][:, 2:3], sm[:, 12:13], rstd[s][:, 1:2], None, ALU.mult).then_inc(z_step.sem[s], z_step.full)
                for n, (lo, hi) in enumerate(FCH):
                    if k == f"gate_up{n}":
                        dve.wait_ge(gu_mm.sem[s], gu_mm.done(it, 2 * n + 1))
                        V.tensor_tensor(hid_g[s][:, lo:hi], B[0][:, 0:hi - lo], gate_s[:, lo:hi], ALU.mult).then_inc(gu_sc.sem[s], 1)
                        dve.wait_ge(gu_mm.sem[s], gu_mm.done(it, 2 * n + 2) if n < 2 else gu_mm.phase_done(it))
                        V.tensor_tensor(hid_u[s][:, lo:hi], B[1][:, 0:hi - lo], up_s[:, lo:hi], ALU.mult).then_inc(gu_sc.sem[s], 1)
                    if k == f"hidden{n}":
                        dve.wait_ge(gu_tanh.sem[s], gu_tanh.done(it, n + 1))
                        V.scalar_tensor_tensor(hid_t[s][:, lo:hi], hid_t[s][:, lo:hi], 1.0, hid_g[s][:, lo:hi],
                                               ALU.add, ALU.mult).then_inc(gu_h.sem[s], gu_h.full if n == 2 else 1)
                    if k == f"hidden{n + 1}" or n == 2 and k == "h_round":
                        dve.wait_ge(hid_ok.sem[s], hid_ok.done(it, n + 1))
                        V.tensor_reduce(sm[:, 16 + n:17 + n], hid_u[s][:, lo:hi], AX.X, ALU.max, apply_absolute_value=True).then_inc(h_step.sem[s], 1)
                if k == "h_round":
                    dve.wait_ge(h_step.sem[s], h_step.done(it, 3))
                    V.tensor_reduce(sm[:, 13:14], sm[:, 16:19], AX.X, ALU.max).then_inc(h_step.sem[s], 1)
                    V.tensor_scalar(sm[:, 14:15], deq[s][:, 1:2], sm[:, 11:12], None, ALU.mult).then_inc(h_step.sem[s], 1)
                    dve.wait_ge(h_step.sem[s], h_step.done(it, 5))
                    V.tensor_scalar(sm[:, 13:14], sm[:, 13:14], sm[:, 14:15], 1.0 / 127.0, ALU.mult, ALU.mult).then_inc(h_step.sem[s], 1)
                    dve.wait_ge(h_step.sem[s], h_step.done(it, 6))
                    V.tensor_scalar(sq[s][:, 1:2], sm[:, 13:14], 1e-8, None, ALU.max).then_inc(h_step.sem[s], 1)
                    dve.wait_ge(h_step.sem[s], h_step.done(it, 7))
                    V.reciprocal(sq[s][:, 2:3], sq[s][:, 1:2]).then_inc(h_step.sem[s], 1)
                    dve.wait_ge(h_step.sem[s], h_step.done(it, 8))
                    V.tensor_scalar(q_scale[s][:, 3:4], sq[s][:, 2:3], sm[:, 14:15], None, ALU.mult).then_inc(h_step.sem[s], 1)
                if k == "down":
                    dve.wait_ge(d_mm.sem[s], d_mm.phase_done(it))
                    V.scalar_tensor_tensor(w[:, :], B[1][:, :], sq[s][:, 1:2], down_s[:, :], ALU.mult, ALU.mult).then_inc(h_step.sem[s], h_step.full)

            rounds(dve, stage)

        @block.tensor
        def _(pe):
            MM, TR = nc.tensor.matmul, nc.tensor.transpose
            pe.wait_ge(ld["lora"], 32)
            for c in range(KC):
                last = MM(psum[c][:, :], loraA[:, c * P:(c + 1) * P], loraB, start=True, stop=True)
            last.then_inc(delta_mm, 1)
            dg = diag
            for n in range(2):
                pe.wait_ge(diag_ok, n + 1)
                if n:
                    pe.wait_ge(near_col, 1)
                    TR(psum[0][0:1, 0:P], cell[:, 1:2], ident).then_inc(near_row, 1)
                for g in range(KC):
                    last = MM(psum[4 + g][:, :], ones, dg[:, g * D:(g + 1) * D], start=True, stop=True)
                last.then_inc(bc_mm, 1)
            pe.wait_ge(abs_sum, 4)
            MM(psum[3][:, 0:4], ones, wabs[:, :], start=True, stop=True).then_inc(abs_tot, 1)
            g_bf = a1[:, 4096:4096 + D // 2].bitcast(bf16)
            u_bf = a1[:, 4608:4608 + D // 2].bitcast(bf16)
            d_bf = a1[:, 5120:5120 + F // 2].bitcast(bf16)

            def turn_rows(c, n):
                for j, buf in enumerate((g_bf, u_bf)):
                    pe.wait_ge(gu_q, 2 * c + j + 1)
                    pe.wait_ge(gu_ev, 2 * c)
                    dst = psum[j][:, 0:256].bitcast(bf16)
                    for i in range(KC):
                        last = TR(dst[:, i * P:i * P + n], buf[0:n, i * P:(i + 1) * P], ident_bf[0:n, 0:n])
                    last.then_inc(gu_T, 1)

            turn_rows(0, P)
            with pe.Fori(1, FC - 1) as c:
                turn_rows(c, P)
            turn_rows(FC - 1, FL)

            def turn_down(c):
                pe.wait_ge(d_q, c + 1)
                pe.wait_ge(d_ev, c)
                for f in range(FC):
                    n = P if f < FC - 1 else FL
                    dst = psum[4 + f // 4][:, 0:256].bitcast(bf16)
                    last = TR(dst[0:n, (f % 4) * P:(f % 4 + 1) * P], d_bf[:, f * P:f * P + n], ident_bf[:, :])
                last.then_inc(d_T, 1)

            turn_down(0)
            with pe.Fori(1, KC) as c:
                turn_down(c)
            pe.wait_ge(diag_ok, 3)
            pe.wait_ge(gu_ev, 2 * FC)
            pe.wait_ge(d_ev, KC)
            NCH = 2 * FC + KC
            for b in range(-(-NCH // 4)):
                n = min(4, NCH - 4 * b) * P
                MM(psum[b % 8][:, 0:n], ones, a0[:, b * 512:b * 512 + n], start=True, stop=True).then_inc(row_mm, 1)
            pe.wait_ge(row_ev, -(-NCH // 4))
            pe.wait_ge(w_eff_ready, 1)
            pe.wait_ge(cast_ready, 1)
            pe.wait_ge(ld["c2"], 64)

            def turn(dst, src, idn):
                for i in range(KC):
                    last = TR(dst[:, i * P:(i + 1) * P], src[:, i * P:(i + 1) * P], idn)
                return last

            def stage(s, k, it):
                B, w = bank[s], work[s]
                if k == "cond":
                    pe.wait_ge(xT_in.sem[s], xT_in.phase_done(it))
                    pe.wait_ge(hT.sem[s], hT.last(it))
                    for c in range(KC):
                        last = MM(B[0][:, :], xT[s][:, c, :], w_eff[:, c, :], start=c == 0, stop=c == KC - 1)
                    last.then_inc(y_mm.sem[s], 1)
                if k == "y_T":
                    pe.wait_ge(yq.sem[s], yq.done(it))
                    pe.wait_ge(h_step.sem[s], h_step.last(it))
                    turn(B[1], w, ident).then_inc(yqT_mm.sem[s], 1)
                if k == "qkv":
                    pe.wait_ge(yqT.sem[s], yqT.done(it))
                    for c in range(KC):
                        MM(B[0][:, :], work_bf[s][:, c, :], w_qkv[:, c, 0:D], start=c == 0, stop=c == KC - 1)
                    for c in range(KC):
                        last = MM(B[1][:, 0:2 * KV], work_bf[s][:, c, :], w_qkv[:, c, D:], start=c == 0, stop=c == KC - 1)
                    last.then_inc(qkv_mm.sem[s], qkv_mm.full)
                if k == "qk_T":
                    pe.wait_ge(qk.sem[s], qk.phase_done(it))
                    pe.wait_ge(v_ev.sem[s], v_ev.phase_done(it))
                    TR(B[1][:, 0:P], rope_c[s][:, D:QK], ident).then_inc(qkT_mm.sem[s], 1)
                    turn(B[0], rope_c[s], ident).then_inc(qkT_mm.sem[s], 1)
                if k == "scores":
                    pe.wait_ge(qT.sem[s], qT.done(it))
                    pe.wait_ge(kbd.sem[s], kbd.phase_done(it))
                    for r in range(R):
                        dst = B[r // 2][:, (r % 2) * 256:(r % 2 + 1) * 256]
                        for b in range(NB):
                            q0 = r * P + b * SEQ
                            last = MM(dst[b * SEQ:(b + 1) * SEQ, :], q_T[s][:, q0:q0 + SEQ],
                                      k_bd[s][:, b * 256:(b + 1) * 256], start=True, stop=True, tile_position=(0, b * SEQ))
                        if r % 2:
                            last.then_inc(s_mm.sem[s], 1)
                if k == "softmax":
                    pe.wait_ge(s_step.sem[s], s_step.done(it, 2))
                    for b in range(NB):
                        last = MM(B[0][:, b * P:(b + 1) * P], rep[:, b * P:(b + 1) * P], v_row[s], start=True, stop=True)
                    last.then_inc(v_mm.sem[s], 1)
                if k == "p_T":
                    pe.wait_ge(vbd.sem[s], vbd.done(it))
                    for j in range(2):
                        pe.wait_ge(s_exp.sem[s], s_exp.done(it, j + 1))
                        turn(B[j], prob[s][:, 512 * j:512 * (j + 1)], ident).then_inc(pT_mm.sem[s], 1)
                if k == "pv":
                    pe.wait_ge(pT.sem[s], pT.done(it))
                    pt = prob_T[s].rearrange("p (r e b q) -> p r e b q", r=R, e=2, b=NB)
                    for b in range(NB):
                        for e in range(2):
                            last = MM(B[0][64 * e:64 * (e + 1), b * P:(b + 1) * P],
                                      v_bd[s][:, (b * 2 + e) * 64:(b * 2 + e + 1) * 64], pt[:, :, e, b, :],
                                      start=True, stop=True, tile_position=(0, 64 * e))
                    last.then_inc(pv_mm.sem[s], 1)
                if k == "att":
                    pe.wait_ge(attT.sem[s], attT.phase_done(it))
                    turn(B[1], att_T[s], ident).then_inc(att_mm.sem[s], att_mm.full)
                if k == "att_T":
                    pe.wait_ge(aq.sem[s], aq.done(it))
                    turn(B[0], w, ident).then_inc(aqT_mm.sem[s], 1)
                if k == "o":
                    pe.wait_ge(aqT.sem[s], aqT.done(it))
                    for c in range(KC):
                        last = MM(B[1][:, :], work_bf[s][:, c, :], w_o[:, c, :], start=c == 0, stop=c == KC - 1)
                    last.then_inc(o_mm.sem[s], 1)
                if k == "x1_T":
                    pe.wait_ge(x1_ok.sem[s], x1_ok.phase_done(it))
                    turn(B[0], x1[s], ident).then_inc(x1T_mm.sem[s], x1T_mm.full)
                if k == "router":
                    pe.wait_ge(x1T_ok.sem[s], x1T_ok.phase_done(it))
                    for c in range(KC):
                        last = MM(B[1][:, 0:ER + E], x1T[s][:, c, :], w_c2[:, c, D:W2N], start=c == 0, stop=c == KC - 1)
                    last.then_inc(hl_mm.sem[s], 1)
                    for c in range(KC):
                        MM(B[0][:, :], x1T[s][:, c, :], w_c2[:, c, 0:D], start=c == 0, stop=False)
                if k == "hg_T":
                    pe.wait_ge(hg_ok.sem[s], hg_ok.phase_done(it))
                    TR(B[1][:, 2 * P:3 * P], hg[s], ident).then_inc(hgT_mm.sem[s], 1)
                if k == "lora":
                    pe.wait_ge(hgT.sem[s], hgT.done(it))
                    MM(B[0][:, :], hg_T[s], b_c2[:, :], start=False, stop=True).then_inc(c2_mm.sem[s], 1)
                if k == "z_T":
                    pe.wait_ge(zq.sem[s], zq.done(it))
                    turn(B[1], w, ident).then_inc(zT_mm.sem[s], zT_mm.full)
                for n, (lo, hi) in enumerate(FCH):
                    if k == f"gate_up{n}":
                        pe.wait_ge(zT.sem[s], zT.phase_done(it))
                        for j, wt in enumerate((w_gate, w_up)):
                            if n:
                                pe.wait_ge(gu_sc.sem[s], gu_sc.done(it, 2 * n - 1 + j))
                            for c in range(KC):
                                last = MM(B[j][:, 0:hi - lo], work_bf[s][:, c, :], wt[:, c, lo:hi],
                                          start=c == 0, stop=c == KC - 1)
                            last.then_inc(gu_mm.sem[s], gu_mm.full if n == 2 and j else 1)
                if k == "h_T":
                    pe.wait_ge(hq.sem[s], hq.done(it))
                    for f in range(FC):
                        n = P if f < FC - 1 else FL
                        if f == 8:
                            pe.wait_ge(hT.sem[s], hT.done(it, 1))
                        last = TR(B[f // 4 % 2][0:n, (f % 4) * P:(f % 4 + 1) * P], hid_g[s][:, f * P:f * P + n], ident)
                        if f % 4 == 3 or f == FC - 1:
                            last.then_inc(hT_mm.sem[s], 1)
                if k == "down":
                    for f in range(FC):
                        n = P if f < FC - 1 else FL
                        if f % 8 == 0:
                            pe.wait_ge(hT.sem[s], hT.phase_done(it) if f else hT.done(it, 2))
                        last = MM(B[1][:, :], hid_bf[s][0:n, f, :], w_down[0:n, f, :], start=f == 0, stop=f == FC - 1)
                    last.then_inc(d_mm.sem[s], d_mm.full)

            rounds(pe, stage)


_OUT = "out"


def _constants():
    import numpy as np
    P, SEQ, HD, G, R, NB, E = 128, 32, 16, 8, 4, 4, 8
    p = np.arange(P)
    ident = np.eye(P, dtype=np.float32)
    inv = (1.0 / np.float32(10000.0) ** (np.arange(0, HD, 2, dtype=np.float32) / HD)).astype(np.float32)
    ang = (np.arange(SEQ, dtype=np.float32)[:, None] * inv[None, :]).astype(np.float32).astype(np.float64)
    cos, sin = np.cos(ang), np.sin(ang)
    heads = G * R + G
    cos_t = np.tile(np.tile(np.concatenate([cos, cos], 1), (NB, 1)), (1, heads)).astype(np.float32)
    sin_t = np.tile(np.tile(np.concatenate([-sin, sin], 1), (NB, 1)), (1, heads)).astype(np.float32)
    mask_k = (p[:, None] // HD == np.arange(G)[None, :]).astype(np.float32)
    mask_v = (p[:, None] // SEQ == np.arange(G // 2)[None, :]).astype(np.float32)
    rep = np.concatenate([(p[:, None] == b * SEQ + p[None, :] % SEQ).astype(np.float32) for b in range(NB)], 1)
    expert = np.tile(np.arange(E, dtype=np.float32), (P, 1))
    ones = np.ones((P, P), np.float32)
    return np.ascontiguousarray(np.concatenate([ident, cos_t, sin_t, mask_k, mask_v, rep, expert, ones], 1))


def kernel(**inputs):
    import numpy as np
    import concourse.bacc as bacc
    from concourse import mybir
    from concourse.bass_utils import run_bass_kernel_spmd

    a = {k: np.asarray(v) for k, v in inputs.items()}
    P, D, G, R, HD = 128, 512, 8, 4, 16
    KC, NT = D // P, a["x"].shape[0] * a["x"].shape[1] // P
    F = a["L0_ffn_Wg"].shape[0]
    FC = -(-F // P)

    def by_chunk(w):
        return w.T.reshape(w.shape[1] // P, P, w.shape[0]).transpose(1, 0, 2)

    def padded_rows(w):
        return np.concatenate([w, w[:FC * P - F]]).reshape(FC, P, D)

    wq = a["L0_attn_Wq"].reshape(G, R, HD, D).transpose(1, 0, 2, 3).reshape(D, D)
    wo = a["L0_attn_Wo"].reshape(D, G, R, HD).transpose(0, 2, 1, 3).reshape(D, D)
    c2a, c2b = a["L0_cond2_A"], a["L0_cond2_B"]
    arrays = {
        "x_tok": a["x"].reshape(NT, P, D),
        "x_T": a["x"].reshape(NT, P, KC, P).transpose(0, 3, 2, 1),
        "ids": np.repeat(a["itok_B_0_7"], a["x"].shape[1]).reshape(NT, P).T,
        "codebook": a["condB_codebook"].reshape(1, -1),
        "w_cond": by_chunk(a["L0_cond_weight"]),
        "scale_log": a["L0_cond_scale_log"].reshape(D // P, P, KC).transpose(1, 2, 0).reshape(P, -1),
        "lora_A": a["L0_cond_lora_A"],
        "lora_B": a["L0_cond_lora_B"].T,
        "ln_g": a["L0_attn_ln_w"].reshape(1, D), "ln_b": a["L0_attn_ln_b"].reshape(1, D),
        "w_qkv": by_chunk(np.concatenate([wq, a["L0_attn_Wk"], a["L0_attn_Wv"]], 0)),
        "w_o": by_chunk(wo),
        "c2_w": by_chunk(a["L0_cond2_W"]),
        "c2_a": by_chunk(c2a.reshape(-1, D)),
        "c2_wr": by_chunk(a["L0_cond2_Wr"]),
        "c2_b": c2b.transpose(0, 2, 1).reshape(-1, D),
        "rms_g": a["L0_ffn_rmsnorm_weight"].reshape(1, D),
        "ffn_wg": padded_rows(a["L0_ffn_Wg"]), "ffn_wu": padded_rows(a["L0_ffn_Wu"]),
        "ffn_wd": a["L0_ffn_Wd"].reshape(KC, P, F),
        "consts": _constants(),
    }
    arrays = {k: np.ascontiguousarray(v) for k, v in arrays.items()}
    nc = bacc.Bacc("TRN2", target_bir_lowering=False, num_devices=1)
    d = {k: nc.dram_tensor("in_" + k, v.shape, mybir.dt.from_np(v.dtype), kind="ExternalInput").ap() for k, v in arrays.items()}
    d["out"] = nc.dram_tensor("out", (NT, P, D), mybir.dt.float32, kind="ExternalOutput").ap()
    adaln_attn_ffn_kernel(nc, d)
    r = run_bass_kernel_spmd(nc, [{"in_" + k: v for k, v in arrays.items()}], core_ids=[0])
    return r.results[0]["out"].reshape(a["x"].shape)
```

```python
import concourse.bass as bass
from concourse import mybir
from contextlib import ExitStack


def adaln_attn_ffn_kernel(nc, d):
    f32, bf16, i32, u8 = mybir.dt.float32, mybir.dt.bfloat16, mybir.dt.int32, mybir.dt.uint8
    ALU, ACT, AX = mybir.AluOpType, mybir.ActivationFunctionType, mybir.AxisListType

    NT, P, D = d["x_tok"].shape
    KC = D // P
    SLOTS = 4
    ITERS = NT // SLOTS
    SEQ, HD, G, R = 32, 16, 8, 4
    NB = P // SEQ
    H = G * R
    KV = G * HD
    QK = D + KV
    HALF = G // 2
    RANK = d["lora_A"].shape[0]
    E, LR = d["c2_wr"].shape[2], d["c2_b"].shape[0] // d["c2_wr"].shape[2]
    ER = E * LR
    W2N = D + ER + E
    F = d["ffn_wd"].shape[2]
    FC = -(-F // P)
    FL = F - (FC - 1) * P
    NCB = d["codebook"].shape[1]
    E_HI = 2.7182817459106445
    E_REST = 3.0367860004432146e-08
    MAGIC = 12582912.0
    FCH = [(n, min(n + 512, F)) for n in range(0, F, 512)]
    STAGES = ("cond", "norm", "norm_round", "y_T", "qkv", "rope", "qk_T", "scores", "softmax", "softmax_sum",
              "p_T", "pv", "att", "att_T", "o", "x1_T", "router", "gates", "hg_T", "lora", "rms", "z_T",
              "gate_up0", "gate_up1", "gate_up2", "hidden0", "hidden1", "hidden2", "h_round", "h_T", "down", "out")

    ctx = ExitStack()
    with ctx:
        def sb(name, shape, dt=f32):
            return ctx.enter_context(nc.sbuf_tensor(name, shape, dt))

        def sem(name):
            return ctx.enter_context(nc.semaphore(name))

        def sems(name):
            return [sem(f"{name}{s}") for s in range(SLOTS)]

        consts = sb("consts", [P, d["consts"].shape[1]])
        at = [0]

        def const(n):
            at[0] += n
            return consts[:, at[0] - n:at[0]]

        ident, cos_t, sin_t = const(P), const(QK), const(QK)
        mask_k, mask_v = const(G), const(HALF)
        rep = const(NB * P)
        expert_no, ones = const(E), const(P)
        ident_bf = sb("ident_bf", [P, P], bf16)
        neg_half = sb("neg_half", [P, 1])
        euler = sb("euler", [P, KC * KC])

        w_eff = sb("w_eff", [P, KC, D])
        w_qkv = sb("w_qkv", [P, KC, D + 2 * KV], bf16)
        w_o = sb("w_o", [P, KC, D], bf16)
        w_c2 = sb("w_c2", [P, KC, W2N])
        b_c2 = sb("b_c2", [ER, D])
        w_gate = sb("w_gate", [P, KC, F], bf16)
        w_up = sb("w_up", [P, KC, F], bf16)
        w_down = sb("w_down", [P, FC, D], bf16)
        ln_g, ln_b, rms_g = sb("ln_g", [P, D]), sb("ln_b", [P, D]), sb("rms_g", [P, D])
        gate_s, up_s, down_s = sb("gate_s", [P, F]), sb("up_s", [P, F]), sb("down_s", [P, D])
        wmean = sb("wmean", [P, 4])
        wrecip = sb("wrecip", [P, 4])
        wabs = sb("wabs", [P, 4])
        lang = sb("lang", [P, NT, E])
        col_s = sb("col_s", [P, 2 * FC + KC])

        A_WORDS = 4480
        area_all = sb("area", [P, SLOTS * A_WORDS])
        area = [area_all[:, s * A_WORDS:(s + 1) * A_WORDS] for s in range(SLOTS)]
        xT = [sb(f"xT{s}", [P, KC, P]) for s in range(SLOTS)]
        xt = [sb(f"xt{s}", [P, D]) for s in range(SLOTS)]
        work = [sb(f"work{s}", [P, D]) for s in range(SLOTS)]
        work_bf = [sb(f"work_bf{s}", [P, KC, P], bf16) for s in range(SLOTS)]
        x1 = [sb(f"x1_{s}", [P, D]) for s in range(SLOTS)]
        small = [sb(f"small{s}", [P, 192]) for s in range(SLOTS)]

        def carve(t, sizes):
            out, o = [], 0
            for n in sizes:
                out.append(t[:, o:o + n])
                o += n
            return out

        att_sizes = [QK, QK, KV, D, NB * G * SEQ, NB * 2 * 64, H * SEQ]
        rope_c, rope_s, v_row, q_T, k_bd, v_bd, prob = zip(*[carve(a, att_sizes) for a in area])
        prob_T = [a[:, QK:QK + H * SEQ] for a in area]
        att_T = [v[:, 0:D] for v in rope_c]
        k_T = [v[:, 0:P] for v in rope_s]
        v_4 = q_T
        x1T = [v[:, 0:D].rearrange("p (c n) -> p c n", c=KC) for v in prob]
        hg, hg_T, squares = zip(*[carve(a, [ER, P, D]) for a in area])
        hid_g, hid_u, hid_t = zip(*[carve(a, [F, F, F]) for a in area])
        hid_bf = [a[:, 2 * F + F % 2:2 * F + F % 2 + FC * P // 2].bitcast(bf16).rearrange("p (f n) -> p f n", f=FC) for a in area]
        (st, mv, rstd, q_scale, deq, v_scale, smax, rsum, logit, top8, keep, ew, sq,
         steps) = zip(*[carve(t, [6, 2, 2, 4, 2, 1, H, H, E, 8, E, E, 4, 20]) for t in small])
        topi = [sb(f"topi{s}", [P, 8], mybir.dt.uint32) for s in range(SLOTS)]

        psum = [ctx.enter_context(nc.psum_tensor(f"bank{b}", [P, 512], f32)) for b in range(2 * SLOTS)]
        bank = [psum[2 * s:2 * s + 2] for s in range(SLOTS)]

        ld = {n: sem("ld_" + n) for n in ("consts", "lora", "w", "sl", "cb", "qkv", "o", "c2", "vec")}
        delta_mm, scale_exp, diag_ok = sem("delta_mm"), sem("scale_exp"), sem("diag_ok")
        bc_mm = sem("bc_mm")
        prep = sem("prep")
        near_col, near_row = sem("near_col"), sem("near_row")
        w_eff_ready = sem("w_eff_ready")
        abs_sum, abs_tot = sem("abs_sum"), sem("abs_tot")
        cast_ready, ident_ok = sem("cast_ready"), sem("ident_ok")
        ld_f, ld_d = [sem(f"ld_f{b}") for b in range(3)], [sem(f"ld_d{c}") for c in range(KC)]
        row_step, col_ok, f_scale, f_round, f_bf, f_T, f_ev = (
            sem("row_step"), sem("col_ok"), sem("f_scale"), sem("f_round"), sem("f_bf"), sem("f_T"), sem("f_ev"))
        rows_diag, row_mm, row_ev = sem("rows_diag"), sem("row_mm"), sem("row_ev")
        search = sem("search")
        c_ready = sem("c_ready")

        TICKS = 16

        class Step:
            def __init__(self, sem, before, n):
                self.sem, self.before, self.n = sem, before, n
                self.full = TICKS - before - n + 1

            def done(self, it, j=None):
                j = self.before + (self.n if j is None else j)
                return it * TICKS + j

            def phase_done(self, it):
                return it * TICKS + TICKS

            def last(self, it):
                return it * TICKS

        def phase(name, *ns):
            group, out, before = sems(name), [], 0
            for n in ns:
                out.append(Step(group, before, n))
                before += n
            return out if len(out) > 1 else out[0]

        xT_in, x_in, out_st = phase("xT_in", 16), phase("x_in", 16), phase("out_st", 16)
        y_mm, yqT_mm, qkv_mm = phase("cond_pe", 1, 1, 1)
        qkT_mm, s_mm, v_mm, pT_mm, pv_mm, att_mm = phase("att_pe", 2, 2, 1, 2, 1, 1)
        aqT_mm, o_mm, x1T_mm = phase("oproj_pe", 1, 1, 1)
        hl_mm, hgT_mm, c2_mm, zT_mm = phase("lora_pe", 1, 1, 1, 1)
        gu_mm = phase("gate_up_pe", 6)
        hT_mm, d_mm = phase("down_pe", 3, 1)
        yq, yqT, v_ev = phase("cond_act", 1, 1, 1)
        k_ev, qT, s_exp, v4_ev, pT, attT = phase("att_act", 1, 1, 2, 1, 2, 1)
        aq, aqT, o_ev, x1T_ok = phase("oproj_act", 1, 1, 1, 1)
        l_exp, hgT, z_sq, zq, zT = phase("lora_act", 1, 1, 1, 1, 1)
        gu_tanh, hq, hT = phase("ffn_act", 3, 1, 3)
        y_step = phase("y_step", 8)
        rope_step = phase("rope_step", 2)
        s_step, s_sum = phase("softmax_dve", 4, 2)
        a_step = phase("a_step", 5)
        l_step, hg_ok = phase("router_dve", 10, 1)
        z_step = phase("z_step", 8)
        gu_sc, gu_h = phase("gate_up_dve", 6, 3)
        h_step = phase("h_step", 10)
        y_rstd, z_rstd = phase("rstd_pool", 1, 1)
        qk, kbd, vbd, x1_ok = phase("att_pool", 1, 1, 1, 1)
        hid_ok, out_ok = phase("ffn_pool", 3, 1)

        block = ctx.enter_context(nc.Block())

        TURNS = ("2112301231202031203103021301131223120210320130323012031201323120"
                 "2132231002332132302123211023031023110301230311203210300130302010")
        ENTER = (15, 9, 1, 7)
        ORDER, nxt = [], list(ENTER)
        for turn_of in map(int, TURNS):
            ORDER.append((turn_of, STAGES[nxt[turn_of] % len(STAGES)], nxt[turn_of] // len(STAGES)))
            nxt[turn_of] += 1

        def rounds(e, stage):
            for i in (-1, 0):
                for s, k, ahead in ORDER:
                    if i + ahead >= 0:
                        stage(s, k, i + ahead)
            with e.Fori(1, ITERS - 1) as i:
                for s, k, ahead in ORDER:
                    stage(s, k, i + ahead)
            for s, k, ahead in ORDER:
                if not ahead:
                    stage(s, k, ITERS - 1)

        def cols(ap, n):
            return ap.unsqueeze(2).to_broadcast([ap.shape[0], ap.shape[1], n])

        def rows(ap, n):
            return ap.unsqueeze(1).to_broadcast([ap.shape[0], n, ap.shape[1]])

        KD = KC * D
        delta, wg, diag, norm, quant, att_w = carve(area_all, [KD] * 5 + [KC * (2 * D + 2 * KV)])
        qkv_w, o_w = att_w[:, 0:KC * (D + 2 * KV)], att_w[:, KC * (D + 2 * KV):]
        BUFS = 3
        rows_end = 5 * KD + KC * (2 * D + 2 * KV)
        gu_f = [area_all[:, rows_end + b * 2 * D:rows_end + (b + 1) * 2 * D] for b in range(2)] + [quant[:, 0:2 * D]]
        gu_b = [x1[b][:, :].bitcast(bf16) for b in range(BUFS)]
        F2 = F + F % 2
        d_f = [t[:, b * F2:b * F2 + F] for t in (area_all, att_w) for b in range(2)]
        d_b = [area_all[:, 2 * F2 + b * F2 // 2:2 * F2 + (b + 1) * F2 // 2].bitcast(bf16)[:, 0:F] for b in range(2)]
        NCH = 2 * FC + KC
        scale_diag = area_all[:, 4 * KD - NCH * P:4 * KD]
        f_col, f_rec = [[sb(f"f_{w}{b}", [P, 2]) for b in range(BUFS)] for w in ("col", "rec")]
        pool_tick = sb("pool_tick", [P, BUFS])
        loraA = xT[0][0:RANK].rearrange("p a b -> p (a b)")
        loraB = xT[1][0:RANK].rearrange("p a b -> p (a b)")
        sl = sb("sl", [P, 2 * KC * KC])
        cbk = sb("cbk", [P, NCB])
        thr = sb("thr", [P, NCB + 1])
        cbx = sb("cbx", [P, 8])
        cell = sb("cell", [P, 8])
        flag = sb("flag", [1, 1], i32)
        picked = w_gate[:, 0, :]
        row_parts = [(gate_s, lo, hi) for lo, hi in FCH] + [(up_s, lo, hi) for lo, hi in FCH] + [(down_s, 0, D)]
        idf = sb("idf", [P, NT])
        ids = sb("ids", [P, NT], i32)

        @block.sync
        def _(sp):
            sp.dma_start(consts[:, :], d["consts"]).then_inc(ld["consts"], 16)
            sp.dma_start(loraA, d["lora_A"]).then_inc(ld["lora"], 16)
            sp.dma_start(loraB, d["lora_B"]).then_inc(ld["lora"], 16)
            sp.dma_start(wg, d["w_cond"].rearrange("p g o -> p (g o)")).then_inc(ld["w"], 16)
            sp.dma_start(qkv_w, d["w_qkv"].rearrange("p c o -> p (c o)")).then_inc(ld["qkv"], 16)
            sp.dma_start(o_w, d["w_o"].rearrange("p c o -> p (c o)")).then_inc(ld["o"], 16)

            def load_rows(i, b, n):
                c = BUFS * i + b
                if not isinstance(i, int) or i:
                    sp.wait_ge(f_bf, c - 2)
                for j, name in enumerate(("ffn_wg", "ffn_wu")):
                    sp.dma_start(gu_f[b][0:n, j * D:(j + 1) * D],
                                 d[name][bass.ds(c, 1), 0:n, :].rearrange("a p n -> (a p) n")).then_inc(ld_f[b], 16)

            load_rows(0, 0, P)
            load_rows(0, 1, P)
            sp.dma_start(w_c2[:, :, 0:D], d["c2_w"]).then_inc(ld["c2"], 16)
            sp.dma_start(w_c2[:, :, D:D + ER], d["c2_a"]).then_inc(ld["c2"], 16)
            with nc.allow_non_contiguous_dma(reason="router columns, once"):
                sp.dma_start(w_c2[:, :, D + ER:W2N], d["c2_wr"]).then_inc(ld["c2"], 16)
            sp.dma_start(b_c2[:, :], d["c2_b"]).then_inc(ld["c2"], 16)
            sp.wait_ge(w_eff_ready, 1)
            load_rows(0, 2, P)
            with sp.Fori(1, FC // BUFS) as i:
                for b in range(BUFS):
                    load_rows(i, b, P)
            load_rows(FC // BUFS, 0, P)
            load_rows(FC // BUFS, 1, FL)
            sp.wait_ge(cast_ready, 1)
            for c in range(KC):
                sp.dma_start(d_f[c], d["ffn_wd"][c]).then_inc(ld_d[c], 16)

            def stage(s, k, it):
                t = it * SLOTS + s
                if k == "cond":
                    sp.wait_ge(y_mm.sem[s], y_mm.last(it))
                    sp.dma_start(xT[s][:, :, :], d["x_T"][bass.ds(t, 1)].rearrange("a p c n -> (a p) c n")).then_inc(xT_in.sem[s], 16)
                    sp.wait_ge(x1_ok.sem[s], x1_ok.last(it))
                    sp.dma_start(xt[s][:, :], d["x_tok"][bass.ds(t, 1)].rearrange("a p n -> (a p) n")).then_inc(x_in.sem[s], 16)
                if k == "out":
                    sp.wait_ge(out_ok.sem[s], out_ok.phase_done(it))
                    sp.dma_start(d["out"][bass.ds(t, 1)].rearrange("a p n -> (a p) n"), work[s][:, :]).then_inc(out_st.sem[s], 16)

            sp.wait_ge(delta_mm, 1)
            rounds(sp, stage)
            for s in range(SLOTS):
                sp.wait_ge(out_st.sem[s], out_st.phase_done(ITERS - 1))

        @block.gpsimd
        def _(pool):
            pool.dma_start(sl[:, 0:KC * KC], d["scale_log"]).then_inc(ld["sl"], 16)
            pool.dma_start(cbk[:, :], d["codebook"].to_broadcast([P, NCB])).then_inc(ld["cb"], 16)
            for v, n in ((ln_g, "ln_g"), (ln_b, "ln_b"), (rms_g, "rms_g")):
                pool.dma_start(v[:, :], d[n].to_broadcast([P, D])).then_inc(ld["vec"], 16)
            pool.dma_start(ids[:, :], d["ids"]).then_inc(ld["vec"], 16)
            nc.gpsimd.memset(neg_half[:, :], -0.5)
            nc.gpsimd.memset(euler[:, :], E_HI).then_inc(c_ready, 1)
            pool.wait_ge(c_ready, 1)
            pool.wait_ge(ld["sl"], 16)
            nc.gpsimd.tensor_tensor(sl[:, KC * KC:2 * KC * KC], euler[:, :], sl[:, 0:KC * KC], ALU.pow).then_inc(scale_exp, 1)

            def to_bf(c, b, dst, src, back=BUFS):
                pool.wait_ge(f_round, c + 1)
                if not isinstance(c, int) or c >= back:
                    pool.wait_ge(f_T, c - back + 1)
                if not isinstance(c, int):
                    nc.gpsimd.tensor_tensor(pool_tick[:, b:b + 1], neg_half[:, :], neg_half[:, :], ALU.add)
                nc.gpsimd.tensor_scalar(dst, src, 1.0, -MAGIC, ALU.mult, ALU.add).then_inc(f_bf, 1)

            for b in range(BUFS):
                to_bf(b, b, gu_b[b], gu_f[b])
            with pool.Fori(1, FC // BUFS) as i:
                for b in range(BUFS):
                    to_bf(BUFS * i + b, b, gu_b[b], gu_f[b])
            to_bf(FC - 2, 0, gu_b[0], gu_f[0])
            to_bf(FC - 1, 1, gu_b[1][0:FL, :], gu_f[1][0:FL, :])
            for c in range(KC):
                to_bf(FC + c, c % 2, d_b[c % 2], d_f[c], 2)

            def stage(s, k, it):
                if k == "norm":
                    pool.wait_ge(y_step.sem[s], y_step.done(it, 3))
                    nc.gpsimd.tensor_tensor(rstd[s][:, 0:1], steps[s][:, 0:1], neg_half[:, :], ALU.pow).then_inc(y_rstd.sem[s], 1)
                if k == "rope":
                    pool.wait_ge(rope_step.sem[s], rope_step.phase_done(it))
                    nc.gpsimd.tensor_tensor(rope_c[s], rope_c[s], rope_s[s], ALU.add).then_inc(qk.sem[s], 1)
                if k == "qk_T":
                    pool.wait_ge(k_ev.sem[s], k_ev.done(it))
                    nc.gpsimd.tensor_tensor(
                        k_bd[s].rearrange("p (b g q) -> p b g q", b=NB, g=G),
                        k_T[s].rearrange("p (b q) -> p b q", b=NB).unsqueeze(2).to_broadcast([P, NB, G, SEQ]),
                        mask_k.unsqueeze(1).unsqueeze(3).to_broadcast([P, NB, G, SEQ]), ALU.mult).then_inc(kbd.sem[s], 1)
                if k == "softmax_sum":
                    pool.wait_ge(v4_ev.sem[s], v4_ev.done(it))
                    nc.gpsimd.tensor_tensor(
                        v_bd[s].rearrange("p (e g j) -> p e g j", e=NB * 2, g=HALF),
                        v_4[s].rearrange("p (e g j) -> p e g j", e=NB * 2, g=HALF),
                        mask_v.unsqueeze(1).unsqueeze(3).to_broadcast([P, NB * 2, HALF, HD]), ALU.mult).then_inc(vbd.sem[s], 1)
                if k == "o":
                    pool.wait_ge(o_ev.sem[s], o_ev.done(it))
                    pool.wait_ge(x_in.sem[s], x_in.phase_done(it))
                    nc.gpsimd.tensor_tensor(x1[s][:, :], x1[s][:, :], xt[s][:, :], ALU.add).then_inc(x1_ok.sem[s], x1_ok.full)
                if k == "lora":
                    pool.wait_ge(z_step.sem[s], z_step.done(it, 1))
                    nc.gpsimd.tensor_tensor(rstd[s][:, 1:2], steps[s][:, 8:9], neg_half[:, :], ALU.pow).then_inc(z_rstd.sem[s], z_rstd.full)
                for n, (lo, hi) in enumerate(FCH):
                    if k == f"hidden{n}":
                        pool.wait_ge(gu_h.sem[s], gu_h.done(it, n + 1) if n < 2 else gu_h.phase_done(it))
                        nc.gpsimd.tensor_tensor(hid_u[s][:, lo:hi], hid_u[s][:, lo:hi], hid_t[s][:, lo:hi], ALU.mult).then_inc(hid_ok.sem[s], 1)
                if k == "out":
                    pool.wait_ge(h_step.sem[s], h_step.phase_done(it))
                    nc.gpsimd.tensor_tensor(work[s][:, :], work[s][:, :], x1[s][:, :], ALU.add).then_inc(out_ok.sem[s], out_ok.full)

            rounds(pool, stage)

        @block.scalar
        def _(act):
            A = nc.scalar.activation
            act.wait_ge(ld["qkv"], 16)
            wq3 = qkv_w.rearrange("p (c o) -> p c o", c=KC)
            spare = w_up.rearrange("p c o -> p (c o)").bitcast(f32)[:, 0:KC * D]
            junk = spare[:, 0:KC * KV].rearrange("p (c o) -> p c o", c=KC)
            A(spare.rearrange("p (c o) -> p c o", c=KC), wq3[:, :, 0:D], ACT.Abs, accum_out=wabs[:, 0:1]).then_inc(abs_sum, 1)
            act.wait_ge(abs_sum, 1)
            A(junk, wq3[:, :, D:D + KV], ACT.Abs, accum_out=wabs[:, 1:2]).then_inc(abs_sum, 1)
            act.wait_ge(abs_sum, 2)
            A(junk, wq3[:, :, D + KV:D + 2 * KV], ACT.Abs, accum_out=wabs[:, 2:3]).then_inc(abs_sum, 1)
            act.wait_ge(ld["o"], 16)
            act.wait_ge(abs_sum, 3)
            A(spare, o_w, ACT.Abs, accum_out=wabs[:, 3:4]).then_inc(abs_sum, 1)

            def round_gu(c, b, n):
                act.wait_ge(f_scale, c + 1)
                for j in range(2):
                    r = gu_f[b][0:n, j * D:(j + 1) * D]
                    last = A(r, r, ACT.Copy, scale=f_rec[b][0:n, j:j + 1], bias=MAGIC)
                last.then_inc(f_round, 1)

            def out_gu(c, b, n):
                act.wait_ge(f_T, c + 1)
                for j, w in enumerate((w_gate, w_up)):
                    src = psum[2 * b + j][:, 0:256].bitcast(bf16).rearrange("p (k n) -> p k n", k=KC)[:, :, 0:n]
                    last = A(w[:, :, bass.ds(c * P, n)], src, ACT.Copy)
                last.then_inc(f_ev, 1)

            round_gu(0, 0, P)
            act.wait_ge(abs_sum, 4)
            for b in range(1, BUFS):
                round_gu(b, b, P)
                out_gu(b - 1, b - 1, P)
            with act.Fori(1, FC // BUFS) as i:
                for b in range(BUFS):
                    round_gu(BUFS * i + b, b, P)
                    out_gu(BUFS * i + (b - 1), (b - 1) % BUFS, P)
            round_gu(FC - 2, 0, P)
            out_gu(FC - 3, BUFS - 1, P)
            round_gu(FC - 1, 1, FL)
            out_gu(FC - 2, 0, P)

            def out_down(c):
                act.wait_ge(f_T, FC + c + 1)
                for q in range(3):
                    m = min(4, FC - 4 * q)
                    full = m - 1 if 4 * q + m == FC else m
                    src = psum[4 * (c % 2) + q][:, 0:256].bitcast(bf16).rearrange("p (k n) -> p k n", k=4)
                    last = A(w_down[:, 4 * q:4 * q + full, c * P:(c + 1) * P], src[:, 0:full, :], ACT.Copy)
                    if full < m:
                        last = A(w_down[0:FL, FC - 1, c * P:(c + 1) * P], src[0:FL, full, :], ACT.Copy)
                last.then_inc(f_ev, 1)

            for c in range(KC):
                act.wait_ge(f_scale, FC + c + 1)
                A(d_f[c], d_f[c], ACT.Copy, scale=f_rec[(FC + c) % BUFS][:, 0:1], bias=MAGIC).then_inc(f_round, 1)
                if c:
                    out_down(c - 1)
                else:
                    out_gu(FC - 1, 1, FL)
            out_down(KC - 1)

            def stage(s, k, it):
                B, w = bank[s], work[s]
                wb = work_bf[s].rearrange("p c n -> p (c n)")
                if k == "norm_round":
                    act.wait_ge(y_step.sem[s], y_step.phase_done(it))
                    A(w[:, :], w[:, :], ACT.Copy, scale=q_scale[s][:, 0:1], bias=MAGIC).then_inc(yq.sem[s], 1)
                if k == "y_T":
                    act.wait_ge(yqT_mm.sem[s], yqT_mm.done(it))
                    A(wb, B[1][:, :], ACT.Copy, bias=-MAGIC).then_inc(yqT.sem[s], 1)
                if k == "rope":
                    act.wait_ge(rope_step.sem[s], rope_step.phase_done(it))
                    A(v_row[s], B[1][:, KV:2 * KV], ACT.Copy, scale=v_scale[s]).then_inc(v_ev.sem[s], v_ev.full)
                if k == "qk_T":
                    act.wait_ge(qkT_mm.sem[s], qkT_mm.done(it, 1))
                    A(k_T[s], B[1][:, 0:P], ACT.Copy).then_inc(k_ev.sem[s], 1)
                    act.wait_ge(qkT_mm.sem[s], qkT_mm.done(it))
                    A(q_T[s], B[0][:, :], ACT.Copy).then_inc(qT.sem[s], 1)
                if k == "softmax":
                    for j in range(2):
                        act.wait_ge(s_step.sem[s], s_step.done(it, 2 * j + 2))
                        p = prob[s][:, 512 * j:512 * (j + 1)]
                        A(p, p, ACT.Exp, scale=HD ** -0.5).then_inc(s_exp.sem[s], 1)
                if k == "softmax_sum":
                    act.wait_ge(v_mm.sem[s], v_mm.done(it))
                    A(v_4[s], B[0][:, :], ACT.Copy).then_inc(v4_ev.sem[s], 1)
                if k == "p_T":
                    act.wait_ge(vbd.sem[s], vbd.done(it))
                    for j in range(2):
                        act.wait_ge(pT_mm.sem[s], pT_mm.done(it, j + 1))
                        A(prob_T[s][:, 512 * j:512 * (j + 1)], B[j][:, :], ACT.Copy).then_inc(pT.sem[s], 1)
                if k == "pv":
                    act.wait_ge(pv_mm.sem[s], pv_mm.done(it))
                    A(att_T[s].rearrange("p (r b q) -> p b r q", r=R, b=NB),
                      B[0].rearrange("p (b r q) -> p b r q", b=NB, r=R), ACT.Copy).then_inc(attT.sem[s], attT.full)
                if k == "att":
                    act.wait_ge(a_step.sem[s], a_step.phase_done(it))
                    A(w[:, :], w[:, :], ACT.Copy, scale=q_scale[s][:, 1:2], bias=MAGIC).then_inc(aq.sem[s], 1)
                if k == "att_T":
                    act.wait_ge(aqT_mm.sem[s], aqT_mm.done(it))
                    A(wb, B[0][:, :], ACT.Copy, bias=-MAGIC).then_inc(aqT.sem[s], 1)
                if k == "o":
                    act.wait_ge(o_mm.sem[s], o_mm.done(it))
                    act.wait_ge(a_step.sem[s], a_step.done(it, 4))
                    A(x1[s][:, :], B[1][:, :], ACT.Copy, scale=deq[s][:, 0:1]).then_inc(o_ev.sem[s], 1)
                if k == "x1_T":
                    act.wait_ge(x1T_mm.sem[s], x1T_mm.phase_done(it))
                    A(prob[s][:, 0:D], B[0][:, :], ACT.Copy).then_inc(x1T_ok.sem[s], x1T_ok.full)
                if k == "router":
                    act.wait_ge(l_step.sem[s], l_step.done(it, 3))
                    A(ew[s], logit[s], ACT.Exp, bias=steps[s][:, 4:5]).then_inc(l_exp.sem[s], 1)
                if k == "hg_T":
                    act.wait_ge(hgT_mm.sem[s], hgT_mm.done(it))
                    A(hg_T[s], B[1][:, 2 * P:3 * P], ACT.Copy).then_inc(hgT.sem[s], 1)
                if k == "lora":
                    act.wait_ge(c2_mm.sem[s], c2_mm.done(it))
                    A(squares[s], B[0][:, :], ACT.Square, accum_out=sq[s][:, 0:1]).then_inc(z_sq.sem[s], 1)
                if k == "rms":
                    act.wait_ge(z_step.sem[s], z_step.phase_done(it))
                    A(w[:, :], w[:, :], ACT.Copy, scale=q_scale[s][:, 2:3], bias=MAGIC).then_inc(zq.sem[s], 1)
                if k == "z_T":
                    act.wait_ge(zT_mm.sem[s], zT_mm.phase_done(it))
                    A(wb, B[1][:, :], ACT.Copy, bias=-MAGIC).then_inc(zT.sem[s], zT.full)
                for n, (lo, hi) in enumerate(FCH):
                    if k == f"gate_up{n}":
                        act.wait_ge(gu_sc.sem[s], gu_sc.done(it, 2 * n + 1))
                        A(hid_t[s][:, lo:hi], hid_g[s][:, lo:hi], ACT.Tanh, scale=deq[s][:, 1:2]).then_inc(gu_tanh.sem[s], 1)
                if k == "h_round":
                    act.wait_ge(h_step.sem[s], h_step.done(it, 9))
                    A(hid_g[s], hid_u[s], ACT.Copy, scale=q_scale[s][:, 3:4], bias=MAGIC).then_inc(hq.sem[s], 1)
                if k == "h_T":
                    for b in range(3):
                        m = min(4, FC - 4 * b)
                        full = m - 1 if 4 * b + m == FC else m
                        act.wait_ge(hT_mm.sem[s], hT_mm.done(it, b + 1))
                        src = B[b % 2].rearrange("p (k n) -> p k n", k=4)
                        ev = A(hid_bf[s][:, 4 * b:4 * b + full, :], src[:, 0:full, :], ACT.Copy, bias=-MAGIC)
                        if full < m:
                            ev = A(hid_bf[s][0:FL, FC - 1, :], src[0:FL, full, :], ACT.Copy, bias=-MAGIC)
                        ev.then_inc(hT.sem[s], hT.full if b == 2 else 1)

            rounds(act, stage)

        @block.vector
        def _(dve):
            V = nc.vector
            n_prep = [0]

            def step(ins):
                n_prep[0] += 1
                ins.then_inc(prep, 1)
                dve.wait_ge(prep, n_prep[0])

            dve.wait_ge(ld["consts"], 16)
            dve.wait_ge(scale_exp, 1)
            step(V.tensor_scalar(sl[:, 0:KC * KC], sl[:, 0:KC * KC], E_REST, 1.0, ALU.mult, ALU.add))
            step(V.tensor_tensor(sl[:, 0:KC * KC], sl[:, 0:KC * KC], sl[:, KC * KC:2 * KC * KC], ALU.mult))
            step(V.reciprocal(sl[:, KC * KC:2 * KC * KC], sl[:, 0:KC * KC]))
            diag3 = diag.rearrange("p (j n) -> p j n", n=P)
            V.tensor_tensor(diag3, rows(ident, KC * KC), cols(sl[:, KC * KC:2 * KC * KC], P), ALU.mult).then_inc(diag_ok, 1)
            dve.wait_ge(ld["cb"], 16)
            step(V.tensor_reduce(cbx[:, 0:1], cbk[:, :], AX.X, ALU.max, apply_absolute_value=True))
            step(V.tensor_scalar(cbx[:, 1:2], cbx[:, 0:1], 1e-8, None, ALU.max))
            step(V.reciprocal(cbx[:, 2:3], cbx[:, 1:2]))
            step(V.tensor_scalar(cbk[:, :], cbk[:, :], cbx[:, 2:3], None, ALU.mult))
            dve.wait_ge(delta_mm, 1)
            for c in range(KC):
                last = V.tensor_scalar(delta[:, c * D:(c + 1) * D], psum[c][:, :], 0.5, None, ALU.mult)
            step(last)
            dve.wait_ge(ld["w"], 16)
            step(V.tensor_tensor(wg, wg, delta, ALU.add))
            dve.wait_ge(bc_mm, 1)
            for c in range(KC):
                last = V.tensor_tensor(norm[:, c * D:(c + 1) * D], wg[:, c * D:(c + 1) * D], psum[4 + c][:, :], ALU.mult)
            step(last)
            V.tensor_tensor(diag3, rows(ident, KC * KC), cols(sl[:, 0:KC * KC], P), ALU.mult).then_inc(diag_ok, 1)
            step(V.tensor_reduce(cell[:, 0:1], norm, AX.X, ALU.min, apply_absolute_value=True))
            step(V.tensor_scalar(quant, norm, 0.0, cbk[:, NCB - 1:NCB], ALU.is_gt, ALU.mult))
            step(V.tensor_scalar(wg, norm, 0.0, cbk[:, 0:1], ALU.is_le, ALU.mult))
            step(V.tensor_tensor(quant, quant, wg, ALU.add))
            nc.vector.tensor_copy(cell[:, 1:2], cell[:, 0:1]).then_inc(near_col, 1)
            dve.wait_ge(near_row, 1)
            step(V.tensor_reduce(cell[0:1, 2:3], psum[0][0:1, 0:P], AX.X, ALU.min))
            step(V.tensor_scalar(flag[:, :], cell[0:1, 2:3], 1.001, None, ALU.is_le))
            near = dve.value_load(flag[0:1, 0:1], min_val=0, max_val=1)
            with dve.If(near == 1):
                m = [0]

                def found(ins):
                    m[0] += 1
                    ins.then_inc(search, 1)
                    dve.wait_ge(search, m[0])

                found(V.memset(thr[:, :], 3e38))
                found(V.memset(thr[:, 0:1], -3e38))
                found(V.tensor_tensor(thr[:, 1:NCB], cbk[:, 0:NCB - 1], cbk[:, 1:NCB], ALU.add))
                found(V.tensor_scalar(thr[:, 1:NCB], thr[:, 1:NCB], 0.5, None, ALU.mult))
                h = NCB // 2
                while h:
                    node = thr[:, h:NCB:2 * h]
                    found(V.tensor_tensor(node, node, thr[:, 0:NCB:2 * h], ALU.max))
                    found(V.tensor_tensor(node, node, thr[:, 2 * h:NCB + 1:2 * h], ALU.min))
                    h //= 2
                found(V.tensor_copy(quant, cbk[:, 0:1].to_broadcast([P, KC * D])))
                base, per = m[0], 4
                mask = picked.bitcast(u8)[:, 0:KC * D]
                with dve.Fori(0, NCB - 1) as j:
                    V.tensor_copy(cbx[:, 4:5], thr[:, bass.ds(j + 1, 1)]).then_inc(search, 1)
                    V.tensor_copy(cbx[:, 5:6], cbk[:, bass.ds(j + 1, 1)]).then_inc(search, 1)
                    dve.wait_ge(search, j * per + (base + 2))
                    V.tensor_scalar(mask, norm, cbx[:, 4:5], None, ALU.is_gt).then_inc(search, 1)
                    dve.wait_ge(search, j * per + (base + 3))
                    V.memset(cell[:, 3:4], 0.0)
                    V.copy_predicated(quant, mask, cbx[:, 5:6].to_broadcast([P, KC * D])).then_inc(search, 1)
                    dve.wait_ge(search, j * per + (base + 4))
            step(V.tensor_tensor(quant, quant, norm, ALU.subtract))
            step(V.tensor_tensor(quant, quant, norm, ALU.add))
            dve.wait_ge(bc_mm, 2)
            for c in range(KC):
                last = V.tensor_tensor(quant[:, c * D:(c + 1) * D], quant[:, c * D:(c + 1) * D], psum[4 + c][:, :], ALU.mult)
            step(last)
            V.tensor_tensor(w_eff.rearrange("p c o -> p (c o)"), quant, delta, ALU.add).then_inc(w_eff_ready, 1)

            dve.wait_ge(abs_tot, 1)
            for j, n in enumerate((D * D, D * KV, D * KV, D * D)):
                last = V.tensor_scalar(wmean[:, j:j + 1], psum[3][:, j:j + 1], 1.0 / n, 1e-5, ALU.mult, ALU.max)
            step(last)
            step(V.reciprocal(wrecip[:, :], wmean[:, :]))
            qkv_src = qkv_w.rearrange("p (c o) -> p c o", c=KC)
            o_src = o_w.rearrange("p (c o) -> p c o", c=KC)
            dve.wait_ge(abs_sum, 4)
            parts = ((qkv_src[:, :, 0:D], w_qkv[:, :, 0:D], 0), (qkv_src[:, :, D:D + KV], w_qkv[:, :, D:D + KV], 1),
                     (qkv_src[:, :, D + KV:D + 2 * KV], w_qkv[:, :, D + KV:D + 2 * KV], 2), (o_src, w_o[:, :, :], 3))
            for src, _, j in parts:
                last = V.tensor_scalar(src, src, wrecip[:, j:j + 1], MAGIC, ALU.mult, ALU.add)
            step(last)
            for src, _, j in parts:
                last = V.tensor_scalar(src, src, MAGIC + 1.0, MAGIC - 1.0, ALU.min, ALU.max)
            step(last)
            for src, dst, j in parts:
                last = V.tensor_scalar(dst, src, -MAGIC, None, ALU.add)
            last.then_inc(cast_ready, 1)
            for tab in (cos_t, sin_t):
                V.tensor_scalar(tab[:, 0:D], tab[:, 0:D], wmean[:, 0:1], None, ALU.mult)
                last = V.tensor_scalar(tab[:, D:QK], tab[:, D:QK], wmean[:, 1:2], None, ALU.mult)
            step(last)
            V.tensor_copy(ident_bf[:, :], ident).then_inc(ident_ok, 1)
            dve.wait_ge(ld["vec"], 64)
            step(V.tensor_copy(idf[:, :], ids[:, :]))
            step(V.tensor_tensor(lang[:, :, :], cols(idf[:, :], E), rows(expert_no, NT), ALU.is_equal))
            step(V.tensor_scalar(lang[:, :, :], lang[:, :, :], 5.0, None, ALU.mult))
            step(V.memset(col_s[:, :], 0.0))
            gu_cols = col_s[:, 0:2 * FC].rearrange("p (j c) -> p j c", j=2)

            def scales(c, src, col, rec):
                V.tensor_reduce(col, src, AX.X, ALU.max, apply_absolute_value=True).then_inc(row_step, 1)
                dve.wait_ge(row_step, 2 * c + 1)
                V.tensor_scalar(col, col, 1.0 / 127.0, 1e-8, ALU.mult, ALU.max).then_inc(row_step, 1)
                dve.wait_ge(row_step, 2 * c + 2)
                V.reciprocal(rec, col).then_inc(f_scale, 1)

            def scales_gu(i, b, n):
                c = BUFS * i + b
                dve.wait_ge(ld_f[b], 32 * i + 32)
                scales(c, gu_f[b][0:n, :].rearrange("p (j n) -> p j n", j=2), f_col[b][0:n, :], f_rec[b][0:n, :])
                V.tensor_copy(gu_cols[0:n, :, bass.ds(c, 1)].rearrange("p j c -> p (j c)"), f_col[b][0:n, :]).then_inc(col_ok, 1)

            for b in range(BUFS):
                scales_gu(0, b, P)
            with dve.Fori(1, FC // BUFS) as i:
                for b in range(BUFS):
                    scales_gu(i, b, P)
            scales_gu(FC // BUFS, 0, P)
            scales_gu(FC // BUFS, 1, FL)
            dg = scale_diag.rearrange("p (j n) -> p j n", n=P)
            dve.wait_ge(col_ok, FC)
            V.tensor_tensor(dg[:, 0:2 * FC, :], rows(ident, 2 * FC), cols(col_s[:, 0:2 * FC], P), ALU.mult).then_inc(rows_diag, 1)
            for c in range(KC):
                b = (FC + c) % BUFS
                dve.wait_ge(ld_d[c], 16)
                dve.wait_ge(f_round, FC + c - 2)
                scales(FC + c, d_f[c], col_s[:, 2 * FC + c:2 * FC + c + 1], f_rec[b][:, 0:1])
            dve.wait_ge(row_step, 2 * FC + 2 * KC)
            V.tensor_tensor(dg[:, 2 * FC:NCH, :], rows(ident, KC), cols(col_s[:, 2 * FC:NCH], P), ALU.mult).then_inc(rows_diag, 1)
            for r, (dst, lo, hi) in enumerate(row_parts):
                dve.wait_ge(row_mm, r + 1)
                V.tensor_copy(dst[:, lo:hi], psum[r % 8][:, 0:hi - lo]).then_inc(row_ev, 1)
            dve.wait_ge(row_ev, len(row_parts))

            def stage(s, k, it):
                B, w, sm = bank[s], work[s], steps[s]
                if k == "norm":
                    dve.wait_ge(y_mm.sem[s], y_mm.done(it))
                    V.bn_stats(st[s], B[0][:, :]).then_inc(y_step.sem[s], 1)
                    dve.wait_ge(y_step.sem[s], y_step.done(it, 1))
                    V.memset(sm[:, 15:16], 0.0)
                    V.bn_aggr(mv[s], st[s]).then_inc(y_step.sem[s], 1)
                    dve.wait_ge(y_step.sem[s], y_step.done(it, 2))
                    V.tensor_scalar(sm[:, 0:1], mv[s][:, 1:2], 1e-5, None, ALU.add).then_inc(y_step.sem[s], 1)
                    dve.wait_ge(out_st.sem[s], out_st.last(it))
                    V.scalar_tensor_tensor(w[:, :], B[0][:, :], mv[s][:, 0:1], ln_g[:, :], ALU.subtract, ALU.mult).then_inc(y_step.sem[s], 1)
                if k == "norm_round":
                    dve.wait_ge(y_rstd.sem[s], y_rstd.done(it))
                    dve.wait_ge(y_step.sem[s], y_step.done(it, 4))
                    V.scalar_tensor_tensor(w[:, :], w[:, :], rstd[s][:, 0:1], ln_b[:, :], ALU.mult, ALU.add).then_inc(y_step.sem[s], 1)
                    dve.wait_ge(y_step.sem[s], y_step.done(it, 5))
                    V.tensor_reduce(sm[:, 1:2], w[:, :], AX.X, ALU.max, apply_absolute_value=True).then_inc(y_step.sem[s], 1)
                    dve.wait_ge(y_step.sem[s], y_step.done(it, 6))
                    V.tensor_scalar(deq[s][:, 0:1], sm[:, 1:2], 1e-5, 1.0 / 127.0, ALU.max, ALU.mult).then_inc(y_step.sem[s], 1)
                    dve.wait_ge(y_step.sem[s], y_step.done(it, 7))
                    V.reciprocal(q_scale[s][:, 0:1], deq[s][:, 0:1]).then_inc(y_step.sem[s], y_step.full)
                if k == "qkv":
                    V.tensor_scalar(v_scale[s], deq[s][:, 0:1], wmean[:, 2:3], None, ALU.mult).then_inc(rope_step.sem[s], 1)
                    dve.wait_ge(qkv_mm.sem[s], qkv_mm.phase_done(it))
                    sc = deq[s][:, 0:1]
                    for o, n, src in ((0, D, B[0][:, :]), (D, KV, B[1][:, 0:KV])):
                        V.scalar_tensor_tensor(rope_c[s][:, o:o + n], src, sc, cos_t[:, o:o + n], ALU.mult, ALU.mult)
                        x3 = src.rearrange("p (h j) -> p h j", j=HD)
                        s3 = sin_t[:, o:o + n].rearrange("p (h j) -> p h j", j=HD)
                        o3 = rope_s[s][:, o:o + n].rearrange("p (h j) -> p h j", j=HD)
                        hh = HD // 2
                        V.scalar_tensor_tensor(o3[:, :, 0:hh], x3[:, :, hh:HD], sc, s3[:, :, 0:hh], ALU.mult, ALU.mult)
                        last = V.scalar_tensor_tensor(o3[:, :, hh:HD], x3[:, :, 0:hh], sc, s3[:, :, hh:HD], ALU.mult, ALU.mult)
                    last.then_inc(rope_step.sem[s], rope_step.full)
                def row_max(j):
                    dve.wait_ge(s_mm.sem[s], s_mm.done(it, j + 1))
                    sc = B[j].rearrange("p (h q) -> p h q", q=SEQ)
                    V.tensor_reduce(smax[s][:, 16 * j:16 * (j + 1)], sc, AX.X, ALU.max).then_inc(s_step.sem[s], 1)

                def less_max(j):
                    dve.wait_ge(s_step.sem[s], s_step.done(it, 2 * j + 1))
                    sc = B[j].rearrange("p (h q) -> p h q", q=SEQ)
                    p = prob[s][:, 512 * j:512 * (j + 1)].rearrange("p (h q) -> p h q", q=SEQ)
                    V.tensor_tensor(p, sc, cols(smax[s][:, 16 * j:16 * (j + 1)], SEQ), ALU.subtract).then_inc(s_step.sem[s], 1)

                if k == "scores":
                    row_max(0)
                if k == "softmax":
                    less_max(0)
                    row_max(1)
                    less_max(1)
                if k == "softmax_sum":
                    dve.wait_ge(s_exp.sem[s], s_exp.done(it))
                    V.tensor_reduce(rsum[s], prob[s].rearrange("p (h q) -> p h q", q=SEQ), AX.X, ALU.add).then_inc(s_sum.sem[s], 1)
                    dve.wait_ge(s_sum.sem[s], s_sum.done(it, 1))
                    V.reciprocal(rsum[s], rsum[s]).then_inc(s_sum.sem[s], s_sum.full)
                if k == "att":
                    dve.wait_ge(att_mm.sem[s], att_mm.phase_done(it))
                    dve.wait_ge(s_sum.sem[s], s_sum.phase_done(it))
                    w3 = w.rearrange("p (h j) -> p h j", j=HD)
                    V.tensor_tensor(w3, B[1].rearrange("p (h j) -> p h j", j=HD), cols(rsum[s], HD), ALU.mult).then_inc(a_step.sem[s], 1)
                    dve.wait_ge(a_step.sem[s], a_step.done(it, 1))
                    V.tensor_reduce(sm[:, 2:3], w[:, :], AX.X, ALU.max, apply_absolute_value=True).then_inc(a_step.sem[s], 1)
                    dve.wait_ge(a_step.sem[s], a_step.done(it, 2))
                    V.tensor_scalar(sm[:, 3:4], sm[:, 2:3], 1e-5, 1.0 / 127.0, ALU.max, ALU.mult).then_inc(a_step.sem[s], 1)
                    dve.wait_ge(a_step.sem[s], a_step.done(it, 3))
                    V.tensor_scalar(deq[s][:, 0:1], sm[:, 3:4], wmean[:, 3:4], None, ALU.mult).then_inc(a_step.sem[s], 1)
                    V.reciprocal(q_scale[s][:, 1:2], sm[:, 3:4]).then_inc(a_step.sem[s], a_step.full)
                if k == "router":
                    t = it * SLOTS + s
                    dve.wait_ge(hl_mm.sem[s], hl_mm.done(it))
                    V.tensor_tensor(logit[s], B[1][:, ER:ER + E], lang[:, bass.ds(t, 1), :].rearrange("p a e -> p (a e)"),
                                    ALU.add).then_inc(l_step.sem[s], 1)
                    dve.wait_ge(l_step.sem[s], l_step.done(it, 1))
                    V.memset(sm[:, 15:16], 0.0)
                    V.max(top8[s], logit[s]).then_inc(l_step.sem[s], 1)
                    dve.wait_ge(l_step.sem[s], l_step.done(it, 2))
                    V.tensor_scalar(sm[:, 4:5], top8[s][:, 0:1], -1.0, None, ALU.mult).then_inc(l_step.sem[s], 1)
                    V.max_index(topi[s][:, :], top8[s], logit[s]).then_inc(l_step.sem[s], 1)
                    dve.wait_ge(l_step.sem[s], l_step.done(it, 4))
                    V.tensor_scalar(keep[s], expert_no, topi[s][:, 0:1], None, ALU.is_equal).then_inc(l_step.sem[s], 1)
                if k == "gates":
                    dve.wait_ge(l_step.sem[s], l_step.done(it, 5))
                    V.scalar_tensor_tensor(keep[s], expert_no, topi[s][:, 1:2], keep[s], ALU.is_equal, ALU.add).then_inc(l_step.sem[s], 1)
                    dve.wait_ge(l_step.sem[s], l_step.done(it, 6))
                    dve.wait_ge(l_exp.sem[s], l_exp.done(it))
                    V.tensor_tensor(ew[s], ew[s], keep[s], ALU.mult).then_inc(l_step.sem[s], 1)
                    dve.wait_ge(l_step.sem[s], l_step.done(it, 7))
                    V.tensor_reduce(sm[:, 5:6], ew[s], AX.X, ALU.add).then_inc(l_step.sem[s], 1)
                    dve.wait_ge(l_step.sem[s], l_step.done(it, 8))
                    V.reciprocal(sm[:, 6:7], sm[:, 5:6]).then_inc(l_step.sem[s], 1)
                    dve.wait_ge(l_step.sem[s], l_step.done(it, 9))
                    V.tensor_scalar(ew[s], ew[s], sm[:, 6:7], 2.0, ALU.mult, ALU.mult).then_inc(l_step.sem[s], 1)
                    dve.wait_ge(l_step.sem[s], l_step.done(it))
                    V.tensor_tensor(hg[s].rearrange("p (e r) -> p e r", e=E), B[1][:, 0:ER].rearrange("p (e r) -> p e r", e=E),
                                    cols(ew[s], LR), ALU.mult).then_inc(hg_ok.sem[s], hg_ok.full)
                if k == "lora":
                    dve.wait_ge(z_sq.sem[s], z_sq.done(it))
                    V.tensor_scalar(sm[:, 8:9], sq[s][:, 0:1], 1.0 / D, 1e-6, ALU.mult, ALU.add).then_inc(z_step.sem[s], 1)
                    V.tensor_tensor(w[:, :], B[0][:, :], rms_g[:, :], ALU.mult).then_inc(z_step.sem[s], 1)
                if k == "rms":
                    dve.wait_ge(z_step.sem[s], z_step.done(it, 2))
                    V.tensor_reduce(sm[:, 9:10], w[:, :], AX.X, ALU.max, apply_absolute_value=True).then_inc(z_step.sem[s], 1)
                    dve.wait_ge(z_step.sem[s], z_step.done(it, 3))
                    dve.wait_ge(z_rstd.sem[s], z_rstd.phase_done(it))
                    V.tensor_scalar(sm[:, 10:11], sm[:, 9:10], rstd[s][:, 1:2], None, ALU.mult).then_inc(z_step.sem[s], 1)
                    dve.wait_ge(z_step.sem[s], z_step.done(it, 4))
                    V.tensor_scalar(sm[:, 11:12], sm[:, 10:11], 1.0 / 127.0, 1e-8, ALU.mult, ALU.max).then_inc(z_step.sem[s], 1)
                    dve.wait_ge(z_step.sem[s], z_step.done(it, 5))
                    V.tensor_scalar(deq[s][:, 1:2], sm[:, 11:12], 0.5, None, ALU.mult).then_inc(z_step.sem[s], 1)
                    V.reciprocal(sm[:, 12:13], sm[:, 11:12]).then_inc(z_step.sem[s], 1)
                    dve.wait_ge(z_step.sem[s], z_step.done(it, 7))
                    V.tensor_scalar(q_scale[s][:, 2:3], sm[:, 12:13], rstd[s][:, 1:2], None, ALU.mult).then_inc(z_step.sem[s], z_step.full)
                for n, (lo, hi) in enumerate(FCH):
                    if k == f"gate_up{n}":
                        dve.wait_ge(gu_mm.sem[s], gu_mm.done(it, 2 * n + 1))
                        V.tensor_tensor(hid_g[s][:, lo:hi], B[0][:, 0:hi - lo], gate_s[:, lo:hi], ALU.mult).then_inc(gu_sc.sem[s], 1)
                        dve.wait_ge(gu_mm.sem[s], gu_mm.done(it, 2 * n + 2) if n < 2 else gu_mm.phase_done(it))
                        V.tensor_tensor(hid_u[s][:, lo:hi], B[1][:, 0:hi - lo], up_s[:, lo:hi], ALU.mult).then_inc(gu_sc.sem[s], 1)
                    if k == f"hidden{n}":
                        dve.wait_ge(gu_tanh.sem[s], gu_tanh.done(it, n + 1))
                        V.scalar_tensor_tensor(hid_t[s][:, lo:hi], hid_t[s][:, lo:hi], 1.0, hid_g[s][:, lo:hi],
                                               ALU.add, ALU.mult).then_inc(gu_h.sem[s], gu_h.full if n == 2 else 1)
                    if k == f"hidden{n + 1}" or n == 2 and k == "h_round":
                        dve.wait_ge(hid_ok.sem[s], hid_ok.done(it, n + 1))
                        V.tensor_reduce(sm[:, 16 + n:17 + n], hid_u[s][:, lo:hi], AX.X, ALU.max, apply_absolute_value=True).then_inc(h_step.sem[s], 1)
                if k == "h_round":
                    dve.wait_ge(h_step.sem[s], h_step.done(it, 3))
                    V.tensor_reduce(sm[:, 13:14], sm[:, 16:19], AX.X, ALU.max).then_inc(h_step.sem[s], 1)
                    V.tensor_scalar(sm[:, 14:15], deq[s][:, 1:2], sm[:, 11:12], None, ALU.mult).then_inc(h_step.sem[s], 1)
                    dve.wait_ge(h_step.sem[s], h_step.done(it, 5))
                    V.tensor_scalar(sm[:, 13:14], sm[:, 13:14], sm[:, 14:15], 1.0 / 127.0, ALU.mult, ALU.mult).then_inc(h_step.sem[s], 1)
                    dve.wait_ge(h_step.sem[s], h_step.done(it, 6))
                    V.tensor_scalar(sq[s][:, 1:2], sm[:, 13:14], 1e-8, None, ALU.max).then_inc(h_step.sem[s], 1)
                    dve.wait_ge(h_step.sem[s], h_step.done(it, 7))
                    V.reciprocal(sq[s][:, 2:3], sq[s][:, 1:2]).then_inc(h_step.sem[s], 1)
                    dve.wait_ge(h_step.sem[s], h_step.done(it, 8))
                    V.tensor_scalar(q_scale[s][:, 3:4], sq[s][:, 2:3], sm[:, 14:15], None, ALU.mult).then_inc(h_step.sem[s], 1)
                if k == "down":
                    dve.wait_ge(d_mm.sem[s], d_mm.phase_done(it))
                    V.scalar_tensor_tensor(w[:, :], B[1][:, :], sq[s][:, 1:2], down_s[:, :], ALU.mult, ALU.mult).then_inc(h_step.sem[s], h_step.full)

            rounds(dve, stage)

        @block.tensor
        def _(pe):
            MM, TR = nc.tensor.matmul, nc.tensor.transpose
            pe.wait_ge(ld["lora"], 32)
            for c in range(KC):
                last = MM(psum[c][:, :], loraA[:, c * P:(c + 1) * P], loraB, start=True, stop=True)
            last.then_inc(delta_mm, 1)
            for n in range(2):
                pe.wait_ge(diag_ok, n + 1)
                if n:
                    pe.wait_ge(near_col, 1)
                    TR(psum[0][0:1, 0:P], cell[:, 1:2], ident).then_inc(near_row, 1)
                for g in range(KC):
                    last = MM(psum[4 + g][:, :], ones, diag[:, g * D:(g + 1) * D], start=True, stop=True)
                last.then_inc(bc_mm, 1)
            pe.wait_ge(abs_sum, 4)
            MM(psum[3][:, 0:4], ones, wabs[:, :], start=True, stop=True).then_inc(abs_tot, 1)
            pe.wait_ge(ident_ok, 1)

            def turn_gu(c, b, n):
                pe.wait_ge(f_bf, c + 1)
                if not isinstance(c, int) or c >= BUFS:
                    pe.wait_ge(f_ev, c - 2)
                for j in range(2):
                    dst = psum[2 * b + j][:, 0:256].bitcast(bf16)
                    for i in range(KC):
                        last = TR(dst[:, i * P:i * P + n], gu_b[b][0:n, j * D + i * P:j * D + (i + 1) * P], ident_bf[0:n, 0:n])
                last.then_inc(f_T, 1)

            for b in range(BUFS):
                turn_gu(b, b, P)
            with pe.Fori(1, FC // BUFS) as i:
                for b in range(BUFS):
                    turn_gu(BUFS * i + b, b, P)
            turn_gu(FC - 2, 0, P)
            turn_gu(FC - 1, 1, FL)
            for c in range(KC):
                pe.wait_ge(f_bf, FC + c + 1)
                pe.wait_ge(f_ev, FC + max(c - 1, 0))
                for f in range(FC):
                    n = P if f < FC - 1 else FL
                    dst = psum[4 * (c % 2) + f // 4][:, 0:256].bitcast(bf16)
                    last = TR(dst[0:n, (f % 4) * P:(f % 4 + 1) * P], d_b[c % 2][:, f * P:f * P + n], ident_bf[:, :])
                last.then_inc(f_T, 1)
            pe.wait_ge(f_ev, FC + KC)
            first = {id(gate_s): 0, id(up_s): FC, id(down_s): 2 * FC}
            for r, (dst, lo, hi) in enumerate(row_parts):
                pe.wait_ge(rows_diag, 2 if dst is down_s else 1)
                o = first[id(dst)] * P + lo
                MM(psum[r % 8][:, 0:hi - lo], ones, scale_diag[:, o:o + hi - lo], start=True, stop=True).then_inc(row_mm, 1)
            pe.wait_ge(row_ev, len(row_parts))
            pe.wait_ge(w_eff_ready, 1)
            pe.wait_ge(cast_ready, 1)
            pe.wait_ge(ld["c2"], 64)

            def turn(dst, src, idn):
                for i in range(KC):
                    last = TR(dst[:, i * P:(i + 1) * P], src[:, i * P:(i + 1) * P], idn)
                return last

            def stage(s, k, it):
                B, w = bank[s], work[s]
                if k == "cond":
                    pe.wait_ge(xT_in.sem[s], xT_in.phase_done(it))
                    pe.wait_ge(hT.sem[s], hT.last(it))
                    for c in range(KC):
                        last = MM(B[0][:, :], xT[s][:, c, :], w_eff[:, c, :], start=c == 0, stop=c == KC - 1)
                    last.then_inc(y_mm.sem[s], 1)
                if k == "y_T":
                    pe.wait_ge(yq.sem[s], yq.done(it))
                    pe.wait_ge(h_step.sem[s], h_step.last(it))
                    turn(B[1], w, ident).then_inc(yqT_mm.sem[s], 1)
                if k == "qkv":
                    pe.wait_ge(yqT.sem[s], yqT.done(it))
                    for c in range(KC):
                        MM(B[0][:, :], work_bf[s][:, c, :], w_qkv[:, c, 0:D], start=c == 0, stop=c == KC - 1)
                    for c in range(KC):
                        last = MM(B[1][:, 0:2 * KV], work_bf[s][:, c, :], w_qkv[:, c, D:], start=c == 0, stop=c == KC - 1)
                    last.then_inc(qkv_mm.sem[s], qkv_mm.full)
                if k == "qk_T":
                    pe.wait_ge(qk.sem[s], qk.done(it))
                    pe.wait_ge(v_ev.sem[s], v_ev.phase_done(it))
                    TR(B[1][:, 0:P], rope_c[s][:, D:QK], ident).then_inc(qkT_mm.sem[s], 1)
                    turn(B[0], rope_c[s], ident).then_inc(qkT_mm.sem[s], 1)
                if k == "scores":
                    pe.wait_ge(qT.sem[s], qT.done(it))
                    pe.wait_ge(kbd.sem[s], kbd.done(it))
                    for r in range(R):
                        dst = B[r // 2][:, (r % 2) * 256:(r % 2 + 1) * 256]
                        for b in range(NB):
                            q0 = r * P + b * SEQ
                            last = MM(dst[b * SEQ:(b + 1) * SEQ, :], q_T[s][:, q0:q0 + SEQ],
                                      k_bd[s][:, b * 256:(b + 1) * 256], start=True, stop=True, tile_position=(0, b * SEQ))
                        if r % 2:
                            last.then_inc(s_mm.sem[s], 1)
                if k == "softmax":
                    pe.wait_ge(s_step.sem[s], s_step.done(it, 2))
                    for b in range(NB):
                        last = MM(B[0][:, b * P:(b + 1) * P], rep[:, b * P:(b + 1) * P], v_row[s], start=True, stop=True)
                    last.then_inc(v_mm.sem[s], 1)
                if k == "p_T":
                    pe.wait_ge(v4_ev.sem[s], v4_ev.done(it))
                    for j in range(2):
                        pe.wait_ge(s_exp.sem[s], s_exp.done(it, j + 1))
                        turn(B[j], prob[s][:, 512 * j:512 * (j + 1)], ident).then_inc(pT_mm.sem[s], 1)
                if k == "pv":
                    pe.wait_ge(pT.sem[s], pT.done(it))
                    pe.wait_ge(vbd.sem[s], vbd.done(it))
                    pt = prob_T[s].rearrange("p (r e b q) -> p r e b q", r=R, e=2, b=NB)
                    for b in range(NB):
                        for e in range(2):
                            last = MM(B[0][64 * e:64 * (e + 1), b * P:(b + 1) * P],
                                      v_bd[s][:, (b * 2 + e) * 64:(b * 2 + e + 1) * 64], pt[:, :, e, b, :],
                                      start=True, stop=True, tile_position=(0, 64 * e))
                    last.then_inc(pv_mm.sem[s], 1)
                if k == "att":
                    pe.wait_ge(attT.sem[s], attT.phase_done(it))
                    turn(B[1], att_T[s], ident).then_inc(att_mm.sem[s], att_mm.full)
                if k == "att_T":
                    pe.wait_ge(aq.sem[s], aq.done(it))
                    turn(B[0], w, ident).then_inc(aqT_mm.sem[s], 1)
                if k == "o":
                    pe.wait_ge(aqT.sem[s], aqT.done(it))
                    for c in range(KC):
                        last = MM(B[1][:, :], work_bf[s][:, c, :], w_o[:, c, :], start=c == 0, stop=c == KC - 1)
                    last.then_inc(o_mm.sem[s], 1)
                if k == "x1_T":
                    pe.wait_ge(x1_ok.sem[s], x1_ok.phase_done(it))
                    turn(B[0], x1[s], ident).then_inc(x1T_mm.sem[s], x1T_mm.full)
                if k == "router":
                    pe.wait_ge(x1T_ok.sem[s], x1T_ok.phase_done(it))
                    for c in range(KC):
                        last = MM(B[1][:, 0:ER + E], x1T[s][:, c, :], w_c2[:, c, D:W2N], start=c == 0, stop=c == KC - 1)
                    last.then_inc(hl_mm.sem[s], 1)
                    for c in range(KC):
                        MM(B[0][:, :], x1T[s][:, c, :], w_c2[:, c, 0:D], start=c == 0, stop=False)
                if k == "hg_T":
                    pe.wait_ge(hg_ok.sem[s], hg_ok.phase_done(it))
                    TR(B[1][:, 2 * P:3 * P], hg[s], ident).then_inc(hgT_mm.sem[s], 1)
                if k == "lora":
                    pe.wait_ge(hgT.sem[s], hgT.done(it))
                    MM(B[0][:, :], hg_T[s], b_c2[:, :], start=False, stop=True).then_inc(c2_mm.sem[s], 1)
                if k == "z_T":
                    pe.wait_ge(zq.sem[s], zq.done(it))
                    turn(B[1], w, ident).then_inc(zT_mm.sem[s], zT_mm.full)
                for n, (lo, hi) in enumerate(FCH):
                    if k == f"gate_up{n}":
                        pe.wait_ge(zT.sem[s], zT.phase_done(it))
                        for j, wt in enumerate((w_gate, w_up)):
                            if n:
                                pe.wait_ge(gu_sc.sem[s], gu_sc.done(it, 2 * n - 1 + j))
                            for c in range(KC):
                                last = MM(B[j][:, 0:hi - lo], work_bf[s][:, c, :], wt[:, c, lo:hi],
                                          start=c == 0, stop=c == KC - 1)
                            last.then_inc(gu_mm.sem[s], gu_mm.full if n == 2 and j else 1)
                if k == "h_T":
                    pe.wait_ge(hq.sem[s], hq.done(it))
                    for f in range(FC):
                        n = P if f < FC - 1 else FL
                        if f == 8:
                            pe.wait_ge(hT.sem[s], hT.done(it, 1))
                        last = TR(B[f // 4 % 2][0:n, (f % 4) * P:(f % 4 + 1) * P], hid_g[s][:, f * P:f * P + n], ident)
                        if f % 4 == 3 or f == FC - 1:
                            last.then_inc(hT_mm.sem[s], 1)
                if k == "down":
                    for f in range(FC):
                        n = P if f < FC - 1 else FL
                        if f % 8 == 0:
                            pe.wait_ge(hT.sem[s], hT.phase_done(it) if f else hT.done(it, 2))
                        last = MM(B[1][:, :], hid_bf[s][0:n, f, :], w_down[0:n, f, :], start=f == 0, stop=f == FC - 1)
                    last.then_inc(d_mm.sem[s], d_mm.full)

            rounds(pe, stage)


_OUT = "out"


def _constants():
    import numpy as np
    P, SEQ, HD, G, R, NB, E = 128, 32, 16, 8, 4, 4, 8
    p = np.arange(P)
    ident = np.eye(P, dtype=np.float32)
    inv = (1.0 / np.float32(10000.0) ** (np.arange(0, HD, 2, dtype=np.float32) / HD)).astype(np.float32)
    ang = (np.arange(SEQ, dtype=np.float32)[:, None] * inv[None, :]).astype(np.float32).astype(np.float64)
    cos, sin = np.cos(ang), np.sin(ang)
    heads = G * R + G
    cos_t = np.tile(np.tile(np.concatenate([cos, cos], 1), (NB, 1)), (1, heads)).astype(np.float32)
    sin_t = np.tile(np.tile(np.concatenate([-sin, sin], 1), (NB, 1)), (1, heads)).astype(np.float32)
    mask_k = (p[:, None] // HD == np.arange(G)[None, :]).astype(np.float32)
    mask_v = (p[:, None] // SEQ == np.arange(G // 2)[None, :]).astype(np.float32)
    rep = np.concatenate([(p[:, None] == b * SEQ + p[None, :] % SEQ).astype(np.float32) for b in range(NB)], 1)
    expert = np.tile(np.arange(E, dtype=np.float32), (P, 1))
    ones = np.ones((P, P), np.float32)
    return np.ascontiguousarray(np.concatenate([ident, cos_t, sin_t, mask_k, mask_v, rep, expert, ones], 1))


def kernel(**inputs):
    import numpy as np
    import concourse.bacc as bacc
    from concourse import mybir
    from concourse.bass_utils import run_bass_kernel_spmd

    a = {k: np.asarray(v) for k, v in inputs.items()}
    P, D, G, R, HD = 128, 512, 8, 4, 16
    KC, NT = D // P, a["x"].shape[0] * a["x"].shape[1] // P
    F = a["L0_ffn_Wg"].shape[0]
    FC = -(-F // P)

    def by_chunk(w):
        return w.T.reshape(w.shape[1] // P, P, w.shape[0]).transpose(1, 0, 2)

    def padded_rows(w):
        return np.concatenate([w, w[:FC * P - F]]).reshape(FC, P, D)

    wq = a["L0_attn_Wq"].reshape(G, R, HD, D).transpose(1, 0, 2, 3).reshape(D, D)
    wo = a["L0_attn_Wo"].reshape(D, G, R, HD).transpose(0, 2, 1, 3).reshape(D, D)
    c2a, c2b = a["L0_cond2_A"], a["L0_cond2_B"]
    arrays = {
        "x_tok": a["x"].reshape(NT, P, D),
        "x_T": a["x"].reshape(NT, P, KC, P).transpose(0, 3, 2, 1),
        "ids": np.repeat(a["itok_B_0_7"], a["x"].shape[1]).reshape(NT, P).T,
        "codebook": a["condB_codebook"].reshape(1, -1),
        "w_cond": by_chunk(a["L0_cond_weight"]),
        "scale_log": a["L0_cond_scale_log"].reshape(D // P, P, KC).transpose(1, 2, 0).reshape(P, -1),
        "lora_A": a["L0_cond_lora_A"],
        "lora_B": a["L0_cond_lora_B"].T,
        "ln_g": a["L0_attn_ln_w"].reshape(1, D), "ln_b": a["L0_attn_ln_b"].reshape(1, D),
        "w_qkv": by_chunk(np.concatenate([wq, a["L0_attn_Wk"], a["L0_attn_Wv"]], 0)),
        "w_o": by_chunk(wo),
        "c2_w": by_chunk(a["L0_cond2_W"]),
        "c2_a": by_chunk(c2a.reshape(-1, D)),
        "c2_wr": by_chunk(a["L0_cond2_Wr"]),
        "c2_b": c2b.transpose(0, 2, 1).reshape(-1, D),
        "rms_g": a["L0_ffn_rmsnorm_weight"].reshape(1, D),
        "ffn_wg": padded_rows(a["L0_ffn_Wg"]), "ffn_wu": padded_rows(a["L0_ffn_Wu"]),
        "ffn_wd": a["L0_ffn_Wd"].reshape(KC, P, F),
        "consts": _constants(),
    }
    arrays = {k: np.ascontiguousarray(v) for k, v in arrays.items()}
    nc = bacc.Bacc("TRN2", target_bir_lowering=False, num_devices=1)
    d = {k: nc.dram_tensor("in_" + k, v.shape, mybir.dt.from_np(v.dtype), kind="ExternalInput").ap() for k, v in arrays.items()}
    d["out"] = nc.dram_tensor("out", (NT, P, D), mybir.dt.float32, kind="ExternalOutput").ap()
    adaln_attn_ffn_kernel(nc, d)
    r = run_bass_kernel_spmd(nc, [{"in_" + k: v for k, v in arrays.items()}], core_ids=[0])
    return r.results[0]["out"].reshape(a["x"].shape)
```
